# Optimizing a Trainium2 kernel written in Bass

```python
import numpy as np
import jax
import jax.numpy as jnp

def _softmax(x, axis=-1):
    return jax.nn.softmax(x, axis=axis)

def _gelu(x):
    return jax.nn.gelu(x, approximate=True)

def _silu(x):
    return jax.nn.silu(x)

def _sigmoid(x):
    return jax.nn.sigmoid(x)

def _layernorm(x, axis=-1, eps=1e-05):
    m = jnp.mean(x, axis=axis, keepdims=True)
    v = jnp.var(x, axis=axis, keepdims=True)
    return (x - m) / jnp.sqrt(v + eps)

def _scatter_add(tgt, idx, src, axis=0):
    return tgt.at[idx].add(src)

def _segment_sum(src, seg, n):
    return jax.ops.segment_sum(src, seg, n)
kernel_name = 'mk_lm_tower_d2_tok_ids768_r4_9f496f'

def setup_inputs(seed: int=0):
    np.random.seed(seed)
    _w = jnp.asarray

    def _rec_inputs():
        import jax
        import jax.numpy as jnp
        _rk = jax.random.key(seed)
        x = jax.random.randint(jax.random.fold_in(_rk, 1), (4, 512), 0, 12564, jnp.int32)
        return x
    x = _rec_inputs()

    def _L0_tok_setup():
        import jax, jax.numpy as jnp
        import numpy as np
        VOCAB = 50257
        FRONT = 768
        EMBED = 192
        key = jax.random.key(seed)
        k1, k2, k3, k4, k5, k6 = jax.random.split(key, 6)
        idxs = jax.random.randint(k1, (4, 1024), 0, VOCAB, dtype=jnp.int64 if jax.config.jax_enable_x64 else jnp.int32)
        tok_embed = jax.random.normal(k2, (VOCAB, FRONT), dtype=jnp.float32)
        lim1 = 1.0 / np.sqrt(FRONT)
        W1 = jax.random.uniform(k3, (EMBED, FRONT), minval=-lim1, maxval=lim1, dtype=jnp.float32)
        b1 = jax.random.uniform(k4, (EMBED,), minval=-lim1, maxval=lim1, dtype=jnp.float32)
        lim2 = 1.0 / np.sqrt(EMBED)
        W2 = jax.random.uniform(k5, (EMBED, EMBED), minval=-lim2, maxval=lim2, dtype=jnp.float32)
        b2 = jax.random.uniform(k6, (EMBED,), minval=-lim2, maxval=lim2, dtype=jnp.float32)
        return {'idxs': idxs, 'tok_embed': tok_embed, 'W1': W1, 'b1': b1, 'W2': W2, 'b2': b2}
    _L0_tok_all = _L0_tok_setup()
    _L0_tok_in = {k: v for k, v in _L0_tok_all.items() if k in ('tok_embed', 'W1', 'b1', 'W2', 'b2')}
    del _L0_tok_all

    def _L0_attn_setup():
        import jax, jax.numpy as jnp
        import numpy as np
        B, N, E, H = (2, 64, 192, 12)
        D = E // H
        LOG_2PI = float(np.log(2.0 * np.pi))
        key = jax.random.key(seed)
        ks = jax.random.split(key, 8)
        return {'x': jax.random.normal(ks[0], (B, N, E), jnp.float32), 'Wqkv': jax.random.normal(ks[1], (E, 3 * E), jnp.float32) * 0.02, 'bqkv': jax.random.normal(ks[2], (3 * E,), jnp.float32) * 0.02, 'Wproj': jax.random.normal(ks[3], (E, E), jnp.float32) * 0.02, 'bproj': jax.random.normal(ks[4], (E,), jnp.float32) * 0.02, 'mean': jax.random.normal(ks[5], (E, E), jnp.float32), 'logvar': jax.random.normal(ks[6], (E, E), jnp.float32), 'mix_coef': jax.random.normal(ks[7], (E,), jnp.float32)}
    _L0_attn_all = _L0_attn_setup()
    _L0_attn_in = {k: v for k, v in _L0_attn_all.items() if k in ('Wqkv', 'bqkv', 'Wproj', 'bproj', 'mean', 'logvar', 'mix_coef')}
    del _L0_attn_all

    def _L0_ffn_setup():
        import math
        import jax, jax.numpy as jnp
        import numpy as np
        N_HEAD = 12
        N_EXP = 8
        TOP_K = 2
        TRAIN_CAPACITY = 1.25
        MIN_CAPACITY = 4
        LN_EPS = 1e-05
        NEG_INF = -1e+30

        def _layer_norm(x, w, b):
            mu = jnp.mean(x, axis=-1, keepdims=True)
            var = jnp.var(x, axis=-1, keepdims=True)
            return (x - mu) * jax.lax.rsqrt(var + LN_EPS) * w + b

        def _attention(x, qkv_w, qkv_b, proj_w, proj_b):
            B, T, C = x.shape
            H, D = (N_HEAD, C // N_HEAD)
            qkv = x @ qkv_w + qkv_b
            q, k, v = jnp.split(qkv, 3, axis=-1)
            q = q.reshape(B, T, H, D).transpose(0, 2, 1, 3)
            k = k.reshape(B, T, H, D).transpose(0, 2, 1, 3)
            v = v.reshape(B, T, H, D).transpose(0, 2, 1, 3)
            scores = jnp.einsum('bhqd,bhkd->bhqk', q, k) / math.sqrt(D)
            causal = jnp.tril(jnp.ones((T, T), bool))
            scores = jnp.where(causal, scores, NEG_INF)
            attn = jax.nn.softmax(scores, axis=-1)
            y = jnp.einsum('bhqk,bhkd->bhqd', attn, v)
            y = y.transpose(0, 2, 1, 3).reshape(B, T, C)
            return y @ proj_w + proj_b

        def _moe(x, w_g, fc_w, fc_b, pj_w, pj_b):
            B, T, C = x.shape
            N, E, K = (B * T, N_EXP, TOP_K)
            cap = int(math.floor(K * TRAIN_CAPACITY * N / E))
            cap += cap % 2
            cap = max(cap, MIN_CAPACITY)
            logits = (x @ w_g).reshape(N, E)
            _, topk_idx = jax.lax.top_k(logits, K)
            hot = jax.nn.one_hot(topk_idx, E, dtype=jnp.int32)
            sel = hot.sum(axis=1) > 0
            router_probs = jax.nn.softmax(jnp.where(sel, logits, NEG_INF), axis=-1)
            exp_mask = hot.transpose(1, 0, 2)
            exp_rank = jnp.cumsum(exp_mask.reshape(K * N, E), axis=0) - 1
            exp_rank = exp_rank.reshape(K, N, E)
            exp_mask = exp_mask * (exp_rank < cap).astype(jnp.int32)
            exp_rank = jnp.sum(exp_mask * exp_rank, axis=-1)
            exp_weights = exp_mask.astype(x.dtype) * router_probs[None]
            rank_sc = jax.nn.one_hot(exp_rank, cap, dtype=x.dtype)
            cb_weight = jnp.einsum('kne,knc->nec', exp_weights, rank_sc)
            sec_mask = (cb_weight != 0).astype(x.dtype)
            xf = x.reshape(N, C)
            xb = jnp.einsum('nec,nd->ecd', sec_mask, xf)
            h = jax.nn.gelu(jnp.einsum('ecd,edf->ecf', xb, fc_w) + fc_b, approximate=False)
            out = jnp.einsum('ecf,efd->ecd', h, pj_w) + pj_b
            y = jnp.einsum('nec,ecd->nd', cb_weight, out)
            return y.reshape(B, T, C)
        key = jax.random.key(seed)
        ks = jax.random.split(key, 12)
        B, T, C = (4, 256, 192)
        E, F = (N_EXP, 4 * C)
        s = 0.02
        return {'x': jax.random.normal(ks[0], (B, T, C), jnp.float32), 'ln1_w': jnp.ones((C,), jnp.float32), 'ln1_b': jnp.zeros((C,), jnp.float32), 'ln2_w': jnp.ones((C,), jnp.float32), 'ln2_b': jnp.zeros((C,), jnp.float32), 'attn_qkv_w': jax.random.normal(ks[1], (C, 3 * C), jnp.float32) * s, 'attn_qkv_b': jnp.zeros((3 * C,), jnp.float32), 'attn_proj_w': jax.random.normal(ks[2], (C, C), jnp.float32) * s, 'attn_proj_b': jnp.zeros((C,), jnp.float32), 'w_g': jax.random.normal(ks[3], (C, E), jnp.float32) * s, 'exp_fc_w': jax.random.normal(ks[4], (E, C, F), jnp.float32) * s, 'exp_fc_b': jnp.zeros((E, 1, F), jnp.float32), 'exp_proj_w': jax.random.normal(ks[5], (E, F, C), jnp.float32) * s, 'exp_proj_b': jnp.zeros((E, 1, C), jnp.float32)}
    _L0_ffn_all = _L0_ffn_setup()
    _L0_ffn_in = {k: v for k, v in _L0_ffn_all.items() if k in ('ln1_w', 'ln1_b', 'ln2_w', 'ln2_b', 'attn_qkv_w', 'attn_qkv_b', 'attn_proj_w', 'attn_proj_b', 'w_g', 'exp_fc_w', 'exp_fc_b', 'exp_proj_w', 'exp_proj_b')}
    del _L0_ffn_all

    def _L1_attn_setup():
        import jax, jax.numpy as jnp
        import numpy as np
        import math
        B, S, H = (2, 512, 192)
        NH = 12
        HD = H // NH // 2
        LAMBDA_INIT = 0.8 - 0.6 * math.exp(-0.3 * 0)
        EPS = 1e-05
        key = jax.random.key(seed)
        ks = jax.random.split(key, 16)
        std = 0.02
        return {'hidden_states': jax.random.normal(ks[0], (B, S, H), dtype=jnp.float32), 'Wq': jax.random.normal(ks[1], (H, H), dtype=jnp.float32) * std, 'bq': jnp.zeros((H,), dtype=jnp.float32), 'Wk': jax.random.normal(ks[2], (H, H), dtype=jnp.float32) * std, 'bk': jnp.zeros((H,), dtype=jnp.float32), 'Wv': jax.random.normal(ks[3], (H, H), dtype=jnp.float32) * std, 'bv': jnp.zeros((H,), dtype=jnp.float32), 'Wo': jax.random.normal(ks[4], (H, H), dtype=jnp.float32) * std, 'bo': jnp.zeros((H,), dtype=jnp.float32), 'lambda_q1': jax.random.normal(ks[5], (HD,), dtype=jnp.float32) * 0.1, 'lambda_k1': jax.random.normal(ks[6], (HD,), dtype=jnp.float32) * 0.1, 'lambda_q2': jax.random.normal(ks[7], (HD,), dtype=jnp.float32) * 0.1, 'lambda_k2': jax.random.normal(ks[8], (HD,), dtype=jnp.float32) * 0.1, 'subln_w': jnp.ones((2 * HD,), dtype=jnp.float32)}
    _L1_attn_all = _L1_attn_setup()
    _L1_attn_in = {k: v for k, v in _L1_attn_all.items() if k in ('Wq', 'bq', 'Wk', 'bk', 'Wv', 'bv', 'Wo', 'bo', 'lambda_q1', 'lambda_k1', 'lambda_q2', 'lambda_k2', 'subln_w')}
    del _L1_attn_all

    def _L1_ffn_setup():
        import jax, jax.numpy as jnp
        import numpy as np
        E = 16
        K = 4
        H = 192
        I = 384
        LIMIT = 7.0
        ALPHA = 1.702
        EPS = 1e-05

        def rmsnorm(x, scale):
            xf = x.astype(jnp.float32)
            inv = jax.lax.rsqrt(jnp.mean(xf * xf, axis=-1, keepdims=True) + EPS)
            return (xf * inv).astype(x.dtype) * scale

        def swiglu(x, limit=LIMIT, alpha=ALPHA):
            x_glu = x[..., ::2]
            x_lin = x[..., 1::2]
            x_glu = jnp.minimum(x_glu, limit)
            x_lin = jnp.clip(x_lin, -limit, limit)
            return x_glu * jax.nn.sigmoid(alpha * x_glu) * (x_lin + 1.0)
        key = jax.random.key(seed)
        ks = jax.random.split(key, 7)
        s = 0.02
        return {'x': jax.random.normal(ks[0], (2, 256, H), dtype=jnp.float32), 'norm_scale': jnp.ones((H,), dtype=jnp.float32), 'gate_w': jax.random.normal(ks[1], (E, H), dtype=jnp.float32) * s, 'gate_b': jnp.zeros((E,), dtype=jnp.float32), 'mlp1_w': jax.random.normal(ks[2], (E, 2 * I, H), dtype=jnp.float32) * s, 'mlp1_b': jax.random.normal(ks[3], (E, 2 * I), dtype=jnp.float32) * s, 'mlp2_w': jax.random.normal(ks[4], (E, H, I), dtype=jnp.float32) * s, 'mlp2_b': jax.random.normal(ks[5], (E, H), dtype=jnp.float32) * s}
    _L1_ffn_all = _L1_ffn_setup()
    _L1_ffn_in = {k: v for k, v in _L1_ffn_all.items() if k in ('norm_scale', 'gate_w', 'gate_b', 'mlp1_w', 'mlp1_b', 'mlp2_w', 'mlp2_b')}
    del _L1_ffn_all
    return {'x': x, 'L0_tok_tok_embed': _L0_tok_in['tok_embed'], 'L0_tok_W1': _L0_tok_in['W1'], 'L0_tok_b1': _L0_tok_in['b1'], 'L0_tok_W2': _L0_tok_in['W2'], 'L0_tok_b2': _L0_tok_in['b2'], 'L0_attn_Wqkv': _L0_attn_in['Wqkv'], 'L0_attn_bqkv': _L0_attn_in['bqkv'], 'L0_attn_Wproj': _L0_attn_in['Wproj'], 'L0_attn_bproj': _L0_attn_in['bproj'], 'L0_attn_mean': _L0_attn_in['mean'], 'L0_attn_logvar': _L0_attn_in['logvar'], 'L0_attn_mix_coef': _L0_attn_in['mix_coef'], 'L0_ffn_ln1_w': _L0_ffn_in['ln1_w'], 'L0_ffn_ln1_b': _L0_ffn_in['ln1_b'], 'L0_ffn_ln2_w': _L0_ffn_in['ln2_w'], 'L0_ffn_ln2_b': _L0_ffn_in['ln2_b'], 'L0_ffn_attn_qkv_w': _L0_ffn_in['attn_qkv_w'], 'L0_ffn_attn_qkv_b': _L0_ffn_in['attn_qkv_b'], 'L0_ffn_attn_proj_w': _L0_ffn_in['attn_proj_w'], 'L0_ffn_attn_proj_b': _L0_ffn_in['attn_proj_b'], 'L0_ffn_w_g': _L0_ffn_in['w_g'], 'L0_ffn_exp_fc_w': _L0_ffn_in['exp_fc_w'], 'L0_ffn_exp_fc_b': _L0_ffn_in['exp_fc_b'], 'L0_ffn_exp_proj_w': _L0_ffn_in['exp_proj_w'], 'L0_ffn_exp_proj_b': _L0_ffn_in['exp_proj_b'], 'L1_attn_Wq': _L1_attn_in['Wq'], 'L1_attn_bq': _L1_attn_in['bq'], 'L1_attn_Wk': _L1_attn_in['Wk'], 'L1_attn_bk': _L1_attn_in['bk'], 'L1_attn_Wv': _L1_attn_in['Wv'], 'L1_attn_bv': _L1_attn_in['bv'], 'L1_attn_Wo': _L1_attn_in['Wo'], 'L1_attn_bo': _L1_attn_in['bo'], 'L1_attn_lambda_q1': _L1_attn_in['lambda_q1'], 'L1_attn_lambda_k1': _L1_attn_in['lambda_k1'], 'L1_attn_lambda_q2': _L1_attn_in['lambda_q2'], 'L1_attn_lambda_k2': _L1_attn_in['lambda_k2'], 'L1_attn_subln_w': _L1_attn_in['subln_w'], 'L1_ffn_norm_scale': _L1_ffn_in['norm_scale'], 'L1_ffn_gate_w': _L1_ffn_in['gate_w'], 'L1_ffn_gate_b': _L1_ffn_in['gate_b'], 'L1_ffn_mlp1_w': _L1_ffn_in['mlp1_w'], 'L1_ffn_mlp1_b': _L1_ffn_in['mlp1_b'], 'L1_ffn_mlp2_w': _L1_ffn_in['mlp2_w'], 'L1_ffn_mlp2_b': _L1_ffn_in['mlp2_b']}

def reference(x, L0_tok_tok_embed, L0_tok_W1, L0_tok_b1, L0_tok_W2, L0_tok_b2, L0_attn_Wqkv, L0_attn_bqkv, L0_attn_Wproj, L0_attn_bproj, L0_attn_mean, L0_attn_logvar, L0_attn_mix_coef, L0_ffn_ln1_w, L0_ffn_ln1_b, L0_ffn_ln2_w, L0_ffn_ln2_b, L0_ffn_attn_qkv_w, L0_ffn_attn_qkv_b, L0_ffn_attn_proj_w, L0_ffn_attn_proj_b, L0_ffn_w_g, L0_ffn_exp_fc_w, L0_ffn_exp_fc_b, L0_ffn_exp_proj_w, L0_ffn_exp_proj_b, L1_attn_Wq, L1_attn_bq, L1_attn_Wk, L1_attn_bk, L1_attn_Wv, L1_attn_bv, L1_attn_Wo, L1_attn_bo, L1_attn_lambda_q1, L1_attn_lambda_k1, L1_attn_lambda_q2, L1_attn_lambda_k2, L1_attn_subln_w, L1_ffn_norm_scale, L1_ffn_gate_w, L1_ffn_gate_b, L1_ffn_mlp1_w, L1_ffn_mlp1_b, L1_ffn_mlp2_w, L1_ffn_mlp2_b):
    import jax
    import jax.numpy as jnp

    def _L0_tok_ref(idxs, tok_embed, W1, b1, W2, b2):
        import jax, jax.numpy as jnp
        import numpy as np
        VOCAB = 50257
        FRONT = 768
        EMBED = 192
        x = tok_embed[idxs]
        x = jnp.einsum('bsf,ef->bse', x, W1) + b1
        x = jax.nn.gelu(x, approximate=False)
        x = jnp.einsum('bse,oe->bso', x, W2) + b2
        return x

    def _L0_attn_ref(x, Wqkv, bqkv, Wproj, bproj, mean, logvar, mix_coef):
        import jax, jax.numpy as jnp
        import numpy as np
        B, N, E, H = (2, 64, 192, 12)
        D = E // H
        LOG_2PI = float(np.log(2.0 * np.pi))
        b, n, e = x.shape
        qkv = (x @ Wqkv + bqkv).reshape(b, n, H, D, 3)
        qkv = jnp.transpose(qkv, (4, 0, 2, 1, 3))
        q, k, v = (qkv[0], qkv[1], qkv[2])
        keys = jnp.transpose(k, (0, 2, 1, 3)).reshape(b, n, e)
        log_mix = jax.nn.log_softmax(mix_coef)
        std = jnp.exp(0.5 * logvar)
        z = (keys[:, :, :, None] - mean[None, None, :, :]) / std
        comp_lp = -0.5 * (z * z) - jnp.log(std) - 0.5 * LOG_2PI
        key_mix = jax.nn.logsumexp(comp_lp + log_mix, axis=-1)
        key_mix = jnp.transpose(key_mix.reshape(b, n, H, D), (0, 2, 1, 3))
        energy = jnp.einsum('bhqd,bhkd->bhqk', q, key_mix)
        att = jax.nn.softmax(energy, axis=-1) / jnp.sqrt(jnp.float32(e))
        out = jnp.einsum('bhql,bhld->bhqd', att, v)
        out = jnp.transpose(out, (0, 2, 1, 3)).reshape(b, n, e)
        return out @ Wproj + bproj

    def _L0_ffn_ref(x, ln1_w, ln1_b, ln2_w, ln2_b, attn_qkv_w, attn_qkv_b, attn_proj_w, attn_proj_b, w_g, exp_fc_w, exp_fc_b, exp_proj_w, exp_proj_b):
        import math
        import jax, jax.numpy as jnp
        import numpy as np
        N_HEAD = 12
        N_EXP = 8
        TOP_K = 2
        TRAIN_CAPACITY = 1.25
        MIN_CAPACITY = 4
        LN_EPS = 1e-05
        NEG_INF = -1e+30

        def _layer_norm(x, w, b):
            mu = jnp.mean(x, axis=-1, keepdims=True)
            var = jnp.var(x, axis=-1, keepdims=True)
            return (x - mu) * jax.lax.rsqrt(var + LN_EPS) * w + b

        def _attention(x, qkv_w, qkv_b, proj_w, proj_b):
            B, T, C = x.shape
            H, D = (N_HEAD, C // N_HEAD)
            qkv = x @ qkv_w + qkv_b
            q, k, v = jnp.split(qkv, 3, axis=-1)
            q = q.reshape(B, T, H, D).transpose(0, 2, 1, 3)
            k = k.reshape(B, T, H, D).transpose(0, 2, 1, 3)
            v = v.reshape(B, T, H, D).transpose(0, 2, 1, 3)
            scores = jnp.einsum('bhqd,bhkd->bhqk', q, k) / math.sqrt(D)
            causal = jnp.tril(jnp.ones((T, T), bool))
            scores = jnp.where(causal, scores, NEG_INF)
            attn = jax.nn.softmax(scores, axis=-1)
            y = jnp.einsum('bhqk,bhkd->bhqd', attn, v)
            y = y.transpose(0, 2, 1, 3).reshape(B, T, C)
            return y @ proj_w + proj_b

        def _moe(x, w_g, fc_w, fc_b, pj_w, pj_b):
            B, T, C = x.shape
            N, E, K = (B * T, N_EXP, TOP_K)
            cap = int(math.floor(K * TRAIN_CAPACITY * N / E))
            cap += cap % 2
            cap = max(cap, MIN_CAPACITY)
            logits = (x @ w_g).reshape(N, E)
            _, topk_idx = jax.lax.top_k(logits, K)
            hot = jax.nn.one_hot(topk_idx, E, dtype=jnp.int32)
            sel = hot.sum(axis=1) > 0
            router_probs = jax.nn.softmax(jnp.where(sel, logits, NEG_INF), axis=-1)
            exp_mask = hot.transpose(1, 0, 2)
            exp_rank = jnp.cumsum(exp_mask.reshape(K * N, E), axis=0) - 1
            exp_rank = exp_rank.reshape(K, N, E)
            exp_mask = exp_mask * (exp_rank < cap).astype(jnp.int32)
            exp_rank = jnp.sum(exp_mask * exp_rank, axis=-1)
            exp_weights = exp_mask.astype(x.dtype) * router_probs[None]
            rank_sc = jax.nn.one_hot(exp_rank, cap, dtype=x.dtype)
            cb_weight = jnp.einsum('kne,knc->nec', exp_weights, rank_sc)
            sec_mask = (cb_weight != 0).astype(x.dtype)
            xf = x.reshape(N, C)
            xb = jnp.einsum('nec,nd->ecd', sec_mask, xf)
            h = jax.nn.gelu(jnp.einsum('ecd,edf->ecf', xb, fc_w) + fc_b, approximate=False)
            out = jnp.einsum('ecf,efd->ecd', h, pj_w) + pj_b
            y = jnp.einsum('nec,ecd->nd', cb_weight, out)
            return y.reshape(B, T, C)
        x = x + _attention(_layer_norm(x, ln1_w, ln1_b), attn_qkv_w, attn_qkv_b, attn_proj_w, attn_proj_b)
        x = x + _moe(_layer_norm(x, ln2_w, ln2_b), w_g, exp_fc_w, exp_fc_b, exp_proj_w, exp_proj_b)
        return x

    def _L1_attn_ref(hidden_states, Wq, bq, Wk, bk, Wv, bv, Wo, bo, lambda_q1, lambda_k1, lambda_q2, lambda_k2, subln_w):
        import jax, jax.numpy as jnp
        import numpy as np
        import math
        B, S, H = (2, 512, 192)
        NH = 12
        HD = H // NH // 2
        LAMBDA_INIT = 0.8 - 0.6 * math.exp(-0.3 * 0)
        EPS = 1e-05
        bsz, seq_len, _ = hidden_states.shape
        scaling = HD ** (-0.5)
        q = hidden_states @ Wq + bq
        k = hidden_states @ Wk + bk
        v = hidden_states @ Wv + bv
        q = q.reshape(bsz, seq_len, 2 * NH, HD).transpose(0, 2, 1, 3) * scaling
        k = k.reshape(bsz, seq_len, 2 * NH, HD).transpose(0, 2, 1, 3)
        v = v.reshape(bsz, seq_len, NH, 2 * HD).transpose(0, 2, 1, 3)
        attn = jnp.einsum('bhqd,bhkd->bhqk', q, k)
        attn = jnp.nan_to_num(attn)
        attn = jax.nn.softmax(attn, axis=-1)
        lambda_1 = jnp.exp(jnp.sum(lambda_q1 * lambda_k1))
        lambda_2 = jnp.exp(jnp.sum(lambda_q2 * lambda_k2))
        lambda_full = lambda_1 - lambda_2 + LAMBDA_INIT
        attn = attn.reshape(bsz, NH, 2, seq_len, seq_len)
        attn = attn[:, :, 0] - lambda_full * attn[:, :, 1]
        ctx = jnp.einsum('bhqk,bhkd->bhqd', attn, v)
        rms = jax.lax.rsqrt(jnp.mean(ctx * ctx, axis=-1, keepdims=True) + EPS)
        ctx = ctx * rms * subln_w
        ctx = ctx * (1.0 - LAMBDA_INIT)
        ctx = ctx.transpose(0, 2, 1, 3).reshape(bsz, seq_len, NH * 2 * HD)
        out = ctx @ Wo + bo
        return out

    def _L1_ffn_ref(x, norm_scale, gate_w, gate_b, mlp1_w, mlp1_b, mlp2_w, mlp2_b):
        import jax, jax.numpy as jnp
        import numpy as np
        E = 16
        K = 4
        H = 192
        I = 384
        LIMIT = 7.0
        ALPHA = 1.702
        EPS = 1e-05

        def rmsnorm(x, scale):
            xf = x.astype(jnp.float32)
            inv = jax.lax.rsqrt(jnp.mean(xf * xf, axis=-1, keepdims=True) + EPS)
            return (xf * inv).astype(x.dtype) * scale

        def swiglu(x, limit=LIMIT, alpha=ALPHA):
            x_glu = x[..., ::2]
            x_lin = x[..., 1::2]
            x_glu = jnp.minimum(x_glu, limit)
            x_lin = jnp.clip(x_lin, -limit, limit)
            return x_glu * jax.nn.sigmoid(alpha * x_glu) * (x_lin + 1.0)
        B, T, _ = x.shape
        t = rmsnorm(x, norm_scale)
        g = jnp.einsum('bth,eh->bte', t, gate_w) + gate_b
        top_vals, top_idx = jax.lax.top_k(g, K)
        route_w = jax.nn.softmax(top_vals, axis=-1)
        t_flat = t.reshape(B * T, H)
        idx_flat = top_idx.reshape(B * T, K)
        w_flat = route_w.reshape(B * T, K)
        onehot = jax.nn.one_hot(idx_flat, E, dtype=t_flat.dtype)
        comb = jnp.einsum('nke,nk->ne', onehot, w_flat)
        h = jnp.einsum('nh,ech->nec', t_flat, mlp1_w) + mlp1_b
        a = swiglu(h)
        y = jnp.einsum('nec,ehc->neh', a, mlp2_w) + mlp2_b
        out_flat = jnp.einsum('neh,ne->nh', y, comb)
        return x + out_flat.reshape(B, T, H)
    h = _L0_tok_ref(x, L0_tok_tok_embed, L0_tok_W1, L0_tok_b1, L0_tok_W2, L0_tok_b2)
    h = h + _L0_attn_ref(_layernorm(h, axis=-1), L0_attn_Wqkv, L0_attn_bqkv, L0_attn_Wproj, L0_attn_bproj, L0_attn_mean, L0_attn_logvar, L0_attn_mix_coef)
    h = h + _L0_ffn_ref(_layernorm(h, axis=-1), L0_ffn_ln1_w, L0_ffn_ln1_b, L0_ffn_ln2_w, L0_ffn_ln2_b, L0_ffn_attn_qkv_w, L0_ffn_attn_qkv_b, L0_ffn_attn_proj_w, L0_ffn_attn_proj_b, L0_ffn_w_g, L0_ffn_exp_fc_w, L0_ffn_exp_fc_b, L0_ffn_exp_proj_w, L0_ffn_exp_proj_b)
    h = h + _L1_attn_ref(_layernorm(h, axis=-1), L1_attn_Wq, L1_attn_bq, L1_attn_Wk, L1_attn_bk, L1_attn_Wv, L1_attn_bv, L1_attn_Wo, L1_attn_bo, L1_attn_lambda_q1, L1_attn_lambda_k1, L1_attn_lambda_q2, L1_attn_lambda_k2, L1_attn_subln_w)
    h = h + _L1_ffn_ref(_layernorm(h, axis=-1), L1_ffn_norm_scale, L1_ffn_gate_w, L1_ffn_gate_b, L1_ffn_mlp1_w, L1_ffn_mlp1_b, L1_ffn_mlp2_w, L1_ffn_mlp2_b)
    return h

_drawn_inputs = setup_inputs


def setup_inputs(seed=0):
    import zlib

    import numpy as np

    out = dict(_drawn_inputs(seed))
    spreads = {'L0_ffn_ln1_w': (1.0, 0.6),
     'L0_ffn_ln1_b': (0.0, 0.703),
     'L0_ffn_ln2_w': (1.0, 0.2),
     'L0_ffn_ln2_b': (0.0, 0.396),
     'L0_ffn_attn_qkv_b': (0.0, 0.294),
     'L0_ffn_attn_proj_b': (0.0, 0.1),
     'L0_ffn_exp_fc_b': (0.0, 0.476),
     'L0_ffn_exp_proj_b': (0.0, 0.1),
     'L1_attn_bq': (0.0, 0.8),
     'L1_attn_bk': (0.0, 0.8),
     'L1_attn_bv': (0.0, 0.1),
     'L1_attn_bo': (0.0, 0.1),
     'L1_attn_subln_w': (1.0, 0.6),
     'L1_ffn_norm_scale': (1.0, 0.6),
     'L1_ffn_gate_b': (0.0, 0.8)}
    factors = {'L0_attn_Wqkv': 4.235,
     'L0_attn_bqkv': 8.0,
     'L0_attn_Wproj': 4.294,
     'L0_attn_mean': 8.0,
     'L0_attn_logvar': 8.0,
     'L0_attn_mix_coef': 8.0,
     'L1_attn_Wq': 8.0,
     'L1_attn_Wk': 8.0,
     'L1_attn_lambda_q1': 8.0,
     'L1_attn_lambda_k1': 8.0,
     'L1_attn_lambda_q2': 8.0,
     'L1_attn_lambda_k2': 8.0,
     'L1_ffn_gate_w': 4.396,
     'L1_ffn_mlp1_w': 4.043,
     'L1_ffn_mlp1_b': 8.0,
     'L1_ffn_mlp2_w': 3.94,
     'L1_ffn_mlp2_b': 8.0}
    for name, (base, spread) in spreads.items():
        noise = np.random.default_rng([zlib.crc32(name.encode()), seed]).standard_normal(out[name].shape)
        drawn = base * np.exp(spread * noise) if base else spread * noise
        out[name] = jnp.asarray(drawn.astype(out[name].dtype))
    for name, factor in factors.items():
        out[name] = (out[name] * factor).astype(out[name].dtype)
    return out
```

```python
from contextlib import ExitStack

import numpy as np

import concourse.bass as bass
from concourse import mybir

F32 = mybir.dt.float32
BF16 = mybir.dt.bfloat16
U32 = mybir.dt.uint32
I32 = mybir.dt.int32
ALU = mybir.AluOpType
ACT = mybir.ActivationFunctionType
AX = mybir.AxisListType

P = 128
B, S = 4, 512
N = B * S
NT = N // P
TPB = S // P
C = 192
HC = C // 2
NH = 12
HD = C // NH
VP = 32
VW = NH * VP
NC4 = NH // 4
FRONT = 768
EPS = 1e-5
MASKED = -1e30
HUGE = 1e30
BIG_SCORE = 1e18
CAPACITY = 640
LAMBDA_INIT = 0.8 - 0.6 * float(np.exp(-0.3 * 0))


def link(eng, sem, count, ins):
    count[0] += 1
    ins.then_inc(sem, 1)
    eng.wait_ge(sem, count[0])


class Slots:

    def __init__(self, sem, name, size):
        self.size = size
        self.ready = [sem(f"{name}_ready{s}") for s in range(size)]
        self.free = [sem(f"{name}_free{s}") for s in range(size)]

    def wait_free(self, pe, n):
        if n >= self.size:
            pe.wait_ge(self.free[n % self.size], n // self.size)

    def wait_ready(self, eng, n):
        eng.wait_ge(self.ready[n % self.size], n // self.size + 1)


def build_constants(nc, cx, sb, sem):
    k = {}
    k["ident"] = sb("ident", [P, P], F32)
    k["identb"] = sb("identb", [P, P], BF16)
    k["before"] = sb("before", [P, P], F32)
    k["ones"] = sb("ones", [P, P], F32)
    k["mask_qk"] = sb("mask_qk", [P, P], BF16)
    k["mask_kq"] = sb("mask_kq", [P, P], BF16)
    k["sel_sum"] = sb("sel_sum", [P, P], F32)
    k["sel_sum_mix"] = sb("sel_sum_mix", [P, P], F32)
    k["sel_mean"] = sb("sel_mean", [P, P], F32)
    filled = sem("const_filled")
    done = sem("const_done")
    with nc.Block() as block:
        @block.gpsimd
        def _(pool):
            for name, value in (("ident", 0.0), ("identb", 0.0), ("before", 1.0), ("ones", 1.0), ("mask_qk", 0.0),
                                ("mask_kq", 0.0), ("sel_sum", 0.0), ("sel_sum_mix", 0.0), ("sel_mean", 1.0 / HD)):
                last = nc.gpsimd.memset(k[name][:], value)
            last.then_inc(filled, 1)
            pool.wait_ge(filled, 1)

            def select(name, pattern, base, mult, op, fill):
                t = k[name][:]
                if len(pattern) == 2:
                    t = t.rearrange("p (a b) -> p a b", a=pattern[0][1])
                return nc.gpsimd.affine_select(out=t, in_=t, pattern=pattern, compare_op=op, fill=fill, base=base,
                                               channel_multiplier=mult)
            select("ident", [[-1, P]], 0, 1, ALU.not_equal, 1.0)
            select("identb", [[-1, P]], 0, 1, ALU.not_equal, 1.0)
            select("before", [[1, P]], 0, -1, ALU.is_gt, 0.0)
            select("mask_qk", [[-1, P]], 0, 1, ALU.is_ge, MASKED)
            select("mask_kq", [[1, P]], 0, -1, ALU.is_ge, MASKED)
            select("sel_sum", [[-VP, 4], [0, VP]], -HD, 1, ALU.not_equal, 1.0)
            select("sel_sum_mix", [[-VP, 4], [0, VP]], -HD, 1, ALU.not_equal, float(np.sqrt(np.float32(C))))
            select("sel_mean", [[-VP, 4], [0, VP]], 0, 1, ALU.is_ge, 0.0).then_inc(done, 1)
            pool.wait_ge(done, 1)
            select("sel_mean", [[VP, 4], [0, VP]], HD - 1, -1, ALU.is_ge, 0.0).then_inc(done, 1)
    return k


def embed(nc, k, sem, d, h):
    FK = FRONT // P
    RING = 2
    with ExitStack() as cx:
        def sb(name, shape, dt=F32):
            return cx.enter_context(nc.sbuf_tensor(name, shape, dt))

        def ps(name, shape, dt=F32):
            return cx.enter_context(nc.psum_tensor(name, shape, dt))
        ids = sb("ids", [P, NT], I32)
        w1 = sb("w1", [P, FK, C])
        w2 = sb("w2", [HC, 2, C])
        b1 = sb("b1", [HC, 2])
        b2 = sb("b2", [P, C])
        rows = sb("rows", [P, RING * TPB, FRONT])
        rowsT = sb("rowsT", [P, RING, FK, S])
        act = sb("act", [HC, RING, 2, S])
        tp = ps("tp", [P, 2, 1024])
        hid = ps("hid", [P, 2, S])
        outp = ps("outp", [P, 2, S])
        ids_in, weights_in = sem("em_ids_in"), sem("em_weights_in")
        gathered = [sem(f"em_gathered{i}") for i in range(RING * TPB)]
        transposed, rows_moved = sem("em_transposed"), sem("em_rows_moved")
        hidden, activated = sem("em_hidden"), sem("em_activated")
        projected, stored = sem("em_projected"), sem("em_stored")
        with nc.Block() as block:
            @block.sync
            def _(sp):
                sp.dma_start(ids[:], d["ids"]).then_inc(ids_in, 16)
                sp.dma_start(w1[:], d["tok_W1"]).then_inc(weights_in, 16)
                sp.dma_start(w2[:], d["tok_W2"]).then_inc(weights_in, 16)
                sp.dma_start(b1[:], d["tok_b1"]).then_inc(weights_in, 16)
                sp.dma_start(b2[:], d["tok_b2"].partition_broadcast(P)).then_inc(weights_in, 16)

            @block.gpsimd
            def _(pool):
                pool.wait_ge(ids_in, 16)
                for t in range(NT):
                    slot = t % (RING * TPB)
                    if t >= RING * TPB:
                        pool.wait_ge(transposed, t - RING * TPB + 1)
                    pool.indirect_dma_start(
                        out=rows[:, slot, :], out_offset=None, in_=d["tok_embed"],
                        in_offset=bass.IndirectOffsetOnAxis(ap=ids[:, t:t + 1].bitcast(U32), axis=0),
                    ).then_inc(gathered[slot], 16)

            @block.tensor
            def _(pe):
                pe.wait_ge(weights_in, 64)

                def project(b):
                    for i in range(TPB):
                        t = b * TPB + i
                        if i == 0:
                            pe.wait_ge(activated, 2 * b + 2)
                        if t >= 2:
                            pe.wait_ge(stored, t - 1)
                        for c in range(2):
                            mm = nc.tensor.matmul(outp[:, t % 2, 0:C], act[:, b % RING, c, i * P:(i + 1) * P], w2[:, c, :],
                                                  start=c == 0, stop=c == 1)
                        mm.then_inc(projected, 1)
                for b in range(B):
                    for i in range(TPB):
                        t = b * TPB + i
                        slot = t % (RING * TPB)
                        pe.wait_ge(gathered[slot], 16 * (t // (RING * TPB) + 1))
                        if t >= 2:
                            pe.wait_ge(rows_moved, t - 1)
                        for f in range(FK):
                            mm = nc.tensor.transpose(tp[:, t % 2, f * P:(f + 1) * P], rows[:, slot, f * P:(f + 1) * P],
                                                     k["ident"][:])
                        mm.then_inc(transposed, 1)
                    pe.wait_ge(rows_moved, (b + 1) * TPB)
                    for m in range(2):
                        if b >= 1:
                            pe.wait_ge(activated, 2 * (b - 1) + m + 1)
                        for f in range(FK):
                            mm = nc.tensor.matmul(hid[0:HC, m, :], w1[:, f, m * HC:(m + 1) * HC], rowsT[:, b % RING, f, :],
                                                  start=f == 0, stop=f == FK - 1)
                        mm.then_inc(hidden, 1)
                    if b >= 1:
                        project(b - 1)
                project(B - 1)

            @block.scalar
            def _(act_):
                act_.wait_ge(weights_in, 64)
                for b in range(B):
                    for m in range(2):
                        act_.wait_ge(hidden, 2 * b + m + 1)
                        if b >= RING:
                            act_.wait_ge(projected, (b - RING + 1) * TPB)
                        nc.scalar.activation(act[:, b % RING, m, :], hid[0:HC, m, :], ACT.Gelu, bias=b1[:, m:m + 1])\
                            .then_inc(activated, 1)

            @block.vector
            def _(dve):
                dve.wait_ge(weights_in, 64)

                def store(b):
                    for i in range(TPB):
                        t = b * TPB + i
                        dve.wait_ge(projected, t + 1)
                        nc.vector.tensor_tensor(h[:, t, :], outp[:, t % 2, 0:C], b2[:], ALU.add).then_inc(stored, 1)
                for b in range(B):
                    for i in range(TPB):
                        t = b * TPB + i
                        dve.wait_ge(transposed, t + 1)
                        if b >= RING:
                            dve.wait_ge(hidden, 2 * (b - RING + 1))
                        nc.vector.tensor_copy(rowsT[:, b % RING, :, i * P:(i + 1) * P],
                                              tp[:, t % 2, 0:FRONT].rearrange("p (f t) -> p f t", f=FK)).then_inc(rows_moved, 1)
                    if b >= 1:
                        store(b - 1)
                store(B - 1)


def normalise(nc, k, sem, tag, src, dst, dstT=None, gain=None, shift=None, rms=False):
    with ExitStack() as cx:
        def sb(name, shape, dt=F32):
            return cx.enter_context(nc.sbuf_tensor(tag + name, shape, dt))
        stats = sb("stats", [P, NT, 6])
        mv = sb("mv", [P, NT, 2])
        spread = sb("spread", [P, NT])
        root = sb("root", [P, NT])
        rstd = sb("rstd", [P, NT])
        gain_bc = sb("gain_bc", [P, C])
        shift_bc = sb("shift_bc", [P, C])
        slot = [cx.enter_context(nc.psum_tensor(f"{tag}slot{i}", [P, 512], F32)) for i in range(2)]
        affine_in = sem(tag + "affine_in")
        chain = sem(tag + "chain")
        spread_ready, root_ready = sem(tag + "spread_ready"), sem(tag + "root_ready")
        tile_ready = sem(tag + "tile_ready")
        transposed, moved = sem(tag + "transposed"), sem(tag + "moved")
        with nc.Block() as block:
            if gain is not None:
                @block.sync
                def _(sp):
                    sp.dma_start(gain_bc[:], gain.partition_broadcast(P)).then_inc(affine_in, 16)
                    if shift is not None:
                        sp.dma_start(shift_bc[:], shift.partition_broadcast(P)).then_inc(affine_in, 16)

            @block.vector
            def _(dve):
                n = [0]
                for t in range(NT):
                    last = nc.vector.bn_stats(stats[:, t, :], src[:, t, :])
                link(dve, chain, n, last)
                for t in range(NT):
                    last = nc.vector.bn_aggr(mv[:, t, :], stats[:, t, :])
                link(dve, chain, n, last)
                if rms:
                    link(dve, chain, n, nc.vector.tensor_tensor(root[:], mv[:, :, 0], mv[:, :, 0], ALU.mult))
                    link(dve, chain, n, nc.vector.tensor_tensor(spread[:], root[:], mv[:, :, 1], ALU.add))
                    nc.vector.tensor_scalar(spread[:], spread[:], EPS, None, ALU.add).then_inc(spread_ready, 1)
                else:
                    nc.vector.tensor_scalar(spread[:], mv[:, :, 1], EPS, None, ALU.add).then_inc(spread_ready, 1)
                dve.wait_ge(root_ready, 1)
                link(dve, chain, n, nc.vector.reciprocal(rstd[:], root[:]))
                if gain is not None:
                    dve.wait_ge(affine_in, 32 if shift is not None else 16)
                for t in range(NT):
                    if rms:
                        last = nc.vector.tensor_scalar(dst[:, t, :], src[:, t, :], rstd[:, t:t + 1], None, ALU.mult)
                    else:
                        last = nc.vector.tensor_scalar(dst[:, t, :], src[:, t, :], mv[:, t, 0:1], rstd[:, t:t + 1],
                                                       ALU.subtract, ALU.mult)
                    if gain is None:
                        last.then_inc(tile_ready, 1)
                if gain is not None:
                    link(dve, chain, n, last)
                    whole = [P, NT, C]
                    g = gain_bc[:].unsqueeze(1).to_broadcast(whole)
                    last = nc.vector.tensor_tensor(dst[:], dst[:], g, ALU.mult)
                    if shift is not None:
                        link(dve, chain, n, last)
                        s = shift_bc[:].unsqueeze(1).to_broadcast(whole)
                        last = nc.vector.tensor_tensor(dst[:], dst[:], s, ALU.add)
                    last.then_inc(tile_ready, 1)

            @block.tensor
            def _(pe):
                for t in range(NT if dstT is not None else 0):
                    pe.wait_ge(tile_ready, t + 1 if gain is None else 1)
                    if t >= 2:
                        pe.wait_ge(moved, t - 1)
                    for c in range(2):
                        mm = nc.tensor.transpose(slot[t % 2][0:HC, c * P:(c + 1) * P], dst[:, t, c * HC:(c + 1) * HC],
                                                 k["ident"][:])
                    mm.then_inc(transposed, 1)

            @block.scalar
            def _(act):
                act.wait_ge(spread_ready, 1)
                nc.scalar.activation(root[:], spread[:], ACT.Sqrt).then_inc(root_ready, 1)
                for t in range(NT if dstT is not None else 0):
                    act.wait_ge(transposed, t + 1)
                    nc.scalar.activation(dstT[0:HC, :, t * P:(t + 1) * P],
                                         slot[t % 2][0:HC, 0:2 * P].rearrange("p (c t) -> p c t", c=2), ACT.Copy)\
                        .then_inc(moved, 1)


def project_qkv(nc, k, sem, tag, d, xT, q_pieces, k_pieces, vals, keys=None, guard=False):
    with ExitStack() as cx:
        def sb(name, shape, dt=F32):
            return cx.enter_context(nc.sbuf_tensor(tag + name, shape, dt))
        wq, wk, wv = (sb(x, [HC, 2, C]) for x in ("wq", "wk", "wv"))
        bq, bk = sb("bq", [HC, 2]), sb("bk", [HC, 2])
        bkp = sb("bkp", [P, 2])
        bv = sb("bv", [P, C])
        R = 2
        x = sb("x", [HC, R, S])
        rest = sb("rest", [HC, R, S])
        piece = [sb(f"piece{i}", [HC, R, S], BF16) for i in range(3)]
        slot = [cx.enter_context(nc.psum_tensor(f"{tag}slot{i}", [P, 512], F32)) for i in range(4)]
        ring = Slots(sem, tag + "slot", 4)
        weights_in = sem(tag + "weights_in")
        chain = sem(tag + "chain")
        x_ready, hi_ready, rest_ready = sem(tag + "x_ready"), sem(tag + "hi_ready"), sem(tag + "rest_ready")
        mid_ready, lo_ready = sem(tag + "mid_ready"), sem(tag + "lo_ready")
        pieces_out = [sem(f"{tag}pieces_out{i}") for i in range(R)]
        ones_set = sem(tag + "ones_set")
        items = [("q", c, b) for c in range(2) for b in range(B)]
        if keys is None:
            items += [("k", c, b) for c in range(2) for b in range(B)]
        splits = list(items)
        if keys is not None:
            items += [("key", i, 0) for i in range(6)]
        items += [("v", t, 0) for t in range(NT)]
        with nc.Block() as block:
            @block.sync
            def _(sp):
                loads = [(wq[:], d["Wq"]), (wk[:], d["Wk"]), (wv[:], d["Wv"]), (bq[:], d["bq"]), (bk[:], d["bk"]),
                         (bv[:], d["bv"].partition_broadcast(P))]
                if keys is not None:
                    loads.append((bkp[:], d["bk_packed"]))
                for dst, src in loads:
                    sp.dma_start(dst, src).then_inc(weights_in, 16)
                for n, (what, c, b) in enumerate(splits):
                    out = q_pieces if what == "q" else k_pieces
                    for i, sig in enumerate((hi_ready, mid_ready, lo_ready)):
                        sp.wait_ge(sig, n + 1)
                        sp.dma_start(out[i, c * HC:(c + 1) * HC, b * S:(b + 1) * S], piece[i][:, n % R, :])\
                            .then_inc(pieces_out[n % R], 16)
                for r in range(R):
                    sp.wait_ge(pieces_out[r], 48 * (len(splits) // R))

            @block.gpsimd
            def _(pool):
                nc.gpsimd.memset(vals[:], 0.0).then_inc(ones_set, 1)
                pool.wait_ge(ones_set, 1)
                nc.gpsimd.memset(vals[:].rearrange("p t (h e) -> p (t h) e", e=VP)[:, :, HD:HD + 1], 1.0)\
                    .then_inc(ones_set, 1)

            @block.tensor
            def _(pe):
                pe.wait_ge(weights_in, 16 * (7 if keys is not None else 6))
                for n, (what, c, b) in enumerate(items):
                    out = slot[n % 4]
                    ring.wait_free(pe, n)
                    for h in range(2):
                        if what == "v":
                            mm = nc.tensor.matmul(out[:, 0:C], xT[0:HC, h, c * P:(c + 1) * P], wv[:, h, :],
                                                  start=h == 0, stop=h == 1)
                        elif what == "key" and c < 4:
                            mm = nc.tensor.matmul(out[:], wk[:, h, 0:P], xT[0:HC, h, c * S:(c + 1) * S],
                                                  start=h == 0, stop=h == 1)
                        elif what == "key":
                            mm = nc.tensor.matmul(out[0:64, :], wk[:, h, P:C], xT[0:HC, h, (c - 4) * S:(c - 3) * S],
                                                  start=h == 0, stop=h == 1)
                        else:
                            w = wq if what == "q" else wk
                            mm = nc.tensor.matmul(out[0:HC, :], w[:, h, c * HC:(c + 1) * HC],
                                                  xT[0:HC, h, b * S:(b + 1) * S], start=h == 0, stop=h == 1)
                    if what == "key" and c >= 4:
                        for h in range(2):
                            mm = nc.tensor.matmul(out[64:P, :], wk[:, h, P:C], xT[0:HC, h, (c - 2) * S:(c - 1) * S],
                                                  start=h == 0, stop=h == 1)
                    mm.then_inc(ring.ready[n % 4], 1)

            @block.vector
            def _(dve):
                cnt = [0]
                dve.wait_ge(weights_in, 16 * (7 if keys is not None else 6))
                for n, (what, c, b) in enumerate(items):
                    ring.wait_ready(dve, n)
                    src = slot[n % 4]
                    if what == "v":
                        if c == 0:
                            dve.wait_ge(ones_set, 2)
                        nc.vector.tensor_tensor(vals[:, c, :].rearrange("p (h e) -> p h e", e=VP)[:, :, 0:HD],
                                                src[:, 0:C].rearrange("p (h e) -> p h e", e=HD),
                                                bv[:].rearrange("p (h e) -> p h e", e=HD), ALU.add)\
                            .then_inc(ring.free[n % 4], 1)
                        continue
                    if what == "key":
                        nc.vector.tensor_scalar(keys[:, c // 2, (c % 2) * S:(c % 2 + 1) * S], src[:],
                                                bkp[:, c // 4:c // 4 + 1], None, ALU.add).then_inc(ring.free[n % 4], 1)
                        continue
                    bias = bq if what == "q" else bk
                    r = n % R
                    ins = nc.vector.tensor_scalar(x[:, r, :], src[0:HC, :], bias[:, c:c + 1], None, ALU.add)
                    ins.then_inc(ring.free[n % 4], 1)
                    dve.wait_ge(ring.free[n % 4], n // 4 + 1)
                    if guard:
                        link(dve, chain, cnt, nc.vector.tensor_scalar(x[:, r, :], x[:, r, :], -BIG_SCORE, BIG_SCORE,
                                                                      ALU.max, ALU.min))
                    if n >= R:
                        dve.wait_ge(pieces_out[r], 48 * (n // R))
                    nc.vector.tensor_copy(piece[0][:, r, :], x[:, r, :]).then_inc(hi_ready, 1)
                    dve.wait_ge(hi_ready, n + 1)
                    nc.vector.tensor_tensor(rest[:, r, :], x[:, r, :], piece[0][:, r, :], ALU.subtract)\
                        .then_inc(rest_ready, 1)
                    dve.wait_ge(mid_ready, n + 1)
                    nc.vector.tensor_tensor(piece[2][:, r, :], rest[:, r, :], piece[1][:, r, :], ALU.subtract)\
                        .then_inc(lo_ready, 1)

            @block.scalar
            def _(act):
                for n in range(len(splits)):
                    r = n % R
                    act.wait_ge(rest_ready, n + 1)
                    if n >= R:
                        act.wait_ge(pieces_out[r], 48 * (n // R))
                    nc.scalar.activation(piece[1][:, r, :], rest[:, r, :], ACT.Copy).then_inc(mid_ready, 1)


def mixture_tables(nc, sem, d, tab):
    with ExitStack() as cx:
        def sb(name, shape, dt=F32):
            return cx.enter_context(nc.sbuf_tensor("mt_" + name, shape, dt))
        mean = sb("mean", [P, 2, C])
        logvar = sb("logvar", [P, 2, C])
        mix = sb("mix", [P, C])
        emix = sb("emix", [P, C])
        top, neg_top, esum, log_esum, off, half_log2 = (sb(x, [P, 1]) for x in (
            "top", "neg_top", "esum", "log_esum", "off", "half_log2"))
        loads, chain = sem("mt_loads"), sem("mt_chain")
        top_ready, exp_ready, log_ready, scale_ready = (sem("mt_" + x) for x in (
            "top_ready", "exp_ready", "log_ready", "scale_ready"))
        with nc.Block() as block:
            @block.sync
            def _(sp):
                for t, name in ((mean, "mix_mean"), (logvar, "mix_logvar")):
                    sp.dma_start(t[:, 0, :], d[name][0:P, :]).then_inc(loads, 16)
                    sp.dma_start(t[0:64, 1, :], d[name][P:C, :]).then_inc(loads, 16)
                    sp.dma_start(t[64:P, 1, :], d[name][P:C, :]).then_inc(loads, 16)
                sp.dma_start(mix[:], d["mix_coef"].partition_broadcast(P)).then_inc(loads, 16)

            @block.scalar
            def _(act):
                act.wait_ge(top_ready, 1)
                nc.scalar.activation(emix[:], mix[:], ACT.Exp, bias=neg_top[:], accum_out=esum[:]).then_inc(exp_ready, 1)
                nc.scalar.activation(tab[:, 0], logvar[:], ACT.Exp, scale=-0.5, bias=half_log2[:]).then_inc(scale_ready, 1)
                act.wait_ge(exp_ready, 1)
                nc.scalar.activation(log_esum[:], esum[:], ACT.Ln).then_inc(log_ready, 1)

            @block.vector
            def _(dve):
                cnt = [0]
                dve.wait_ge(loads, 16 * 7)
                nc.vector.memset(half_log2[:], float(-0.5 * np.log(2.0)))
                link(dve, chain, cnt, nc.vector.tensor_reduce(top[:], mix[:], axis=AX.X, op=ALU.max))
                nc.vector.tensor_scalar(neg_top[:], top[:], -1.0, None, ALU.mult).then_inc(top_ready, 1)
                dve.wait_ge(log_ready, 1)
                link(dve, chain, cnt, nc.vector.tensor_tensor(off[:], neg_top[:], log_esum[:], ALU.subtract))
                link(dve, chain, cnt, nc.vector.tensor_scalar(emix[:], mix[:], off[:], float(-0.5 * np.log(2.0 * np.pi)),
                                                              ALU.add, ALU.add))
                dve.wait_ge(scale_ready, 1)
                nc.vector.scalar_tensor_tensor(out=tab[:, 2], in0=logvar[:], scalar=-0.5,
                                               in1=emix[:].unsqueeze(1).to_broadcast([P, 2, C]), op0=ALU.mult, op1=ALU.add)
                nc.vector.scalar_tensor_tensor(out=tab[:, 1], in0=mean[:], scalar=-1.0, in1=tab[:, 0],
                                               op0=ALU.mult, op1=ALU.mult)


def mixture_keys(nc, k, sem, tab, keys, k_pieces):
    G = 12
    D = 8
    PART = 2
    EXPS = D // PART + G - D
    POOLS = (G - D) // PART
    PARTS = G // PART
    LATE = PARTS - 2
    NG = C // G
    BLOCKS = 3
    W = N // 2
    with ExitStack() as cx:
        def sb(name, shape, dt=F32):
            return cx.enter_context(nc.sbuf_tensor("mk_" + name, shape, dt))
        buf = sb("buf", [P, 2, G, W])
        neg_max = sb("neg_max", [P, 2, W])
        last_neg_max = sb("last_neg_max", [P, W])
        drop, alpha, scaled, mixed = (sb(x, [P, W]) for x in ("drop", "alpha", "scaled", "mixed"))
        piece = [sb(f"piece{i}", [P, W], BF16) for i in range(3)]
        total = [cx.enter_context(nc.psum_tensor(f"mk_total{i}", [P, W], F32)) for i in range(2)]
        lowest = cx.enter_context(nc.psum_tensor("mk_lowest", [P, W], F32))
        squared, lowered, off_dve, off_pool, exped, summed = (sem("mk_" + x) for x in (
            "squared", "lowered", "off_dve", "off_pool", "exped", "summed"))
        dropped, alpha_ready, scaled_ready, total_ready = (sem("mk_" + x) for x in (
            "dropped", "alpha_ready", "scaled_ready", "total_ready"))
        log_ready, kept_ready, pieces_ready = (sem("mk_" + x) for x in ("log_ready", "kept_ready", "pieces_ready"))
        chain, stored = sem("mk_chain"), sem("mk_stored")

        def column(t, ch, m):
            return tab[:, t, ch // 2, bass.ds(m, 1)]

        def back(ch, g, by):
            if isinstance(g, int) and g < by:
                ch, g = ch - 1, g + NG
            return None if ch < 0 or (ch == BLOCKS and isinstance(g, int)) or ch > BLOCKS else (ch, g - by)

        def each_group(engine, step):
            for ch in range(BLOCKS + 1):
                for g in range(2):
                    step(ch, g, g, ch * NG + g)
                if ch < BLOCKS:
                    with engine.Fori(1, NG // 2) as i:
                        for par in range(2):
                            step(ch, 2 * i + par, par, 2 * i + (ch * NG + par))
        with nc.Block() as block:
            @block.scalar
            def _(act):
                def squares(ch, g, par, n, part):
                    if not isinstance(n, int) or n >= 2:
                        act.wait_ge(summed, (n - 2) * PARTS + part + 1)
                    for j in range(part * PART, part * PART + PART):
                        nc.scalar.activation(buf[:, par, j, :], keys[:, ch, :], ACT.Square, scale=column(0, ch, g * G + j),
                                             bias=column(1, ch, g * G + j)).then_inc(squared, 1)

                def exps(ch, g, par, n, part):
                    if part * PART < D:
                        act.wait_ge(off_dve, n * D + part * PART + PART)
                        both = buf[:, par, part * PART:part * PART + PART, :]
                        nc.scalar.activation(both, both, ACT.Exp, scale=-1.0).then_inc(exped, 1)
                        return
                    act.wait_ge(off_pool, n * POOLS + part - D // PART + 1)
                    for j in range(part * PART, part * PART + PART):
                        nc.scalar.activation(buf[:, par, j, :], buf[:, par, j, :], ACT.Exp, scale=-1.0,
                                             bias=column(2, ch, g * G + j)).then_inc(exped, 1)

                def step(ch, g, par, n):
                    for part in range(PARTS):
                        if ch < BLOCKS:
                            squares(ch, g, par, n, part)
                        if part == 0 and back(ch, g, 2):
                            exps(*back(ch, g, 2), par, n - 2, PARTS - 1)
                        if part > 0 and back(ch, g, 1):
                            exps(*back(ch, g, 1), 1 - par, n - 1, part - 1)
                        if part == 1 and back(ch, g, 1):
                            act.wait_ge(dropped, n)
                            if not isinstance(n, int) or n >= 2:
                                act.wait_ge(scaled_ready, n - 1)
                            nc.scalar.activation(alpha[:], drop[:], ACT.Exp).then_inc(alpha_ready, 1)
                        if part == LATE and isinstance(g, int) and g == 1 and ch > 0:
                            act.wait_ge(total_ready, ch * NG + 1)
                            if ch > 1:
                                act.wait_ge(pieces_ready, ch - 1)
                            nc.scalar.activation(mixed[:], total[1][:], ACT.Ln).then_inc(log_ready, 1)
                each_group(act, step)

            @block.vector
            def _(dve):
                def minimum(ch, g, par, n, j):
                    dve.wait_ge(squared, n * G + j + 1)
                    if not isinstance(n, int) or n > 0 or j > 0:
                        dve.wait_ge(lowered, n * G + j)
                    if j == G - 1 and (not isinstance(n, int) or n >= 2):
                        dve.wait_ge(dropped, n)
                        dve.wait_ge(off_dve, (n - 1) * D)
                        if isinstance(g, int) and g == 1 and ch > 0:
                            dve.wait_ge(kept_ready, ch)
                    out = lowest[:] if j < G - 1 else neg_max[:, par, :]
                    if j == 0 and isinstance(g, int) and g == 0:
                        nc.vector.tensor_scalar(out, buf[:, par, j, :], column(2, ch, g * G + j), None, ALU.subtract)\
                            .then_inc(lowered, 1)
                    else:
                        nc.vector.scalar_tensor_tensor(out=out, in0=buf[:, par, j, :], scalar=column(2, ch, g * G + j),
                                                       in1=lowest[:] if j else neg_max[:, 1 - par, :],
                                                       op0=ALU.subtract, op1=ALU.min).then_inc(lowered, 1)

                def take_off(ch, g, par, j):
                    nc.vector.scalar_tensor_tensor(out=buf[:, par, j, :], in0=buf[:, par, j, :],
                                                   scalar=column(2, ch, g * G + j), in1=neg_max[:, par, :],
                                                   op0=ALU.subtract, op1=ALU.subtract).then_inc(off_dve, 1)

                def step(ch, g, par, n):
                    if back(ch, g, 1):
                        dve.wait_ge(lowered, n * G)
                    for j in range(G):
                        if j < D and back(ch, g, 1):
                            take_off(*back(ch, g, 1), 1 - par, j)
                        if ch < BLOCKS:
                            minimum(ch, g, par, n, j)
                        if j == LATE * PART and back(ch, g, 1):
                            dve.wait_ge(alpha_ready, n)
                            dve.wait_ge(total_ready, n)
                            if isinstance(g, int) and g == 1 and ch > 0:
                                dve.wait_ge(log_ready, ch)
                            nc.vector.tensor_tensor(scaled[:], total[par][:], alpha[:], ALU.mult).then_inc(scaled_ready, 1)
                nc.vector.memset(total[1][:], 0.0).then_inc(total_ready, 1)
                each_group(dve, step)

            @block.gpsimd
            def _(pool):
                count = [0]

                def group(ch, g, par):
                    n = ch * NG + g
                    pool.wait_ge(lowered, (n + 1) * G)
                    if not isinstance(n, int) or n > 0:
                        pool.wait_ge(alpha_ready, n)
                    if isinstance(g, int) and g == 0:
                        nc.gpsimd.memset(drop[:], -HUGE).then_inc(dropped, 1)
                    else:
                        nc.gpsimd.tensor_tensor(drop[:], neg_max[:, par, :], neg_max[:, 1 - par, :], ALU.subtract)\
                            .then_inc(dropped, 1)
                    for j in range(D, G, PART):
                        part = buf[:, par, j:j + PART, :]
                        nc.gpsimd.tensor_tensor(part, part, neg_max[:, par, :].unsqueeze(1).to_broadcast([P, PART, W]),
                                                ALU.subtract).then_inc(off_pool, 1)

                def finish(ch):
                    pool.wait_ge(log_ready, ch + 1)
                    link(pool, chain, count, nc.gpsimd.tensor_tensor(mixed[:], mixed[:], last_neg_max[:], ALU.subtract))
                    if ch:
                        pool.wait_ge(stored, 48 * ch)
                    link(pool, chain, count, nc.gpsimd.tensor_copy(piece[0][:], mixed[:]))
                    link(pool, chain, count, nc.gpsimd.tensor_tensor(mixed[:], mixed[:], piece[0][:], ALU.subtract))
                    link(pool, chain, count, nc.gpsimd.tensor_copy(piece[1][:], mixed[:]))
                    nc.gpsimd.tensor_tensor(piece[2][:], mixed[:], piece[1][:], ALU.subtract).then_inc(pieces_ready, 1)
                for ch in range(BLOCKS):
                    group(ch, 0, 0)
                    group(ch, 1, 1)
                    if ch:
                        finish(ch - 1)
                    with pool.Fori(1, NG // 2) as i:
                        for par in range(2):
                            group(ch, 2 * i + par, par)
                    if ch:
                        pool.wait_ge(pieces_ready, ch)
                    nc.gpsimd.tensor_copy(last_neg_max[:], neg_max[:, 1, :]).then_inc(kept_ready, 1)
                pool.wait_ge(kept_ready, BLOCKS)
                finish(BLOCKS - 1)

            @block.tensor
            def _(pe):
                def sums(ch, g, par, first=False, logged=False):
                    n = ch * NG + g
                    for j in range(G):
                        if j < D and j % PART == 0:
                            pe.wait_ge(exped, n * EXPS + j // PART + 1)
                        elif j >= D:
                            pe.wait_ge(exped, n * EXPS + D // PART + j - D + 1)
                        if j == 0 and not first:
                            pe.wait_ge(scaled_ready, n)
                            if logged:
                                pe.wait_ge(log_ready, ch)
                        for w in range(0, W, 512):
                            mm = nc.tensor.matmul(total[par][:, w:w + 512], k["ident"][:], buf[:, par, j, w:w + 512],
                                                  start=j == 0, stop=False)
                        if j % PART == PART - 1:
                            mm.then_inc(summed, 1)
                    pe.wait_ge(scaled_ready, n + 1)
                    for w in range(0, W, 512):
                        mm = nc.tensor.matmul(total[par][:, w:w + 512], k["ident"][:], scaled[:, w:w + 512],
                                              start=False, stop=True)
                    mm.then_inc(total_ready, 1)
                for ch in range(BLOCKS):
                    sums(ch, 0, 0, first=ch == 0)
                    sums(ch, 1, 1, logged=ch > 0)
                    with pe.Fori(1, NG // 2) as i:
                        sums(ch, 2 * i, 0)
                        sums(ch, 2 * i + 1, 1)

            @block.sync
            def _(sp):
                for ch in range(BLOCKS):
                    sp.wait_ge(pieces_ready, ch + 1)
                    for i in range(3):
                        if ch < 2:
                            sp.dma_start(k_pieces[i, 0:P, ch * W:(ch + 1) * W], piece[i][:]).then_inc(stored, 16)
                        else:
                            sp.dma_start(k_pieces[i, P:C, 0:W], piece[i][0:64, :]).then_inc(stored, 16)
                            sp.dma_start(k_pieces[i, P:C, W:N], piece[i][64:P, :]).then_inc(stored, 16)
                sp.wait_ge(stored, 48 * 4)


PAIRS = [(0, 0), (0, 1), (1, 0), (1, 1), (0, 2), (2, 0), (1, 2), (2, 1), (2, 2)]
ROWS = 96


def attend(nc, k, sem, tag, q_pieces, k_pieces, vals, yT, heads, scale, causal=False, sel="sel_sum", neg_lambda=None):
    hd = C // heads
    subs = heads // NH
    pairs = PAIRS[:6] if hd == HD else PAIRS
    groups = [(c, s, kt) for c in range(NC4) for s in range(subs) for kt in range(TPB)]
    EI = 2 * len(groups)
    items = [("max", g, qt) for g in range(heads // 2) for qt in range(TPB)] + [("rows", 0, 0)]
    for i, (c, s, kt) in enumerate(groups):
        items += [("exp", 2 * i, (c, s, kt, 0)), ("exp", 2 * i + 1, (c, s, kt, 1))]
        if c > 0 and (s, kt) == (0, 1):
            items.append(("norm", c - 1, 0))
    items.append(("norm", NC4 - 1, 0))
    assert len(items) % 2 == 0 and EI % 4 == 0
    nth = []
    for n, item in enumerate(items):
        nth.append(sum((x[0] == "exp") == (item[0] == "exp") for x in items[:n]))
    DI = len(items) - EI
    LOADS = 16 * 2 * len(pairs)
    with ExitStack() as cx:
        def sb(name, shape, dt=F32):
            return cx.enter_context(nc.sbuf_tensor(tag + name, shape, dt))
        qs = sb("qs", [ROWS + 3, heads, S], BF16)
        ks = sb("ks", [ROWS + 3, heads, S], BF16)
        vb = sb("vb", [P, TPB, VW])
        pt = sb("pt", [P, 4, 2, S])
        top = sb("top", [P, TPB, heads])
        rest = sb("rest", [P, TPB, heads])
        top_all = sb("top_all", [P, TPB, P], BF16)
        top_pieces = top_all[:, :, 0:3 * heads].rearrange("p t (i h) -> p t i h", i=3)
        top_rows = sb("top_rows", [3 * heads, S], BF16)
        ctx_sb = sb("ctx_sb", [P, subs, S])
        recip = sb("recip", [P, subs, S])
        slot = [cx.enter_context(nc.psum_tensor(f"{tag}slot{i}", [P, 2, S], F32)) for i in range(2)]
        ctx = [cx.enter_context(nc.psum_tensor(f"{tag}ctx{i}", [P, subs, S], F32)) for i in range(2)]
        for_exp, for_dve, emptied = sem(tag + "for_exp"), sem(tag + "for_dve"), sem(tag + "emptied")
        cleared, loaded, vb_ready = sem(tag + "cleared"), sem(tag + "loaded"), sem(tag + "vb_ready")
        top_ready, rows_ready, rows_in = sem(tag + "top_ready"), sem(tag + "rows_ready"), sem(tag + "rows_in")
        probs_ready, probs_used = sem(tag + "probs_ready"), sem(tag + "probs_used")
        ctx_copied, chain = sem(tag + "ctx_copied"), sem(tag + "chain")

        def q_from(kt):
            return kt * P if causal else 0

        def k_to(qt):
            return (qt + 1) * P if causal else S
        with nc.Block() as block:
            @block.sync
            def _(sp):
                def load(b):
                    for i, (qp, kp) in enumerate(pairs):
                        for dst, src, p in ((qs, q_pieces, qp), (ks, k_pieces, kp)):
                            sp.dma_start(dst[i * hd:(i + 1) * hd, :, :],
                                         src[p, :, bass.ds(b * S, S)].rearrange("(h d) t -> d h t", d=hd)).then_inc(loaded, 16)

                def rows(b):
                    sp.wait_ge(rows_ready, b + 1)
                    for i in range(3):
                        sp.dma_start(qs[ROWS + i:ROWS + i + 1, :, :], top_rows[i * heads:(i + 1) * heads, :])\
                            .then_inc(rows_in, 16)
                sp.wait_ge(cleared, 1)
                load(0)
                with sp.Fori(0, B - 1) as b:
                    rows(b)
                    sp.wait_ge(probs_ready, b * EI + EI)
                    load(b + 1)
                rows(B - 1)

            @block.gpsimd
            def _(pool):
                nc.gpsimd.memset(top_all[:], 0.0)
                nc.gpsimd.memset(qs[:], 0.0)
                nc.gpsimd.memset(ks[:], 1.0).then_inc(cleared, 1)
                pool.wait_ge(cleared, 1)
                for i in range(4):
                    nc.gpsimd.memset(pt[:, i, :, :], 0.0).then_inc(probs_used, 1)
                nc.gpsimd.tensor_copy(vb[:], vals[:, 0:TPB, :]).then_inc(vb_ready, 1)
                with pool.Fori(1, B) as b:
                    pool.wait_ge(probs_used, b * EI + 4)
                    nc.gpsimd.tensor_copy(vb[:], vals[:, bass.ds(b * TPB, TPB), :]).then_inc(vb_ready, 1)

            @block.tensor
            def _(pe):
                def slot_is_free(b, n):
                    if n == 0:
                        pe.wait_ge(ctx_copied, b * NC4 + 1)
                    elif n == 1:
                        pe.wait_ge(emptied, b * DI + 1)
                    elif items[n - 2][0] == "exp":
                        pe.wait_ge(probs_ready, b * EI + nth[n - 2] + 1)
                    else:
                        pe.wait_ge(emptied, b * DI + nth[n - 2] + 2)

                def weigh(b, gi):
                    c, s, kt = groups[gi]
                    if (s, kt) == (0, 0) and c == 0:
                        pe.wait_ge(vb_ready, b + 1)
                        pe.wait_ge(ctx_copied, b * NC4 + 1)
                    if (s, kt) == (0, 0) and c == 2:
                        pe.wait_ge(ctx_copied, b * NC4 + 2)
                    lo = q_from(kt)
                    for half in range(2):
                        e = 2 * gi + half
                        pe.wait_ge(probs_ready, b * EI + e + 1)
                        for i in range(2):
                            j = 2 * half + i
                            mm = nc.tensor.matmul(ctx[c % 2][VP * j:VP * j + VP, s, lo:S],
                                                  vb[:, kt, (4 * c + j) * VP:(4 * c + j + 1) * VP],
                                                  pt[:, e % 4, i, lo:S], start=kt == 0, stop=kt == TPB - 1)
                        mm.then_inc(probs_used, 1)
                pe.wait_ge(cleared, 1)
                with pe.Fori(0, B) as b:
                    pe.wait_ge(loaded, b * LOADS + LOADS)
                    pending = None
                    for n, (what, a, z) in enumerate(items):
                        sl = slot[n % 2]
                        slot_is_free(b, n)
                        if what == "max":
                            for i in range(2):
                                hh = 2 * a + i
                                mm = nc.tensor.matmul(sl[:, i, 0:k_to(z)], qs[0:ROWS, hh, z * P:(z + 1) * P],
                                                      ks[0:ROWS, hh, 0:k_to(z)], start=True, stop=not causal)
                                if causal:
                                    mm = nc.tensor.matmul(sl[:, i, z * P:(z + 1) * P], k["identb"][:], k["mask_qk"][:],
                                                          start=False, stop=True)
                            mm.then_inc(for_dve, 1)
                        elif what == "rows":
                            pe.wait_ge(top_ready, b + 1)
                            out = sl[:, 0, :].bitcast(BF16)
                            for qt in range(TPB):
                                mm = nc.tensor.transpose(out[:, qt * P:(qt + 1) * P], top_all[:, qt, :], k["identb"][:])
                            mm.then_inc(for_dve, 1)
                        elif what == "exp":
                            c, s, kt, half = z
                            if a == 0:
                                pe.wait_ge(rows_in, b * 48 + 48)
                            lo = q_from(kt)
                            for i in range(2):
                                hh = (4 * c + 2 * half + i) * subs + s
                                mm = nc.tensor.matmul(sl[:, i, lo:S], ks[:, hh, kt * P:(kt + 1) * P], qs[:, hh, lo:S],
                                                      start=True, stop=not causal)
                                if causal:
                                    mm = nc.tensor.matmul(sl[:, i, lo:lo + P], k["identb"][:], k["mask_kq"][:],
                                                          start=False, stop=True)
                            mm.then_inc(for_exp, 1)
                            if half == 1:
                                if pending is not None:
                                    weigh(b, pending)
                                pending = a // 2
                        else:
                            if a == NC4 - 1:
                                weigh(b, pending)
                            pe.wait_ge(ctx_copied, b * NC4 + a + 2)
                            for s in range(subs):
                                mm = nc.tensor.matmul(sl[:, s, :], k[sel][:], ctx_sb[:, s, :], start=True, stop=True)
                            mm.then_inc(for_dve, 1)

            @block.scalar
            def _(act):
                with act.Fori(0, B) as b:
                    for n, (what, e, z) in enumerate(items):
                        if what == "exp":
                            lo = q_from(z[2])
                            act.wait_ge(for_exp, b * EI + e + 1)
                            act.wait_ge(probs_used, b * EI + e + 1)
                            nc.scalar.activation(pt[:, e % 4, :, lo:S], slot[n % 2][:, :, lo:S], ACT.Exp, scale=scale)\
                                .then_inc(probs_ready, 1)

            @block.vector
            def _(dve):
                dve.wait_ge(cleared, 1)
                nc.vector.memset(ctx_sb[:], 0.0).then_inc(ctx_copied, 1)
                nc.vector.memset(recip[:], 0.0).then_inc(emptied, 1)
                with dve.Fori(0, B) as b:
                    links = 0

                    def linked(ins):
                        nonlocal links
                        links += 1
                        ins.then_inc(chain, 1)
                        dve.wait_ge(chain, b * PER + links)
                    PER = 5 + NC4 * subs
                    for n, (what, a, z) in enumerate(items):
                        if what == "max":
                            dve.wait_ge(for_dve, b * DI + nth[n] + 1)
                            nc.vector.tensor_reduce(top[:, z, 2 * a:2 * a + 2], slot[n % 2][:, :, 0:k_to(z)], axis=AX.X,
                                                    op=ALU.max).then_inc(emptied, 1)
                        elif what == "rows":
                            dve.wait_ge(emptied, b * DI + nth[n] + 1)
                            linked(nc.vector.tensor_scalar(top[:], top[:], -1.0, None, ALU.mult))
                            linked(nc.vector.tensor_copy(top_pieces[:, :, 0, :], top[:]))
                            linked(nc.vector.tensor_tensor(rest[:], top[:], top_pieces[:, :, 0, :], ALU.subtract))
                            linked(nc.vector.tensor_copy(top_pieces[:, :, 1, :], rest[:]))
                            nc.vector.tensor_tensor(top_pieces[:, :, 2, :], rest[:], top_pieces[:, :, 1, :], ALU.subtract)\
                                .then_inc(top_ready, 1)
                            dve.wait_ge(for_dve, b * DI + nth[n] + 1)
                            linked(nc.vector.tensor_copy(top_rows[:], slot[n % 2][0:3 * heads, 0, :].bitcast(BF16)[:, 0:S]))
                            nc.vector.tensor_scalar(rest[:, 0, 0:1], top[:, 0, 0:1], 1.0, None, ALU.mult)\
                                .then_inc(emptied, 1)
                            nc.vector.tensor_scalar(rest[:, 0, 1:2], top[:, 0, 0:1], 1.0, None, ALU.mult)\
                                .then_inc(rows_ready, 1)
                            dve.wait_ge(rows_ready, b + 1)
                        elif what == "norm":
                            gi = max(i for i, g in enumerate(groups) if g[0] == a)
                            dve.wait_ge(probs_used, b * EI + 2 * gi + 2 + 4)
                            nc.vector.tensor_copy(ctx_sb[:], ctx[a % 2][:]).then_inc(ctx_copied, 1)
                            dve.wait_ge(ctx_copied, b * NC4 + a + 2)
                            dve.wait_ge(for_dve, b * DI + nth[n] + 1)
                            nc.vector.reciprocal(recip[:], slot[n % 2][:, 0:subs, :]).then_inc(emptied, 1)
                            dve.wait_ge(emptied, b * DI + nth[n] + 2)
                            out = yT[:, a, bass.ds(b * S, S)]
                            if subs == 1:
                                linked(nc.vector.tensor_tensor(out, ctx_sb[:, 0, :], recip[:, 0, :], ALU.mult))
                            else:
                                linked(nc.vector.tensor_tensor(recip[:], ctx_sb[:], recip[:], ALU.mult))
                                linked(nc.vector.scalar_tensor_tensor(out=out, in0=recip[:, 1, :],
                                                                      scalar=neg_lambda[:], in1=recip[:, 0, :],
                                                                      op0=ALU.mult, op1=ALU.add))


def attention_lambda(nc, sem, d, neg_lambda, init):
    W = C // NH // 2
    with ExitStack() as cx:
        vecs = cx.enter_context(nc.sbuf_tensor("la_vecs", [P, 4, W], F32))
        prod = cx.enter_context(nc.sbuf_tensor("la_prod", [P, 2, W], F32))
        dots = cx.enter_context(nc.sbuf_tensor("la_dots", [P, 2], F32))
        exps = cx.enter_context(nc.sbuf_tensor("la_exps", [P, 2], F32))
        diff = cx.enter_context(nc.sbuf_tensor("la_diff", [P, 1], F32))
        vecs_in, chain, dots_ready, exps_ready = sem("la_vecs_in"), sem("la_chain"), sem("la_dots_ready"), sem("la_exps_ready")
        with nc.Block() as block:
            @block.sync
            def _(sp):
                for i in range(4):
                    sp.dma_start(vecs[:, i, :], d["lambdas"][i, :].partition_broadcast(P)).then_inc(vecs_in, 16)

            @block.scalar
            def _(act):
                act.wait_ge(dots_ready, 1)
                nc.scalar.activation(exps[:], dots[:], ACT.Exp).then_inc(exps_ready, 1)

            @block.vector
            def _(dve):
                n = [0]
                dve.wait_ge(vecs_in, 64)
                link(dve, chain, n, nc.vector.tensor_tensor(prod[:], vecs[:, 0:2, :], vecs[:, 2:4, :], ALU.mult))
                nc.vector.tensor_reduce(dots[:], prod[:], axis=AX.X, op=ALU.add).then_inc(dots_ready, 1)
                dve.wait_ge(exps_ready, 1)
                link(dve, chain, n, nc.vector.tensor_tensor(diff[:], exps[:, 1:2], exps[:, 0:1], ALU.subtract))
                nc.vector.tensor_scalar(neg_lambda[:], diff[:], -init, None, ALU.add)


def head_rms(nc, k, sem, d, yT, factor):
    with ExitStack() as cx:
        def sb(name, shape, dt=F32):
            return cx.enter_context(nc.sbuf_tensor("hr_" + name, shape, dt))
        weight = sb("weight", [P, 1])
        eps = sb("eps", [P, 1])
        square = sb("square", [P, 2, S])
        root = sb("root", [P, 2, S])
        recip = sb("recip", [P, 2, S])
        slot = [cx.enter_context(nc.psum_tensor(f"hr_slot{i}", [P, S], F32)) for i in range(2)]
        weight_in, cleared, weight_ready = sem("hr_weight_in"), sem("hr_cleared"), sem("hr_weight_ready")
        square_ready, mean_ready, root_ready, chain = (sem("hr_" + x) for x in (
            "square_ready", "mean_ready", "root_ready", "chain"))
        items = [(c, b) for c in range(NC4) for b in range(B)]
        with nc.Block() as block:
            @block.sync
            def _(sp):
                sp.wait_ge(cleared, 1)
                for j in range(4):
                    sp.dma_start(weight[VP * j:VP * j + HD, :], d["subln"]).then_inc(weight_in, 16)

            @block.vector
            def _(dve):
                n_links = [0]
                nc.vector.memset(eps[:], EPS)
                nc.vector.memset(weight[:], 0.0).then_inc(cleared, 1)
                dve.wait_ge(weight_in, 64)
                link(dve, chain, n_links, nc.vector.tensor_scalar(weight[:], weight[:], factor, None, ALU.mult))

                def finish(n):
                    c, b = items[n]
                    part = yT[:, c, b * S:(b + 1) * S]
                    dve.wait_ge(root_ready, n + 1)
                    link(dve, chain, n_links, nc.vector.reciprocal(recip[:, n % 2, :], root[:, n % 2, :]))
                    nc.vector.scalar_tensor_tensor(out=part, in0=part, scalar=weight[:], in1=recip[:, n % 2, :],
                                                   op0=ALU.mult, op1=ALU.mult)
                for n, (c, b) in enumerate(items):
                    part = yT[:, c, b * S:(b + 1) * S]
                    if n >= 2:
                        dve.wait_ge(mean_ready, n - 1)
                    nc.vector.tensor_tensor(square[:, n % 2, :], part, part, ALU.mult).then_inc(square_ready, 1)
                    if n >= 1:
                        finish(n - 1)
                finish(len(items) - 1)

            @block.tensor
            def _(pe):
                for n in range(len(items)):
                    pe.wait_ge(square_ready, n + 1)
                    if n >= 2:
                        pe.wait_ge(root_ready, n - 1)
                    nc.tensor.matmul(slot[n % 2][:], k["sel_mean"][:], square[:, n % 2, :], start=True, stop=True)\
                        .then_inc(mean_ready, 1)

            @block.scalar
            def _(act):
                act.wait_ge(cleared, 1)
                for n in range(len(items)):
                    act.wait_ge(mean_ready, n + 1)
                    if n >= 2:
                        act.wait_ge(square_ready, n + 1)
                    nc.scalar.activation(root[:, n % 2, :], slot[n % 2][:], ACT.Sqrt, bias=eps[:]).then_inc(root_ready, 1)


def project_out(nc, k, sem, tag, d, yT, resid, out):
    with ExitStack() as cx:
        def sb(name, shape, dt=F32):
            return cx.enter_context(nc.sbuf_tensor(tag + name, shape, dt))
        wo = sb("wo", [P, NC4, C])
        bo = sb("bo", [P, C])
        base = sb("base", [P, NT, C])
        slot = [cx.enter_context(nc.psum_tensor(f"{tag}slot{i}", [P, 512], F32)) for i in range(2)]
        cleared, bias_in, weights_in, based = sem(tag + "cleared"), sem(tag + "bias_in"), sem(tag + "weights_in"), sem(tag + "based")
        projected, added = sem(tag + "projected"), sem(tag + "added")
        with nc.Block() as block:
            @block.sync
            def _(sp):
                sp.dma_start(bo[:], d["bo"].partition_broadcast(P)).then_inc(bias_in, 16)
                sp.wait_ge(cleared, 1)
                for j in range(4):
                    sp.dma_start(wo[VP * j:VP * j + HD, :, :], d["Wo"].rearrange("(c j e) n -> j e c n", j=4, e=HD)[j])\
                        .then_inc(weights_in, 16)

            @block.gpsimd
            def _(pool):
                nc.gpsimd.memset(wo[:], 0.0).then_inc(cleared, 1)

            @block.vector
            def _(dve):
                dve.wait_ge(bias_in, 16)
                nc.vector.tensor_tensor(base[:], resid[:], bo[:].unsqueeze(1).to_broadcast([P, NT, C]), ALU.add)\
                    .then_inc(based, 1)
                dve.wait_ge(based, 1)
                for t in range(NT):
                    dve.wait_ge(projected, t + 1)
                    nc.vector.tensor_tensor(out[:, t, :], slot[t % 2][:, 0:C], base[:, t, :], ALU.add).then_inc(added, 1)

            @block.tensor
            def _(pe):
                pe.wait_ge(weights_in, 64)
                for t in range(NT):
                    if t >= 2:
                        pe.wait_ge(added, t - 1)
                    for c in range(NC4):
                        mm = nc.tensor.matmul(slot[t % 2][:, 0:C], yT[:, c, t * P:(t + 1) * P], wo[:, c, :],
                                              start=c == 0, stop=c == NC4 - 1)
                    mm.then_inc(projected, 1)


def route(nc, k, sem, tag, d, x, xT, E, K, capacity, tiles, slot_put, slot_get, weight, comb, tile_expert, rows_in, zero_tiles):
    G = K if capacity else 1
    NE = NT * E
    with ExitStack() as cx:
        def sb(name, shape, dt=F32):
            return cx.enter_context(nc.sbuf_tensor(tag + name, shape, dt))
        wg = sb("wg", [HC, 2, E])
        bg = sb("bg", [P, E])
        zeros = sb("zeros", [P, zero_tiles, C])
        io_e = sb("io_e", [P, E])
        io_128 = sb("io_128", [P, NT])
        io_tile = sb("io_tile", [P, tiles])
        logit = sb("logit", [P, NT, E])
        best = sb("best", [P, K, NT])
        same = sb("same", [P, NT, E])
        key = sb("key", [P, NT, E])
        least = sb("least", [P, NT])
        hot = sb("hot", [P, K, NT, E])
        counted = sb("counted", [P, G, NT, E])
        tot = sb("tot", [P, G, NT, E])
        run = [sb(f"run{i}", [P, G, NT, E]) for i in range(2)]
        rank = sb("rank", [P, G, NT, E])
        prod = sb("prod", [P, K, NT, E])
        prod2 = sb("prod2", [P, K, NT, E])
        over = sb("over", [P, E, NT])
        padded = sb("padded", [P, E])
        end = [sb(f"end{i}", [P, E]) for i in range(2)]
        start = sb("start", [P, E])
        past = sb("past", [P, tiles, E])
        tile_f = sb("tile_f", [P, tiles])
        rank_k = sb("rank_k", [P, K, NT])
        slot_k = sb("slot_k", [P, K, NT])
        valid = sb("valid", [P, K, NT])
        put_f = sb("put_f", [P, K, NT])
        gap = sb("gap", [P, K, NT])
        expo = sb("expo", [P, K, NT])
        sumexp = sb("sumexp", [P, NT])
        inv = sb("inv", [P, NT])
        acc_logit = cx.enter_context(nc.psum_tensor(tag + "acc_logit", [P, 512], F32))
        acc_before = cx.enter_context(nc.psum_tensor(tag + "acc_before", [P, 512], F32))
        acc_total = cx.enter_context(nc.psum_tensor(tag + "acc_total", [P, 512], F32))
        loads, iotas, zeroed, filled = sem(tag + "loads"), sem(tag + "iotas"), sem(tag + "zeroed"), sem(tag + "filled")
        logits_ready, chain, counted_ready, counts_ready, gap_ready, expo_ready = (sem(tag + x) for x in (
            "logits_ready", "chain", "counted_ready", "counts_ready", "gap_ready", "expo_ready"))
        with nc.Block() as block:
            @block.sync
            def _(sp):
                sp.dma_start(wg[:], d["wg"]).then_inc(loads, 16)
                if "bg" in d:
                    sp.dma_start(bg[:], d["bg"].partition_broadcast(P)).then_inc(loads, 16)
                sp.wait_ge(zeroed, 1)
                for i in range(tiles // zero_tiles):
                    part = rows_in[i * zero_tiles * P:(i + 1) * zero_tiles * P, :]
                    sp.dma_start(part.rearrange("(a p) c -> p a c", p=P), zeros[:]).then_inc(filled, 16)
                sp.wait_ge(filled, 16 * (tiles // zero_tiles))

            @block.gpsimd
            def _(pool):
                nc.gpsimd.memset(zeros[:], 0.0).then_inc(zeroed, 1)
                nc.gpsimd.iota(io_e[:], pattern=[[1, E]], base=0, channel_multiplier=0, allow_small_or_imprecise_dtypes=True)
                nc.gpsimd.iota(io_128[:], pattern=[[P, NT]], base=0, channel_multiplier=0,
                               allow_small_or_imprecise_dtypes=True)
                nc.gpsimd.iota(io_tile[:], pattern=[[P, tiles]], base=0, channel_multiplier=0,
                               allow_small_or_imprecise_dtypes=True).then_inc(iotas, 1)

            @block.tensor
            def _(pe):
                pe.wait_ge(loads, 32 if "bg" in d else 16)
                for t in range(NT):
                    for c in range(2):
                        mm = nc.tensor.matmul(acc_logit[:, t * E:(t + 1) * E], xT[0:HC, c, t * P:(t + 1) * P], wg[:, c, :],
                                              start=c == 0, stop=c == 1)
                mm.then_inc(logits_ready, 1)
                pe.wait_ge(counted_ready, 1)
                cols = counted[:].rearrange("p g t e -> p (g t e)")
                nc.tensor.matmul(acc_before[:, 0:G * NE], k["before"][:], cols, start=True, stop=True)
                nc.tensor.matmul(acc_total[:, 0:G * NE], k["ones"][:], cols, start=True, stop=True).then_inc(counts_ready, 1)

            @block.scalar
            def _(act):
                act.wait_ge(gap_ready, 1)
                nc.scalar.activation(expo[:], gap[:], ACT.Exp).then_inc(expo_ready, 1)

            @block.vector
            def _(dve):
                n = [0]
                V = nc.vector

                def do(ins):
                    link(dve, chain, n, ins)
                whole = [P, NT, E]

                def over_e(a):
                    return a.unsqueeze(2).to_broadcast(whole)
                dve.wait_ge(iotas, 1)
                dve.wait_ge(logits_ready, 1)
                psum = acc_logit[:, 0:NE].rearrange("p (t e) -> p t e", e=E)
                if "bg" in d:
                    do(V.tensor_tensor(logit[:], psum, bg[:].unsqueeze(1).to_broadcast(whole), ALU.add))
                else:
                    do(V.tensor_copy(logit[:], psum))
                for j in range(K):
                    do(V.tensor_reduce(best[:, j, :], logit[:], axis=AX.X, op=ALU.max))
                    do(V.tensor_tensor(same[:], logit[:], over_e(best[:, j, :]), ALU.is_equal))
                    do(V.scalar_tensor_tensor(out=key[:], in0=same[:], scalar=-64.0,
                                              in1=io_e[:].unsqueeze(1).to_broadcast(whole), op0=ALU.mult, op1=ALU.add))
                    do(V.tensor_reduce(least[:], key[:], axis=AX.X, op=ALU.min))
                    do(V.tensor_tensor(hot[:, j], key[:], over_e(least[:]), ALU.is_equal))
                    if j < K - 1:
                        do(V.scalar_tensor_tensor(out=logit[:], in0=hot[:, j], scalar=-3e38, in1=logit[:],
                                                  op0=ALU.mult, op1=ALU.add))
                if capacity:
                    V.tensor_copy(counted[:], hot[:]).then_inc(counted_ready, 1)
                else:
                    do(V.tensor_tensor(same[:], hot[:, 0], hot[:, 1], ALU.add))
                    do(V.tensor_tensor(key[:], hot[:, 2], hot[:, 3], ALU.add))
                    V.tensor_tensor(counted[:, 0], same[:], key[:], ALU.add).then_inc(counted_ready, 1)
                for j in range(K):
                    last = V.tensor_tensor(gap[:, j], best[:, j], best[:, 0], ALU.subtract)
                last.then_inc(gap_ready, 1)
                dve.wait_ge(expo_ready, 1)
                do(V.tensor_reduce(sumexp[:], expo[:].rearrange("p k t -> p t k"), axis=AX.X, op=ALU.add))
                do(V.reciprocal(inv[:], sumexp[:]))
                do(V.tensor_tensor(weight[:], expo[:], inv[:].unsqueeze(1).to_broadcast([P, K, NT]), ALU.mult))
                dve.wait_ge(counts_ready, 1)
                grid = "p (g t e) -> p g t e"
                do(V.tensor_copy(tot[:], acc_total[:, 0:G * NE].rearrange(grid, g=G, t=NT)))
                do(V.tensor_copy(run[0][:], tot[:]))
                a, b = run
                for s in (1, 2, 4, 8):
                    do(V.tensor_copy(b[:, :, 0:s, :], a[:, :, 0:s, :]))
                    do(V.tensor_tensor(b[:, :, s:NT, :], a[:, :, s:NT, :], a[:, :, 0:NT - s, :], ALU.add))
                    a, b = b, a
                do(V.tensor_tensor(rank[:], a[:], tot[:], ALU.subtract))
                do(V.tensor_tensor(rank[:], rank[:], acc_before[:, 0:G * NE].rearrange(grid, g=G, t=NT), ALU.add))
                if capacity:
                    do(V.tensor_tensor(rank[:, 1], rank[:, 1], a[:, 0, NT - 1, :].unsqueeze(1).to_broadcast(whole), ALU.add))
                    do(V.tensor_scalar(start[:], io_e[:], float(capacity), None, ALU.mult))
                    do(V.tensor_scalar(end[0][:], start[:], float(capacity), None, ALU.add))
                    last_end = end[0]
                else:
                    count = a[:, 0, NT - 1, :].unsqueeze(2).to_broadcast([P, E, NT])
                    do(V.tensor_tensor(over[:], count, io_128[:].unsqueeze(1).to_broadcast([P, E, NT]), ALU.is_gt))
                    do(V.tensor_reduce(padded[:], over[:], axis=AX.X, op=ALU.add))
                    do(V.tensor_scalar(padded[:], padded[:], float(P), None, ALU.mult))
                    do(V.tensor_copy(end[0][:], padded[:]))
                    u, v = end
                    for s in (1, 2, 4, 8):
                        do(V.tensor_copy(v[:, 0:s], u[:, 0:s]))
                        do(V.tensor_tensor(v[:, s:E], u[:, s:E], u[:, 0:E - s], ALU.add))
                        u, v = v, u
                    last_end = u
                    do(V.tensor_tensor(start[:], last_end[:], padded[:], ALU.subtract))
                do(V.tensor_tensor(past[:], last_end[:].unsqueeze(1).to_broadcast([P, tiles, E]),
                                   io_tile[:].unsqueeze(2).to_broadcast([P, tiles, E]), ALU.is_le))
                do(V.tensor_reduce(tile_f[:], past[:], axis=AX.X, op=ALU.add))
                do(V.tensor_scalar(tile_f[:], tile_f[:], float(E - 1), None, ALU.min))
                do(V.tensor_copy(tile_expert[:], tile_f[:]))
                for j in range(K):
                    g = j if capacity else 0
                    do(V.tensor_tensor(prod[:, j], hot[:, j], rank[:, g], ALU.mult))
                    do(V.tensor_tensor(prod2[:, j], hot[:, j], start[:].unsqueeze(1).to_broadcast(whole), ALU.mult))
                do(V.tensor_reduce(rank_k[:], prod[:], axis=AX.X, op=ALU.add))
                do(V.tensor_reduce(slot_k[:], prod2[:], axis=AX.X, op=ALU.add))
                do(V.tensor_tensor(slot_k[:], slot_k[:], rank_k[:], ALU.add))
                if capacity:
                    do(V.tensor_scalar(valid[:], rank_k[:], float(capacity), None, ALU.is_lt))
                    do(V.tensor_tensor(weight[:], weight[:], valid[:], ALU.mult))
                    do(V.tensor_scalar(put_f[:], valid[:], float(-tiles * P), float(tiles * P), ALU.mult, ALU.add))
                    do(V.tensor_tensor(put_f[:], put_f[:], slot_k[:], ALU.add))
                    do(V.tensor_tensor(slot_k[:], slot_k[:], valid[:], ALU.mult))
                    do(V.tensor_copy(slot_put[:], put_f[:]))
                else:
                    do(V.tensor_copy(slot_put[:], slot_k[:]))
                do(V.tensor_copy(slot_get[:], slot_k[:]))
                do(V.tensor_tensor(comb[:], hot[:, 0], over_e(weight[:, 0]), ALU.mult))
                for j in range(1, K):
                    do(V.tensor_tensor(prod[:, j], hot[:, j], over_e(weight[:, j]), ALU.mult))
                    do(V.tensor_tensor(comb[:], comb[:], prod[:, j], ALU.add))


def dispatch(nc, sem, tag, x, K, slot_put, rows_in, total):
    sent = sem(tag + "sent")
    with nc.Block() as block:
        @block.gpsimd
        def _(pool):
            for t in range(NT):
                for j in range(K):
                    pool.indirect_dma_start(out=rows_in, out_offset=bass.IndirectOffsetOnAxis(ap=slot_put[:, j, t:t + 1], axis=0),
                                            in_=x[:, t, :], in_offset=None, bounds_check=total - 1, oob_is_err=False)\
                        .then_inc(sent, 16)
            pool.wait_ge(sent, 16 * NT * K)


def experts(nc, k, sem, tag, d, E, F, A, swiglu, tiles, tile_expert, rows_in, rows_out):
    AC = A // P
    FH = F // 2
    LIMIT, ALPHA = 7.0, 1.702
    with ExitStack() as cx:
        def sb(name, shape, dt=F32):
            return cx.enter_context(nc.sbuf_tensor(tag + name, shape, dt))

        def ps(name, shape, dt=F32):
            return cx.enter_context(nc.psum_tensor(tag + name, shape, dt))
        w1 = sb("w1", [HC + 1, E, 2, F])
        w2 = sb("w2", [P, E, AC, C])
        w1_flat = w1[:].rearrange("p e c f -> p (e c f)")
        w2_flat = w2[:].rearrange("p e c f -> p (e c f)")
        xr = sb("xr", [P, 2, C])
        xrT = sb("xrT", [HC + 1, 2, 2, P])
        act_sb = sb("act_sb", [P, 2, A])
        glu = sb("glu", [P, 2, A]) if swiglu else None
        lin = sb("lin", [P, 2, A]) if swiglu else None
        gate = sb("gate", [P, 2, A]) if swiglu else None
        actT = sb("actT", [P, 2, AC, P])
        y = sb("y", [P, 2, C])
        xt_ps = ps("xt_ps", [P, 512])
        hid = [ps(f"hid{i}", [P, 2, 512]) for i in range(2)]
        at_ps = ps("at_ps", [P, AC * P if AC * P > 512 else 512])
        y_ps = ps("y_ps", [P, 512])
        weights_in, ones_set, row_in = sem(tag + "weights_in"), sem(tag + "ones_set"), [sem(f"{tag}row_in{i}") for i in range(2)]
        x_turned, x_moved, hid_ready, glu_ready, gate_ready, act_ready = (sem(tag + x) for x in (
            "x_turned", "x_moved", "hid_ready", "glu_ready", "gate_ready", "act_ready"))
        lin_ready, mix_ready, a_turned, a_moved, y_ready, y_moved = (sem(tag + x) for x in (
            "lin_ready", "mix_ready", "a_turned", "a_moved", "y_ready", "y_moved"))
        sent = [sem(f"{tag}sent{i}") for i in range(2)]

        def ge(eng, s, value):
            if not isinstance(value, int) or value > 0:
                eng.wait_ge(s, value)

        def steady(eng, body):
            body(1, 1)
            body(2, 0)
            with eng.Fori(1, (tiles - 2) // 2) as p:
                body(2 * p + 1, 1)
                body(2 * p + 2, 0)
        with nc.Block() as block:
            @block.sync
            def _(sp):
                for e in range(E):
                    sp.dma_start(w1[:, e, :, :], d["w1"][e]).then_inc(weights_in, 16)
                    sp.dma_start(w2[:, e, :, :], d["w2"][e]).then_inc(weights_in, 16)

                def load(i, par):
                    ge(sp, x_turned, i - 1)
                    sp.dma_start(xr[:, par, :], rows_in[bass.ds(i * P, P), :]).then_inc(row_in[par], 16)

                def store(i, par):
                    sp.wait_ge(y_moved, i + 1)
                    sp.dma_start(rows_out[bass.ds(i * P, P), :], y[:, par, :]).then_inc(sent[par], 16)
                for i in range(4):
                    load(i, i % 2)
                with sp.Fori(2, tiles // 2) as p:
                    load(2 * p, 0)
                    store(2 * p - 4, 0)
                    load(2 * p + 1, 1)
                    store(2 * p - 3, 1)
                for i in range(tiles - 4, tiles):
                    store(i, i % 2)
                for par in range(2):
                    sp.wait_ge(sent[par], 16 * (tiles // 2))

            @block.gpsimd
            def _(pool):
                nc.gpsimd.memset(xrT[HC:HC + 1, :, :, :], 1.0).then_inc(ones_set, 1)

            @block.tensor
            def _(pe):
                def turn_x(i, par, half):
                    pe.wait_ge(row_in[par], 16 * (half + 1))
                    ge(pe, x_moved, i)
                    for c in range(2):
                        mm = nc.tensor.transpose(xt_ps[0:HC, c * P:(c + 1) * P], xr[:, par, c * HC:(c + 1) * HC],
                                                 k["ident"][:])
                    mm.then_inc(x_turned, 1)

                def turn_a(i, par):
                    pe.wait_ge(act_ready, i + 1)
                    ge(pe, a_moved, i)
                    for c in range(AC):
                        mm = nc.tensor.transpose(at_ps[:, c * P:(c + 1) * P], act_sb[:, par, c * P:(c + 1) * P],
                                                 k["ident"][:])
                    mm.then_inc(a_turned, 1)

                def layer1(i, par, e):
                    pe.wait_ge(x_moved, i + 1)
                    ge(pe, act_ready, i - 1)
                    for c in range(2):
                        for o in range(2):
                            rows = HC + c
                            mm = nc.tensor.matmul(hid[par][:, o, 0:FH], xrT[0:rows, par, c, :],
                                                  w1_flat[0:rows, bass.ds(e * (2 * F) + c * F + o * FH, FH)],
                                                  start=c == 0, stop=c == 1)
                    mm.then_inc(hid_ready, 1)

                def layer2(i, par, e):
                    pe.wait_ge(a_moved, i + 1)
                    ge(pe, y_moved, i)
                    for c in range(AC):
                        mm = nc.tensor.matmul(y_ps[:, 0:C], actT[:, par, c, :], w2_flat[:, bass.ds(e * (AC * C) + c * C, C)],
                                              start=c == 0, stop=c == AC - 1)
                    mm.then_inc(y_ready, 1)

                def expert(i):
                    return pe.value_load(tile_expert[0:1, bass.ds(i, 1)], min_val=0, max_val=E - 1)
                pe.wait_ge(ones_set, 1)
                pe.wait_ge(weights_in, 32 * E)
                turn_x(0, 0, 0)
                turn_x(1, 1, 0)
                layer1(0, 0, expert(0))

                def body(i, par, half):
                    turn_x(i + 1, 1 - par, half)
                    turn_a(i - 1, 1 - par)
                    layer1(i, par, expert(i))
                    layer2(i - 1, 1 - par, expert(i - 1))
                body(1, 1, 1)
                body(2, 0, 1)
                with pe.Fori(1, (tiles - 2) // 2) as p:
                    body(2 * p + 1, 1, p + 1)
                    body(2 * p + 2, 0, p + 1)
                last = tiles - 1
                turn_a(last - 1, 0)
                layer1(last, 1, expert(last))
                layer2(last - 1, 0, expert(last - 1))
                turn_a(last, 1)
                layer2(last, 1, expert(last))

            @block.vector
            def _(dve):
                def move_x(i, par):
                    dve.wait_ge(x_turned, i + 1)
                    ge(dve, hid_ready, i - 1)
                    nc.vector.tensor_copy(xrT[0:HC, par, :, :], xt_ps[0:HC, 0:2 * P].rearrange("p (c t) -> p c t", c=2))\
                        .then_inc(x_moved, 1)

                def move_a(i, par):
                    dve.wait_ge(a_turned, i + 1)
                    ge(dve, y_ready, i - 1)
                    nc.vector.tensor_copy(actT[:, par, :, :], at_ps[:, 0:AC * P].rearrange("p (c t) -> p c t", c=AC))\
                        .then_inc(a_moved, 1)

                def activate(i, par):
                    if not swiglu:
                        return
                    dve.wait_ge(hid_ready, i + 1)
                    ge(dve, act_ready, i - 1)
                    nc.vector.tensor_scalar(glu[:, par, :], hid[par][:, 0, 0:A], LIMIT, None, ALU.min).then_inc(glu_ready, 1)
                    nc.vector.tensor_scalar(lin[:, par, :], hid[par][:, 1, 0:A], LIMIT, -LIMIT, ALU.min, ALU.max)\
                        .then_inc(lin_ready, 1)
                    dve.wait_ge(lin_ready, i + 1)
                    dve.wait_ge(glu_ready, i + 1)
                    nc.vector.scalar_tensor_tensor(out=lin[:, par, :], in0=lin[:, par, :], scalar=1.0, in1=glu[:, par, :],
                                                   op0=ALU.add, op1=ALU.mult).then_inc(mix_ready, 1)
                    dve.wait_ge(mix_ready, i + 1)
                    dve.wait_ge(gate_ready, i + 1)
                    ge(dve, a_turned, i - 1)
                    nc.vector.tensor_tensor(act_sb[:, par, :], lin[:, par, :], gate[:, par, :], ALU.mult).then_inc(act_ready, 1)
                move_x(0, 0)
                move_x(1, 1)
                activate(0, 0)

                def body(i, par):
                    move_x(i + 1, 1 - par)
                    move_a(i - 1, 1 - par)
                    activate(i, par)
                steady(dve, body)
                last = tiles - 1
                move_a(last - 1, 0)
                activate(last, 1)
                move_a(last, 1)

            @block.scalar
            def _(act):
                def activate(i, par):
                    if swiglu:
                        act.wait_ge(glu_ready, i + 1)
                        ge(act, act_ready, i - 1)
                        nc.scalar.activation(gate[:, par, :], glu[:, par, :], ACT.Sigmoid, scale=ALPHA).then_inc(gate_ready, 1)
                    else:
                        act.wait_ge(hid_ready, i + 1)
                        ge(act, a_turned, i - 1)
                        nc.scalar.activation(act_sb[:, par, :].rearrange("p (o f) -> p o f", o=2), hid[par][:, :, 0:FH],
                                             ACT.Gelu).then_inc(act_ready, 1)

                def move_y(i, par, half):
                    act.wait_ge(y_ready, i + 1)
                    if not isinstance(half, int) or half > 0:
                        act.wait_ge(sent[par], 16 * half)
                    nc.scalar.activation(y[:, par, :], y_ps[:, 0:C], ACT.Copy).then_inc(y_moved, 1)
                activate(0, 0)
                activate(1, 1)
                move_y(0, 0, 0)
                activate(2, 0)
                move_y(1, 1, 0)
                with act.Fori(1, (tiles - 2) // 2) as p:
                    activate(2 * p + 1, 1)
                    move_y(2 * p, 0, p)
                    activate(2 * p + 2, 0)
                    move_y(2 * p + 1, 1, p)
                last = tiles - 1
                activate(last, 1)
                move_y(last - 1, 0, (last - 1) // 2)
                move_y(last, 1, last // 2)


def combine(nc, k, sem, tag, d, E, K, slot_get, weight, comb, rows_out, first, second, out):
    R = 8
    with ExitStack() as cx:
        def sb(name, shape, dt=F32):
            return cx.enter_context(nc.sbuf_tensor(tag + name, shape, dt))
        b2 = sb("b2", [E, C])
        combT = sb("combT", [E, NT, P])
        base = sb("base", [P, NT, C])
        acc = sb("acc", [P, 2, C])
        got = sb("got", [P, R, C])
        turned_ps = cx.enter_context(nc.psum_tensor(tag + "turned_ps", [P, 2, 512], F32))
        bias_ps = cx.enter_context(nc.psum_tensor(tag + "bias_ps", [P, 2, 512], F32))
        b2_in, turned, moved, biased, added, chain = (sem(tag + x) for x in (
            "b2_in", "turned", "moved", "biased", "added", "chain"))
        gathered = [sem(f"{tag}gathered{i}") for i in range(R)]
        used = sem(tag + "used")
        with nc.Block() as block:
            @block.sync
            def _(sp):
                sp.dma_start(b2[:], d["b2"]).then_inc(b2_in, 16)

            @block.gpsimd
            def _(pool):
                for t in range(NT):
                    for j in range(K):
                        n = t * K + j
                        if n >= R:
                            pool.wait_ge(used, n - R + 1)
                        pool.indirect_dma_start(out=got[:, n % R, :], out_offset=None, in_=rows_out,
                                                in_offset=bass.IndirectOffsetOnAxis(ap=slot_get[:, j, t:t + 1], axis=0))\
                            .then_inc(gathered[n % R], 16)

            @block.tensor
            def _(pe):
                pe.wait_ge(b2_in, 16)
                for t in range(NT):
                    if t >= 2:
                        pe.wait_ge(moved, t - 1)
                    nc.tensor.transpose(turned_ps[0:E, t % 2, 0:P], comb[:, t, :], k["ident"][:]).then_inc(turned, 1)
                for t in range(NT):
                    pe.wait_ge(moved, t + 1)
                    if t >= 2:
                        pe.wait_ge(added, t - 1)
                    nc.tensor.matmul(bias_ps[:, t % 2, 0:C], combT[:, t, :], b2[:], start=True, stop=True).then_inc(biased, 1)

            @block.scalar
            def _(act):
                for t in range(NT):
                    act.wait_ge(turned, t + 1)
                    nc.scalar.activation(combT[:, t, :], turned_ps[0:E, t % 2, 0:P], ACT.Copy).then_inc(moved, 1)

            @block.vector
            def _(dve):
                n_links = [0]
                link(dve, chain, n_links, nc.vector.tensor_tensor(base[:], first[:], second[:], ALU.add))
                for t in range(NT):
                    dve.wait_ge(biased, t + 1)
                    nc.vector.tensor_tensor(base[:, t, :], bias_ps[:, t % 2, 0:C], base[:, t, :], ALU.add).then_inc(added, 1)
                    dve.wait_ge(added, t + 1)
                    prev = base[:, t, :]
                    for j in range(K):
                        n = t * K + j
                        dst = out[:, t, :] if j == K - 1 else acc[:, j % 2, :]
                        dve.wait_ge(gathered[n % R], 16 * (n // R + 1))
                        nc.vector.scalar_tensor_tensor(out=dst, in0=got[:, n % R, :], scalar=weight[:, j, t:t + 1], in1=prev,
                                                       op0=ALU.mult, op1=ALU.add).then_inc(used, 1)
                        dve.wait_ge(used, n + 1)
                        prev = dst


def mixture_of_experts(nc, k, sem, tag, d, scope, prepare, E, K, F, A, swiglu, capacity, tiles, first, second, out):
    total = tiles * P
    rows_in = nc.dram_tensor(tag + "rows_in", (total, C), F32, kind="Internal").ap()
    rows_out = nc.dram_tensor(tag + "rows_out", (total, C), F32, kind="Internal").ap()
    with scope() as tables:
        slot_put = tables.sb(tag + "slot_put", [P, K, NT], U32)
        slot_get = tables.sb(tag + "slot_get", [P, K, NT], U32)
        weight = tables.sb(tag + "weight", [P, K, NT])
        comb = tables.sb(tag + "comb", [P, NT, E])
        tile_expert = tables.sb(tag + "tile_expert", [P, tiles], I32)
        with scope() as tokens:
            x = tokens.sb(tag + "x", [P, NT, C])
            with scope() as turned:
                xT = turned.sb(tag + "xT", [HC, 2, N])
                prepare(x, xT)
                route(nc, k, sem, tag + "r_", d, x, xT, E, K, capacity, tiles, slot_put, slot_get, weight, comb,
                      tile_expert, rows_in, 10)
            dispatch(nc, sem, tag + "d_", x, K, slot_put, rows_in, total)
        experts(nc, k, sem, tag + "e_", d, E, F, A, swiglu, tiles, tile_expert, rows_in, rows_out)
        combine(nc, k, sem, tag + "c_", d, E, K, slot_get, weight, comb, rows_out, first, second, out)


def finish_program(nc, sem, h, out):
    sent = sem("result_sent")
    with nc.Block() as block:
        @block.sync
        def _(sp):
            sp.dma_start(out.rearrange("(t p) c -> p t c", p=P), h[:]).then_inc(sent, 16)
            sp.wait_ge(sent, 16)


def tower(nc, d, out):
    with ExitStack() as cx:
        def sb(name, shape, dt=F32):
            return cx.enter_context(nc.sbuf_tensor(name, shape, dt))

        held = []

        def sem(name):
            held.append(nc.alloc_semaphore(name=name))
            return held[-1]

        def clear_semaphores():
            nc.clear_and_free_semaphores(list(held))
            held.clear()
            nc.all_engine_barrier()
        k = build_constants(nc, cx, sb, sem)
        h = sb("h", [P, NT, C])
        q_pieces = nc.dram_tensor("q_pieces", (3, C, N), BF16, kind="Internal").ap()
        k_pieces = nc.dram_tensor("k_pieces", (3, C, N), BF16, kind="Internal").ap()

        def scope():
            stack = ExitStack()
            stack.sb = lambda name, shape, dt=F32: stack.enter_context(nc.sbuf_tensor(name, shape, dt))
            return stack
        def mixture_keyed_attention():
            with scope() as attn:
                vals = attn.sb("vals0", [P, NT, VW])
                with scope() as mix:
                    keys = mix.sb("keys", [P, 3, N // 2])
                    tab = mix.sb("tab", [P, 3, 2, C])
                    with scope() as norm:
                        x, xT = norm.sb("x0", [P, NT, C]), norm.sb("xT0", [HC, 2, N])
                        normalise(nc, k, sem, "n0_", h, x, xT)
                        project_qkv(nc, k, sem, "p0_", d["mix"], xT, q_pieces, k_pieces, vals, keys=keys)
                    mixture_tables(nc, sem, d, tab)
                    mixture_keys(nc, k, sem, tab, keys, k_pieces)
                yT = attn.sb("yT0", [P, NC4, N])
                attend(nc, k, sem, "a0_", q_pieces, k_pieces, vals, yT, NH, 1.0, sel="sel_sum_mix")
                project_out(nc, k, sem, "o0_", d["mix"], yT, h, h)
        def pre_norm_block():
            with scope() as ffn:
                x2 = ffn.sb("x2", [P, NT, C])
                with scope() as attn:
                    x1 = attn.sb("x1", [P, NT, C])
                    vals = attn.sb("vals1", [P, NT, VW])
                    normalise(nc, k, sem, "n1_", h, x1)
                    with scope() as norm:
                        x, xT = norm.sb("x1n", [P, NT, C]), norm.sb("x1nT", [HC, 2, N])
                        normalise(nc, k, sem, "n2_", x1, x, xT, d["ffn"]["ln1_w"], d["ffn"]["ln1_b"])
                        project_qkv(nc, k, sem, "p1_", d["ffn"], xT, q_pieces, k_pieces, vals)
                    yT = attn.sb("yT1", [P, NC4, N])
                    attend(nc, k, sem, "a1_", q_pieces, k_pieces, vals, yT, NH, 1.0 / float(np.sqrt(HD)), causal=True)
                    project_out(nc, k, sem, "o1_", d["ffn"], yT, x1, x2)
                mixture_of_experts(nc, k, sem, "m0_", d["moe0"], scope,
                                   lambda x, xT: normalise(nc, k, sem, "n3_", x2, x, xT, d["ffn"]["ln2_w"], d["ffn"]["ln2_b"]),
                                   E=8, K=2, F=4 * C, A=4 * C, swiglu=False, capacity=CAPACITY, tiles=8 * CAPACITY // P,
                                   first=h, second=x2, out=h)
        def differential_attention():
            with scope() as attn:
                vals = attn.sb("vals2", [P, NT, VW])
                neg_lambda = attn.sb("neg_lambda", [P, 1])
                attention_lambda(nc, sem, d["diff"], neg_lambda, LAMBDA_INIT)
                with scope() as norm:
                    x, xT = norm.sb("x3", [P, NT, C]), norm.sb("x3T", [HC, 2, N])
                    normalise(nc, k, sem, "n4_", h, x, xT)
                    project_qkv(nc, k, sem, "p2_", d["diff"], xT, q_pieces, k_pieces, vals, guard=True)
                yT = attn.sb("yT2", [P, NC4, N])
                attend(nc, k, sem, "a2_", q_pieces, k_pieces, vals, yT, 2 * NH, float(HD // 2) ** -0.5,
                       neg_lambda=neg_lambda)
                head_rms(nc, k, sem, d["diff"], yT, 1.0 - LAMBDA_INIT)
                project_out(nc, k, sem, "o2_", d["diff"], yT, h, h)
        def gated_experts():
            with scope() as moe:
                x = moe.sb("x4", [P, NT, C])
                normalise(nc, k, sem, "n5_", h, x)
                mixture_of_experts(nc, k, sem, "m1_", d["moe1"], scope,
                                   lambda t, tT: normalise(nc, k, sem, "n6_", x, t, tT, d["moe1"]["scale"], rms=True),
                                   E=16, K=4, F=4 * C, A=2 * C, swiglu=True, capacity=None, tiles=4 * NT + 16,
                                   first=h, second=x, out=h)

        embed(nc, k, sem, d, h)
        mixture_keyed_attention()
        clear_semaphores()
        pre_norm_block()
        clear_semaphores()
        differential_attention()
        clear_semaphores()
        gated_experts()
        finish_program(nc, sem, h, out)


def kernel(**inputs):
    import concourse.bacc as _bacc
    from concourse.bass_utils import run_bass_kernel_spmd as _run
    a = {n: np.asarray(v) for n, v in inputs.items()}

    def halves(w):
        return w.reshape(2, HC, -1).transpose(1, 0, 2)

    arrays = {}
    arrays["ids"] = a["x"].reshape(NT, P).T
    arrays["tok_embed"] = a["L0_tok_tok_embed"]
    arrays["tok_W1"] = a["L0_tok_W1"].T.reshape(FRONT // P, P, C).transpose(1, 0, 2)
    arrays["tok_W2"] = halves(a["L0_tok_W2"].T)
    arrays["tok_b1"] = a["L0_tok_b1"].reshape(2, HC).T
    arrays["tok_b2"] = a["L0_tok_b2"]
    w = a["L0_attn_Wqkv"].reshape(C, C, 3)
    bias = a["L0_attn_bqkv"].reshape(C, 3)
    for i, n in enumerate("qkv"):
        arrays[f"mix.W{n}"] = halves(w[:, :, i])
    arrays["mix.bq"] = bias[:, 0].reshape(2, HC).T
    arrays["mix.bk"] = bias[:, 1].reshape(2, HC).T
    arrays["mix.bk_packed"] = np.stack([bias[0:P, 1], np.concatenate([bias[P:C, 1], bias[P:C, 1]])], axis=1)
    arrays["mix.bv"] = bias[:, 2]
    arrays["mix.Wo"] = a["L0_attn_Wproj"]
    arrays["mix.bo"] = a["L0_attn_bproj"]
    arrays["mix_mean"] = a["L0_attn_mean"]
    arrays["mix_logvar"] = a["L0_attn_logvar"]
    arrays["mix_coef"] = a["L0_attn_mix_coef"]
    for g, p in (("ffn", "L0_ffn_"), ("diff", "L1_attn_")):
        for i, n in enumerate("qkv"):
            if g == "ffn":
                wn, bn = a[p + "attn_qkv_w"][:, i * C:(i + 1) * C], a[p + "attn_qkv_b"][i * C:(i + 1) * C]
            else:
                wn, bn = a[p + "W" + n], a[p + "b" + n]
            arrays[f"{g}.W{n}"] = halves(wn)
            arrays[f"{g}.b{n}"] = bn if n == "v" else bn.reshape(2, HC).T
    arrays["ffn.Wo"], arrays["ffn.bo"] = a["L0_ffn_attn_proj_w"], a["L0_ffn_attn_proj_b"]
    arrays["diff.Wo"], arrays["diff.bo"] = a["L1_attn_Wo"], a["L1_attn_bo"]
    for n in ("ln1_w", "ln1_b", "ln2_w", "ln2_b"):
        arrays["ffn." + n] = a["L0_ffn_" + n]
    arrays["diff.lambdas"] = np.stack([a["L1_attn_lambda_" + n] for n in ("q1", "q2", "k1", "k2")])
    arrays["diff.subln"] = a["L1_attn_subln_w"].reshape(HD, 1)

    def first_layer(w, bias):
        e, _, f = w.shape
        w = w.reshape(e, 2, HC, f)
        rows = np.stack([np.zeros_like(bias), bias], axis=1)
        return np.concatenate([w, rows[:, :, None, :]], axis=2).transpose(0, 2, 1, 3)

    def second_layer(w):
        e, f, _ = w.shape
        return w.reshape(e, f // P, P, C).transpose(0, 2, 1, 3)
    arrays["moe0.wg"] = halves(a["L0_ffn_w_g"])
    arrays["moe0.w1"] = first_layer(a["L0_ffn_exp_fc_w"], a["L0_ffn_exp_fc_b"][:, 0, :])
    arrays["moe0.w2"] = second_layer(a["L0_ffn_exp_proj_w"])
    arrays["moe0.b2"] = a["L0_ffn_exp_proj_b"][:, 0, :]
    arrays["moe1.scale"] = a["L1_ffn_norm_scale"]
    arrays["moe1.wg"] = halves(a["L1_ffn_gate_w"].T)
    arrays["moe1.bg"] = a["L1_ffn_gate_b"]
    m1, mb1 = a["L1_ffn_mlp1_w"].transpose(0, 2, 1), a["L1_ffn_mlp1_b"]
    arrays["moe1.w1"] = first_layer(np.concatenate([m1[:, :, 0::2], m1[:, :, 1::2]], axis=2),
                                    np.concatenate([mb1[:, 0::2], mb1[:, 1::2]], axis=1))
    arrays["moe1.w2"] = second_layer(a["L1_ffn_mlp2_w"].transpose(0, 2, 1))
    arrays["moe1.b2"] = a["L1_ffn_mlp2_b"]
    arrays = {n: np.ascontiguousarray(v) for n, v in arrays.items()}

    nc = _bacc.Bacc("TRN2", target_bir_lowering=False, num_devices=1)
    d, feeds = {}, {}
    for n, v in arrays.items():
        name = "in_" + n.replace(".", "_")
        ap = nc.dram_tensor(name, v.shape, mybir.dt.from_np(v.dtype), kind="ExternalInput").ap()
        feeds[name] = v
        if "." in n:
            group, member = n.split(".")
            d.setdefault(group, {})[member] = ap
        else:
            d[n] = ap
    out = nc.dram_tensor("out_0", (N, C), F32, kind="ExternalOutput").ap()
    tower(nc, d, out)
    r = _run(nc, [feeds], core_ids=[0])
    return r.results[0]["out_0"].reshape(B, S, C)
```

```python
from contextlib import ExitStack

import numpy as np

import concourse.bass as bass
from concourse import mybir

F32 = mybir.dt.float32
BF16 = mybir.dt.bfloat16
U32 = mybir.dt.uint32
I32 = mybir.dt.int32
ALU = mybir.AluOpType
ACT = mybir.ActivationFunctionType
AX = mybir.AxisListType

P = 128
B, S = 4, 512
N = B * S
NT = N // P
TPB = S // P
C = 192
HC = C // 2
NH = 12
HD = C // NH
VP = 32
VW = NH * VP
NC4 = NH // 4
FRONT = 768
EPS = 1e-5
MASKED = -1e30
HUGE = 1e30
BIG_SCORE = 1e18
CAPACITY = 640
LAMBDA_INIT = 0.8 - 0.6 * float(np.exp(-0.3 * 0))


def link(eng, sem, count, ins):
    count[0] += 1
    ins.then_inc(sem, 1)
    eng.wait_ge(sem, count[0])


class Slots:

    def __init__(self, sem, name, size):
        self.size = size
        self.ready = [sem(f"{name}_ready{s}") for s in range(size)]
        self.free = [sem(f"{name}_free{s}") for s in range(size)]

    def wait_free(self, pe, n):
        if n >= self.size:
            pe.wait_ge(self.free[n % self.size], n // self.size)

    def wait_ready(self, eng, n):
        eng.wait_ge(self.ready[n % self.size], n // self.size + 1)


def build_constants(nc, cx, sb, sem):
    k = {}
    k["ident"] = sb("ident", [P, P], F32)
    k["identb"] = sb("identb", [P, P], BF16)
    k["before"] = sb("before", [P, P], F32)
    k["ones"] = sb("ones", [P, P], F32)
    k["mask_qk"] = sb("mask_qk", [P, P], BF16)
    k["mask_kq"] = sb("mask_kq", [P, P], BF16)
    k["sel_mean"] = sb("sel_mean", [P, P], F32)
    filled = sem("const_filled")
    done = sem("const_done")
    with nc.Block() as block:
        @block.gpsimd
        def _(pool):
            for name, value in (("ident", 0.0), ("identb", 0.0), ("before", 1.0), ("ones", 1.0), ("mask_qk", 0.0),
                                ("mask_kq", 0.0), ("sel_mean", 1.0 / HD)):
                last = nc.gpsimd.memset(k[name][:], value)
            last.then_inc(filled, 1)
            pool.wait_ge(filled, 1)

            def select(name, pattern, base, mult, op, fill):
                t = k[name][:]
                if len(pattern) == 2:
                    t = t.rearrange("p (a b) -> p a b", a=pattern[0][1])
                return nc.gpsimd.affine_select(out=t, in_=t, pattern=pattern, compare_op=op, fill=fill, base=base,
                                               channel_multiplier=mult)
            select("ident", [[-1, P]], 0, 1, ALU.not_equal, 1.0)
            select("identb", [[-1, P]], 0, 1, ALU.not_equal, 1.0)
            select("before", [[1, P]], 0, -1, ALU.is_gt, 0.0)
            select("mask_qk", [[-1, P]], 0, 1, ALU.is_ge, MASKED)
            select("mask_kq", [[1, P]], 0, -1, ALU.is_ge, MASKED)
            select("sel_mean", [[-VP, 4], [0, VP]], 0, 1, ALU.is_ge, 0.0).then_inc(done, 1)
            pool.wait_ge(done, 1)
            select("sel_mean", [[VP, 4], [0, VP]], HD - 1, -1, ALU.is_ge, 0.0).then_inc(done, 1)
    return k


def embed(nc, k, sem, d, h):
    FK = FRONT // P
    RING = 2
    with ExitStack() as cx:
        def sb(name, shape, dt=F32):
            return cx.enter_context(nc.sbuf_tensor(name, shape, dt))

        def ps(name, shape, dt=F32):
            return cx.enter_context(nc.psum_tensor(name, shape, dt))
        ids = sb("ids", [P, NT], I32)
        w1 = sb("w1", [P, FK, C])
        w2 = sb("w2", [HC, 2, C])
        b1 = sb("b1", [HC, 2])
        b2 = sb("b2", [P, C])
        rows = sb("rows", [P, RING * TPB, FRONT])
        rowsT = sb("rowsT", [P, RING, FK, S])
        act = sb("act", [HC, RING, 2, S])
        tp = ps("tp", [P, 2, 1024])
        hid = ps("hid", [P, 2, S])
        outp = ps("outp", [P, 2, S])
        ids_in, weights_in = sem("em_ids_in"), sem("em_weights_in")
        gathered = [sem(f"em_gathered{i}") for i in range(RING * TPB)]
        transposed, rows_moved = sem("em_transposed"), sem("em_rows_moved")
        hidden, activated = sem("em_hidden"), sem("em_activated")
        projected, stored = sem("em_projected"), sem("em_stored")
        with nc.Block() as block:
            @block.sync
            def _(sp):
                sp.dma_start(ids[:], d["ids"]).then_inc(ids_in, 16)
                sp.dma_start(w1[:], d["tok_W1"]).then_inc(weights_in, 16)
                sp.dma_start(w2[:], d["tok_W2"]).then_inc(weights_in, 16)
                sp.dma_start(b1[:], d["tok_b1"]).then_inc(weights_in, 16)
                sp.dma_start(b2[:], d["tok_b2"].partition_broadcast(P)).then_inc(weights_in, 16)

            @block.gpsimd
            def _(pool):
                pool.wait_ge(ids_in, 16)
                for t in range(NT):
                    slot = t % (RING * TPB)
                    if t >= RING * TPB:
                        pool.wait_ge(transposed, t - RING * TPB + 1)
                    pool.indirect_dma_start(
                        out=rows[:, slot, :], out_offset=None, in_=d["tok_embed"],
                        in_offset=bass.IndirectOffsetOnAxis(ap=ids[:, t:t + 1].bitcast(U32), axis=0),
                    ).then_inc(gathered[slot], 16)

            @block.tensor
            def _(pe):
                pe.wait_ge(weights_in, 64)

                def project(b):
                    for i in range(TPB):
                        t = b * TPB + i
                        if i == 0:
                            pe.wait_ge(activated, 2 * b + 2)
                        if t >= 2:
                            pe.wait_ge(stored, t - 1)
                        for c in range(2):
                            mm = nc.tensor.matmul(outp[:, t % 2, 0:C], act[:, b % RING, c, i * P:(i + 1) * P], w2[:, c, :],
                                                  start=c == 0, stop=c == 1)
                        mm.then_inc(projected, 1)
                for b in range(B):
                    for i in range(TPB):
                        t = b * TPB + i
                        slot = t % (RING * TPB)
                        pe.wait_ge(gathered[slot], 16 * (t // (RING * TPB) + 1))
                        if t >= 2:
                            pe.wait_ge(rows_moved, t - 1)
                        for f in range(FK):
                            mm = nc.tensor.transpose(tp[:, t % 2, f * P:(f + 1) * P], rows[:, slot, f * P:(f + 1) * P],
                                                     k["ident"][:])
                        mm.then_inc(transposed, 1)
                    pe.wait_ge(rows_moved, (b + 1) * TPB)
                    for m in range(2):
                        if b >= 1:
                            pe.wait_ge(activated, 2 * (b - 1) + m + 1)
                        for f in range(FK):
                            mm = nc.tensor.matmul(hid[0:HC, m, :], w1[:, f, m * HC:(m + 1) * HC], rowsT[:, b % RING, f, :],
                                                  start=f == 0, stop=f == FK - 1)
                        mm.then_inc(hidden, 1)
                    if b >= 1:
                        project(b - 1)
                project(B - 1)

            @block.scalar
            def _(act_):
                act_.wait_ge(weights_in, 64)
                for b in range(B):
                    for m in range(2):
                        act_.wait_ge(hidden, 2 * b + m + 1)
                        if b >= RING:
                            act_.wait_ge(projected, (b - RING + 1) * TPB)
                        nc.scalar.activation(act[:, b % RING, m, :], hid[0:HC, m, :], ACT.Gelu, bias=b1[:, m:m + 1])\
                            .then_inc(activated, 1)

            @block.vector
            def _(dve):
                dve.wait_ge(weights_in, 64)

                def store(b):
                    for i in range(TPB):
                        t = b * TPB + i
                        dve.wait_ge(projected, t + 1)
                        nc.vector.tensor_tensor(h[:, t, :], outp[:, t % 2, 0:C], b2[:], ALU.add).then_inc(stored, 1)
                for b in range(B):
                    for i in range(TPB):
                        t = b * TPB + i
                        dve.wait_ge(transposed, t + 1)
                        if b >= RING:
                            dve.wait_ge(hidden, 2 * (b - RING + 1))
                        nc.vector.tensor_copy(rowsT[:, b % RING, :, i * P:(i + 1) * P],
                                              tp[:, t % 2, 0:FRONT].rearrange("p (f t) -> p f t", f=FK)).then_inc(rows_moved, 1)
                    if b >= 1:
                        store(b - 1)
                store(B - 1)


def normalise(nc, k, sem, tag, src, dst, dstT=None, gain=None, shift=None, rms=False, ahead=()):
    QT = NT // 4
    with ExitStack() as cx:
        def sb(name, shape, dt=F32):
            return cx.enter_context(nc.sbuf_tensor(tag + name, shape, dt))
        stats = sb("stats", [P, NT, 6])
        mv = sb("mv", [P, NT, 2])
        spread = sb("spread", [P, NT])
        root = sb("root", [P, NT])
        rstd = sb("rstd", [P, NT])
        gain_bc = sb("gain_bc", [P, C])
        shift_bc = sb("shift_bc", [P, C])
        slot = [cx.enter_context(nc.psum_tensor(f"{tag}slot{i}", [P, 512], F32)) for i in range(2)]
        affine_in = sem(tag + "affine_in")
        chain = sem(tag + "chain")
        spread_ready, root_ready = sem(tag + "spread_ready"), sem(tag + "root_ready")
        quarter_ready = sem(tag + "quarter_ready")
        transposed, moved = sem(tag + "transposed"), sem(tag + "moved")
        with nc.Block() as block:
            if gain is not None:
                @block.sync
                def _(sp):
                    sp.dma_start(gain_bc[:], gain.partition_broadcast(P)).then_inc(affine_in, 16)
                    if shift is not None:
                        sp.dma_start(shift_bc[:], shift.partition_broadcast(P)).then_inc(affine_in, 16)

            @block.vector
            def _(dve):
                n = [0]
                for t in range(NT):
                    last = nc.vector.bn_stats(stats[:, t, :], src[:, t, :])
                link(dve, chain, n, last)
                for t in range(NT):
                    last = nc.vector.bn_aggr(mv[:, t, :], stats[:, t, :])
                link(dve, chain, n, last)
                if rms:
                    link(dve, chain, n, nc.vector.tensor_tensor(root[:], mv[:, :, 0], mv[:, :, 0], ALU.mult))
                    link(dve, chain, n, nc.vector.tensor_tensor(spread[:], root[:], mv[:, :, 1], ALU.add))
                    nc.vector.tensor_scalar(spread[:], spread[:], EPS, None, ALU.add).then_inc(spread_ready, 1)
                else:
                    nc.vector.tensor_scalar(spread[:], mv[:, :, 1], EPS, None, ALU.add).then_inc(spread_ready, 1)
                dve.wait_ge(root_ready, 1)
                link(dve, chain, n, nc.vector.reciprocal(rstd[:], root[:]))
                if gain is not None:
                    dve.wait_ge(affine_in, 32 if shift is not None else 16)
                for q in range(0, NT, QT):
                    for t in range(q, q + QT):
                        if rms:
                            last = nc.vector.tensor_scalar(dst[:, t, :], src[:, t, :], rstd[:, t:t + 1], None, ALU.mult)
                        else:
                            last = nc.vector.tensor_scalar(dst[:, t, :], src[:, t, :], mv[:, t, 0:1], rstd[:, t:t + 1],
                                                           ALU.subtract, ALU.mult)
                    part = dst[:, q:q + QT, :]
                    if gain is not None:
                        link(dve, chain, n, last)
                        last = nc.vector.tensor_tensor(part, part, gain_bc[:].unsqueeze(1).to_broadcast([P, QT, C]), ALU.mult)
                    if shift is not None:
                        link(dve, chain, n, last)
                        last = nc.vector.tensor_tensor(part, part, shift_bc[:].unsqueeze(1).to_broadcast([P, QT, C]), ALU.add)
                    last.then_inc(quarter_ready, 1)

            @block.tensor
            def _(pe):
                for t in range(NT if dstT is not None else 0):
                    pe.wait_ge(quarter_ready, t // QT + 1)
                    if t >= 2:
                        pe.wait_ge(moved, t - 1)
                    for c in range(2):
                        mm = nc.tensor.transpose(slot[t % 2][0:HC, c * P:(c + 1) * P], dst[:, t, c * HC:(c + 1) * HC],
                                                 k["ident"][:])
                    mm.then_inc(transposed, 1)

            @block.scalar
            def _(act):
                if ahead:
                    act.wait_ge(affine_in, 32 if shift is not None else 16)
                for to, source, arrived in ahead:
                    act.dma_start(to, source).then_inc(arrived, 16)
                act.wait_ge(spread_ready, 1)
                nc.scalar.activation(root[:], spread[:], ACT.Sqrt).then_inc(root_ready, 1)
                for t in range(NT if dstT is not None else 0):
                    act.wait_ge(transposed, t + 1)
                    nc.scalar.activation(dstT[0:HC, :, t * P:(t + 1) * P],
                                         slot[t % 2][0:HC, 0:2 * P].rearrange("p (c t) -> p c t", c=2), ACT.Copy)\
                        .then_inc(moved, 1)


def project_qkv(nc, k, sem, tag, d, xT, q_pieces, k_pieces, vals, keys=None, guard=False):
    with ExitStack() as cx:
        def sb(name, shape, dt=F32):
            return cx.enter_context(nc.sbuf_tensor(tag + name, shape, dt))
        wq, wk, wv = (sb(x, [HC, 2, C]) for x in ("wq", "wk", "wv"))
        bq, bk = sb("bq", [HC, 2]), sb("bk", [HC, 2])
        bkp = sb("bkp", [P, 2])
        bv = sb("bv", [P, C])
        R = 4
        x = sb("x", [HC, R, S])
        rest = sb("rest", [HC, R, S])
        piece = [sb(f"piece{i}", [HC, R, S], BF16) for i in range(3)]
        slot = [cx.enter_context(nc.psum_tensor(f"{tag}slot{i}", [P, 512], F32)) for i in range(4)]
        ring = Slots(sem, tag + "slot", 4)
        weights_in = sem(tag + "weights_in")
        chain = sem(tag + "chain")
        hi_ready, rest_ready = sem(tag + "hi_ready"), sem(tag + "rest_ready")
        mid_ready, lo_ready = sem(tag + "mid_ready"), sem(tag + "lo_ready")
        pieces_out = [sem(f"{tag}pieces_out{i}") for i in range(R)]
        ones_set = sem(tag + "ones_set")
        items = [("q", c, b) for c in range(2) for b in range(B)]
        if keys is None:
            items += [("k", c, b) for c in range(2) for b in range(B)]
        splits = list(items)
        if keys is not None:
            items += [("key", i, 0) for i in range(6)]
        items += [("v", t, 0) for t in range(NT)]
        with nc.Block() as block:
            @block.sync
            def _(sp):
                loads = [(wq[:], d["Wq"]), (wk[:], d["Wk"]), (wv[:], d["Wv"]), (bq[:], d["bq"]), (bk[:], d["bk"]),
                         (bv[:], d["bv"].partition_broadcast(P))]
                if keys is not None:
                    loads.append((bkp[:], d["bk_packed"]))
                for dst, src in loads:
                    sp.dma_start(dst, src).then_inc(weights_in, 16)
                for n, (what, c, b) in enumerate(splits):
                    out = q_pieces if what == "q" else k_pieces
                    for i, sig in enumerate((hi_ready, mid_ready, lo_ready)):
                        sp.wait_ge(sig, n + 1)
                        sp.dma_start(out[i, c * HC:(c + 1) * HC, b * S:(b + 1) * S], piece[i][:, n % R, :])\
                            .then_inc(pieces_out[n % R], 16)
                for r in range(R):
                    sp.wait_ge(pieces_out[r], 48 * (len(splits) // R))

            @block.gpsimd
            def _(pool):
                nc.gpsimd.memset(vals[:], 0.0).then_inc(ones_set, 1)
                pool.wait_ge(ones_set, 1)
                nc.gpsimd.memset(vals[:].rearrange("p t (h e) -> p (t h) e", e=VP)[:, :, HD:HD + 1], 1.0)\
                    .then_inc(ones_set, 1)

            @block.tensor
            def _(pe):
                pe.wait_ge(weights_in, 16 * (7 if keys is not None else 6))
                for n, (what, c, b) in enumerate(items):
                    out = slot[n % 4]
                    ring.wait_free(pe, n)
                    for h in range(2):
                        if what == "v":
                            mm = nc.tensor.matmul(out[:, 0:C], xT[0:HC, h, c * P:(c + 1) * P], wv[:, h, :],
                                                  start=h == 0, stop=h == 1)
                        elif what == "key" and c < 4:
                            mm = nc.tensor.matmul(out[:], wk[:, h, 0:P], xT[0:HC, h, c * S:(c + 1) * S],
                                                  start=h == 0, stop=h == 1)
                        elif what == "key":
                            mm = nc.tensor.matmul(out[0:64, :], wk[:, h, P:C], xT[0:HC, h, (c - 4) * S:(c - 3) * S],
                                                  start=h == 0, stop=h == 1)
                        else:
                            w = wq if what == "q" else wk
                            mm = nc.tensor.matmul(out[0:HC, :], w[:, h, c * HC:(c + 1) * HC],
                                                  xT[0:HC, h, b * S:(b + 1) * S], start=h == 0, stop=h == 1)
                    if what == "key" and c >= 4:
                        for h in range(2):
                            mm = nc.tensor.matmul(out[64:P, :], wk[:, h, P:C], xT[0:HC, h, (c - 2) * S:(c - 1) * S],
                                                  start=h == 0, stop=h == 1)
                    mm.then_inc(ring.ready[n % 4], 1)

            @block.vector
            def _(dve):
                cnt = [0]

                def lowest(n):
                    dve.wait_ge(mid_ready, n + 1)
                    nc.vector.tensor_tensor(piece[2][:, n % R, :], rest[:, n % R, :], piece[1][:, n % R, :], ALU.subtract)\
                        .then_inc(lo_ready, 1)
                dve.wait_ge(weights_in, 16 * (7 if keys is not None else 6))
                for n, (what, c, b) in enumerate(items):
                    if n == len(splits):
                        lowest(n - 1)
                    if n >= len(splits):
                        ring.wait_ready(dve, n)
                    src = slot[n % 4]
                    if what == "v":
                        if c == 0:
                            dve.wait_ge(ones_set, 2)
                        nc.vector.tensor_tensor(vals[:, c, :].rearrange("p (h e) -> p h e", e=VP)[:, :, 0:HD],
                                                src[:, 0:C].rearrange("p (h e) -> p h e", e=HD),
                                                bv[:].rearrange("p (h e) -> p h e", e=HD), ALU.add)\
                            .then_inc(ring.free[n % 4], 1)
                        continue
                    if what == "key":
                        nc.vector.tensor_scalar(keys[:, c // 2, (c % 2) * S:(c % 2 + 1) * S], src[:],
                                                bkp[:, c // 4:c // 4 + 1], None, ALU.add).then_inc(ring.free[n % 4], 1)
                        continue
                    r = n % R
                    dve.wait_ge(ring.free[n % 4], n // 4 + 1)
                    if guard:
                        link(dve, chain, cnt, nc.vector.tensor_scalar(x[:, r, :], x[:, r, :], -BIG_SCORE, BIG_SCORE,
                                                                      ALU.max, ALU.min))
                    if n >= R:
                        dve.wait_ge(pieces_out[r], 48 * (n // R))
                    nc.vector.tensor_copy(piece[0][:, r, :], x[:, r, :]).then_inc(hi_ready, 1)
                    dve.wait_ge(hi_ready, n + 1)
                    nc.vector.tensor_tensor(rest[:, r, :], x[:, r, :], piece[0][:, r, :], ALU.subtract)\
                        .then_inc(rest_ready, 1)
                    if n >= 1:
                        lowest(n - 1)

            @block.scalar
            def _(act):
                def whole(n):
                    what, c, b = items[n]
                    ring.wait_ready(act, n)
                    if n >= R:
                        act.wait_ge(rest_ready, n - R + 1)
                    nc.scalar.activation(x[:, n % R, :], slot[n % 4][0:HC, :], ACT.Identity,
                                         bias=(bq if what == "q" else bk)[:, c:c + 1]).then_inc(ring.free[n % 4], 1)
                act.wait_ge(weights_in, 16 * (7 if keys is not None else 6))
                whole(0)
                for n in range(len(splits)):
                    r = n % R
                    if n + 1 < len(splits):
                        whole(n + 1)
                    act.wait_ge(rest_ready, n + 1)
                    if n >= R:
                        act.wait_ge(pieces_out[r], 48 * (n // R))
                    nc.scalar.activation(piece[1][:, r, :], rest[:, r, :], ACT.Copy).then_inc(mid_ready, 1)


def mixture_tables(nc, sem, d, tab):
    with ExitStack() as cx:
        def sb(name, shape, dt=F32):
            return cx.enter_context(nc.sbuf_tensor("mt_" + name, shape, dt))
        mean = sb("mean", [P, 2, C])
        logvar = sb("logvar", [P, 2, C])
        mix = sb("mix", [P, C])
        emix = sb("emix", [P, C])
        top, neg_top, esum, log_esum, off, half_log2 = (sb(x, [P, 1]) for x in (
            "top", "neg_top", "esum", "log_esum", "off", "half_log2"))
        loads, chain = sem("mt_loads"), sem("mt_chain")
        top_ready, exp_ready, log_ready, scale_ready = (sem("mt_" + x) for x in (
            "top_ready", "exp_ready", "log_ready", "scale_ready"))
        with nc.Block() as block:
            @block.sync
            def _(sp):
                for t, name in ((mean, "mix_mean"), (logvar, "mix_logvar")):
                    sp.dma_start(t[:, 0, :], d[name][0:P, :]).then_inc(loads, 16)
                    sp.dma_start(t[0:64, 1, :], d[name][P:C, :]).then_inc(loads, 16)
                    sp.dma_start(t[64:P, 1, :], d[name][P:C, :]).then_inc(loads, 16)
                sp.dma_start(mix[:], d["mix_coef"].partition_broadcast(P)).then_inc(loads, 16)

            @block.scalar
            def _(act):
                act.wait_ge(top_ready, 1)
                nc.scalar.activation(emix[:], mix[:], ACT.Exp, bias=neg_top[:], accum_out=esum[:]).then_inc(exp_ready, 1)
                nc.scalar.activation(tab[:, 0], logvar[:], ACT.Exp, scale=-0.5, bias=half_log2[:]).then_inc(scale_ready, 1)
                act.wait_ge(exp_ready, 1)
                nc.scalar.activation(log_esum[:], esum[:], ACT.Ln).then_inc(log_ready, 1)

            @block.vector
            def _(dve):
                cnt = [0]
                dve.wait_ge(loads, 16 * 7)
                nc.vector.memset(half_log2[:], float(-0.5 * np.log(2.0)))
                link(dve, chain, cnt, nc.vector.tensor_reduce(top[:], mix[:], axis=AX.X, op=ALU.max))
                nc.vector.tensor_scalar(neg_top[:], top[:], -1.0, None, ALU.mult).then_inc(top_ready, 1)
                dve.wait_ge(log_ready, 1)
                link(dve, chain, cnt, nc.vector.tensor_tensor(off[:], neg_top[:], log_esum[:], ALU.subtract))
                link(dve, chain, cnt, nc.vector.tensor_scalar(emix[:], mix[:], off[:], float(-0.5 * np.log(2.0 * np.pi)),
                                                              ALU.add, ALU.add))
                dve.wait_ge(scale_ready, 1)
                nc.vector.scalar_tensor_tensor(out=tab[:, 2], in0=logvar[:], scalar=-0.5,
                                               in1=emix[:].unsqueeze(1).to_broadcast([P, 2, C]), op0=ALU.mult, op1=ALU.add)
                nc.vector.scalar_tensor_tensor(out=tab[:, 1], in0=mean[:], scalar=-1.0, in1=tab[:, 0],
                                               op0=ALU.mult, op1=ALU.mult)


def mixture_keys(nc, k, sem, tab, keys, k_pieces):
    G = 12
    D = 8
    PART = 2
    EXPS = D // PART + G - D
    POOLS = (G - D) // PART
    PARTS = G // PART
    LATE = PARTS - 2
    NG = C // G
    BLOCKS = 3
    W = N // 2
    with ExitStack() as cx:
        def sb(name, shape, dt=F32):
            return cx.enter_context(nc.sbuf_tensor("mk_" + name, shape, dt))
        buf = sb("buf", [P, 2, G, W])
        neg_max = sb("neg_max", [P, 2, W])
        last_neg_max = sb("last_neg_max", [P, W])
        drop, alpha, scaled, mixed = (sb(x, [P, W]) for x in ("drop", "alpha", "scaled", "mixed"))
        piece = [sb(f"piece{i}", [P, W], BF16) for i in range(3)]
        total = [cx.enter_context(nc.psum_tensor(f"mk_total{i}", [P, W], F32)) for i in range(2)]
        lowest = cx.enter_context(nc.psum_tensor("mk_lowest", [P, W], F32))
        squared, lowered, off_dve, off_pool, exped, summed = (sem("mk_" + x) for x in (
            "squared", "lowered", "off_dve", "off_pool", "exped", "summed"))
        dropped, alpha_ready, scaled_ready, total_ready = (sem("mk_" + x) for x in (
            "dropped", "alpha_ready", "scaled_ready", "total_ready"))
        log_ready, kept_ready, pieces_ready = (sem("mk_" + x) for x in ("log_ready", "kept_ready", "pieces_ready"))
        chain, stored = sem("mk_chain"), sem("mk_stored")

        def column(t, ch, m):
            return tab[:, t, ch // 2, bass.ds(m, 1)]

        def back(ch, g, by):
            if isinstance(g, int) and g < by:
                ch, g = ch - 1, g + NG
            return None if ch < 0 or (ch == BLOCKS and isinstance(g, int)) or ch > BLOCKS else (ch, g - by)

        def each_group(engine, step):
            for ch in range(BLOCKS + 1):
                for g in range(2):
                    step(ch, g, g, ch * NG + g)
                if ch < BLOCKS:
                    with engine.Fori(1, NG // 2) as i:
                        for par in range(2):
                            step(ch, 2 * i + par, par, 2 * i + (ch * NG + par))

        def finish(engine, ops, ch):
            count = [4 * ch]
            engine.wait_ge(log_ready, ch + 1)
            link(engine, chain, count, ops.tensor_tensor(mixed[:], mixed[:], last_neg_max[:], ALU.subtract))
            if ch:
                engine.wait_ge(stored, 48 * ch)
            link(engine, chain, count, ops.tensor_copy(piece[0][:], mixed[:]))
            link(engine, chain, count, ops.tensor_tensor(mixed[:], mixed[:], piece[0][:], ALU.subtract))
            link(engine, chain, count, ops.tensor_copy(piece[1][:], mixed[:]))
            ops.tensor_tensor(piece[2][:], mixed[:], piece[1][:], ALU.subtract).then_inc(pieces_ready, 1)
        with nc.Block() as block:
            @block.scalar
            def _(act):
                def squares(ch, g, par, n, part):
                    if not isinstance(n, int) or n >= 2:
                        act.wait_ge(summed, (n - 2) * PARTS + part + 1)
                    for j in range(part * PART, part * PART + PART):
                        nc.scalar.activation(buf[:, par, j, :], keys[:, ch, :], ACT.Square, scale=column(0, ch, g * G + j),
                                             bias=column(1, ch, g * G + j)).then_inc(squared, 1)

                def exps(ch, g, par, n, part):
                    if part * PART < D:
                        act.wait_ge(off_dve, n * D + part * PART + PART)
                        both = buf[:, par, part * PART:part * PART + PART, :]
                        nc.scalar.activation(both, both, ACT.Exp, scale=-1.0).then_inc(exped, 1)
                        return
                    act.wait_ge(off_pool, n * POOLS + part - D // PART + 1)
                    for j in range(part * PART, part * PART + PART):
                        nc.scalar.activation(buf[:, par, j, :], buf[:, par, j, :], ACT.Exp, scale=-1.0,
                                             bias=column(2, ch, g * G + j)).then_inc(exped, 1)

                def step(ch, g, par, n):
                    for part in range(PARTS):
                        if ch < BLOCKS:
                            squares(ch, g, par, n, part)
                        if part == 0 and back(ch, g, 2):
                            exps(*back(ch, g, 2), par, n - 2, PARTS - 1)
                        if part > 0 and back(ch, g, 1):
                            exps(*back(ch, g, 1), 1 - par, n - 1, part - 1)
                        if part == 1 and back(ch, g, 1):
                            act.wait_ge(dropped, n)
                            if not isinstance(n, int) or n >= 2:
                                act.wait_ge(scaled_ready, n - 1)
                            nc.scalar.activation(alpha[:], drop[:], ACT.Exp).then_inc(alpha_ready, 1)
                        if part == LATE and isinstance(g, int) and g == 1 and ch > 0:
                            act.wait_ge(total_ready, ch * NG + 1)
                            if ch > 1:
                                act.wait_ge(pieces_ready, ch - 1)
                            nc.scalar.activation(mixed[:], total[1][:], ACT.Ln).then_inc(log_ready, 1)
                each_group(act, step)

            @block.vector
            def _(dve):
                def minimum(ch, g, par, n, j):
                    dve.wait_ge(squared, n * G + j + 1)
                    if not isinstance(n, int) or n > 0 or j > 0:
                        dve.wait_ge(lowered, n * G + j)
                    if j == G - 1 and (not isinstance(n, int) or n >= 2):
                        dve.wait_ge(dropped, n)
                        dve.wait_ge(off_dve, (n - 1) * D)
                        if isinstance(g, int) and g == 1 and ch > 0:
                            dve.wait_ge(kept_ready, ch)
                    out = lowest[:] if j < G - 1 else neg_max[:, par, :]
                    if j == 0 and isinstance(g, int) and g == 0:
                        nc.vector.tensor_scalar(out, buf[:, par, j, :], column(2, ch, g * G + j), None, ALU.subtract)\
                            .then_inc(lowered, 1)
                    else:
                        nc.vector.scalar_tensor_tensor(out=out, in0=buf[:, par, j, :], scalar=column(2, ch, g * G + j),
                                                       in1=lowest[:] if j else neg_max[:, 1 - par, :],
                                                       op0=ALU.subtract, op1=ALU.min).then_inc(lowered, 1)

                def take_off(ch, g, par, j):
                    nc.vector.scalar_tensor_tensor(out=buf[:, par, j, :], in0=buf[:, par, j, :],
                                                   scalar=column(2, ch, g * G + j), in1=neg_max[:, par, :],
                                                   op0=ALU.subtract, op1=ALU.subtract).then_inc(off_dve, 1)

                def step(ch, g, par, n):
                    if back(ch, g, 1):
                        dve.wait_ge(lowered, n * G)
                    for j in range(G):
                        if j < D and back(ch, g, 1):
                            take_off(*back(ch, g, 1), 1 - par, j)
                        if ch < BLOCKS:
                            minimum(ch, g, par, n, j)
                        if j == LATE * PART and back(ch, g, 1):
                            dve.wait_ge(alpha_ready, n)
                            dve.wait_ge(total_ready, n)
                            if isinstance(g, int) and g == 1 and ch > 0:
                                dve.wait_ge(log_ready, ch)
                            nc.vector.tensor_tensor(scaled[:], total[par][:], alpha[:], ALU.mult).then_inc(scaled_ready, 1)
                nc.vector.memset(total[1][:], 0.0).then_inc(total_ready, 1)
                each_group(dve, step)
                dve.wait_ge(kept_ready, BLOCKS)
                finish(dve, nc.vector, BLOCKS - 1)

            @block.gpsimd
            def _(pool):
                def group(ch, g, par):
                    n = ch * NG + g
                    pool.wait_ge(lowered, (n + 1) * G)
                    if not isinstance(n, int) or n > 0:
                        pool.wait_ge(alpha_ready, n)
                    if isinstance(g, int) and g == 0:
                        nc.gpsimd.memset(drop[:], -HUGE).then_inc(dropped, 1)
                    else:
                        nc.gpsimd.tensor_tensor(drop[:], neg_max[:, par, :], neg_max[:, 1 - par, :], ALU.subtract)\
                            .then_inc(dropped, 1)
                    for j in range(D, G, PART):
                        part = buf[:, par, j:j + PART, :]
                        nc.gpsimd.tensor_tensor(part, part, neg_max[:, par, :].unsqueeze(1).to_broadcast([P, PART, W]),
                                                ALU.subtract).then_inc(off_pool, 1)

                for ch in range(BLOCKS):
                    group(ch, 0, 0)
                    group(ch, 1, 1)
                    if ch:
                        finish(pool, nc.gpsimd, ch - 1)
                    with pool.Fori(1, NG // 2) as i:
                        for par in range(2):
                            group(ch, 2 * i + par, par)
                    if ch:
                        pool.wait_ge(pieces_ready, ch)
                    nc.gpsimd.tensor_copy(last_neg_max[:], neg_max[:, 1, :]).then_inc(kept_ready, 1)

            @block.tensor
            def _(pe):
                def sums(ch, g, par, first=False, logged=False):
                    n = ch * NG + g
                    for j in range(G):
                        if j < D and j % PART == 0:
                            pe.wait_ge(exped, n * EXPS + j // PART + 1)
                        elif j >= D:
                            pe.wait_ge(exped, n * EXPS + D // PART + j - D + 1)
                        if j == 0 and not first:
                            pe.wait_ge(scaled_ready, n)
                            if logged:
                                pe.wait_ge(log_ready, ch)
                        for w in range(0, W, 512):
                            mm = nc.tensor.matmul(total[par][:, w:w + 512], k["ident"][:], buf[:, par, j, w:w + 512],
                                                  start=j == 0, stop=False)
                        if j % PART == PART - 1:
                            mm.then_inc(summed, 1)
                    pe.wait_ge(scaled_ready, n + 1)
                    for w in range(0, W, 512):
                        mm = nc.tensor.matmul(total[par][:, w:w + 512], k["ident"][:], scaled[:, w:w + 512],
                                              start=False, stop=True)
                    mm.then_inc(total_ready, 1)
                for ch in range(BLOCKS):
                    sums(ch, 0, 0, first=ch == 0)
                    sums(ch, 1, 1, logged=ch > 0)
                    with pe.Fori(1, NG // 2) as i:
                        sums(ch, 2 * i, 0)
                        sums(ch, 2 * i + 1, 1)

            @block.sync
            def _(sp):
                for ch in range(BLOCKS):
                    sp.wait_ge(pieces_ready, ch + 1)
                    for i in range(3):
                        if ch < 2:
                            sp.dma_start(k_pieces[i, 0:P, ch * W:(ch + 1) * W], piece[i][:]).then_inc(stored, 16)
                        else:
                            sp.dma_start(k_pieces[i, P:C, 0:W], piece[i][0:64, :]).then_inc(stored, 16)
                            sp.dma_start(k_pieces[i, P:C, W:N], piece[i][64:P, :]).then_inc(stored, 16)
                sp.wait_ge(stored, 48 * 4)


PAIRS = [(0, 0), (0, 1), (1, 0), (1, 1), (0, 2), (2, 0), (1, 2), (2, 1), (2, 2)]
ROWS = 96


def attend(nc, k, sem, tag, q_pieces, k_pieces, vals, yT, heads, scale, causal=False, sum_factor=1.0, neg_lambda=None):
    hd = C // heads
    subs = heads // NH
    GH = 4 * subs
    pairs = PAIRS[:6] if hd == HD else PAIRS
    U = NC4 * subs
    ES = 2 * subs * TPB
    LEAD = 2
    LOADS = 16 * 2 * len(pairs)
    GROUPS = [(s, kt) for s in range(subs) for kt in range(TPB)]
    HALF = len(GROUPS) // 2

    def step(c, maxima=True, before_last=True, last=True, norm=False, rows=True):
        todo = []

        def part(mx, groups, norm=False, rows=None):
            nonlocal todo
            todo += mx[:LEAD]
            mx = mx[LEAD:]
            if rows:
                todo.append(rows)
            for i, (back, xc, g) in enumerate(groups):
                todo += [("exp", (back, xc, *GROUPS[g], half, 2 * g + half)) for half in range(2)]
                share = -(-len(mx) // (len(groups) - i))
                todo += mx[:share // 2]
                if g > 0:
                    weigh(back, xc, g - 1)
                elif (back, xc) != (0, 0) or norm:
                    weigh(*((back, xc - 1) if xc else (back - 1, NC4 - 1)), len(GROUPS) - 1)
                if norm and i == 0:
                    todo.append(("gather", ()))
                if norm and i == 1:
                    todo += [("spread", (u,)) for u in range(U)]
                todo += mx[share // 2:share]
                mx = mx[share:]
            todo += mx

        def weigh(back, xc, g):
            nonlocal todo
            todo.append(("weigh", (back, xc, *GROUPS[g], g)))
            if GROUPS[g][1] == TPB - 1:
                todo.append(("copy", (back, xc, GROUPS[g][0])))
        mx = [("max", (c, l, qt)) for l in range(GH) for qt in range(TPB)] if maxima else []
        two, one = [(-1, 1), (-1, 2), (0, 0)][c], [(-1, 2), (0, 0), (0, 1)][c]
        part(mx[:len(mx) // 2], [(*two, g) for g in range(HALF, 2 * HALF)] if before_last else [],
             rows=("rows", (0, c - 1) if c else (-1, NC4 - 1)) if rows else None)
        part(mx[len(mx) // 2:], [(*one, g) for g in range(HALF)] if last else [], norm)
        if maxima:
            todo.append(("pieces", (c,)))
        if not last:
            if before_last:
                weigh(*two, len(GROUPS) - 1)
                todo += [("gather", ())] + [("spread", (u,)) for u in range(U)]
        return todo

    def numbered(events):
        out, n = [], 0
        for what, args in events:
            out.append((what, args, n))
            n += what in ("max", "rows", "gather", "spread")
        return out, n
    first, n_first = numbered(step(0, before_last=False, last=False, rows=False) + step(1, before_last=False) + step(2))
    middle, n_middle = numbered(step(0) + step(1, norm=True) + step(2))
    after, _ = numbered(step(0, maxima=False) + step(1, maxima=False, last=False, rows=False))

    def base(b):
        return 0 if isinstance(b, int) and b == 0 else b * n_middle - (n_middle - n_first)

    def number_of(events, what, *args):
        return next(n for w, a_, n in events if w == what and a_ == args)

    def ge(eng, s, value):
        if not isinstance(value, int) or value > 0:
            eng.wait_ge(s, value)

    def each_sequence(engine, run):
        run(0, first)
        with engine.Fori(1, B) as b:
            run(b, middle)
        run(B, after)

    def exp_base(b, back, c):
        return 3 * b * ES + (3 * back + c) * ES

    def q_from(kt):
        return kt * P if causal else 0

    def k_to(qt):
        return (qt + 1) * P if causal else S
    with ExitStack() as cx:
        def sb(name, shape, dt=F32):
            return cx.enter_context(nc.sbuf_tensor(tag + name, shape, dt))
        qs = sb("qs", [ROWS + 3, heads, S], BF16)
        ks = sb("ks", [ROWS + 3, heads, S], BF16)
        vb = sb("vb", [P, TPB, VW])
        pt = sb("pt", [P, 4, 2, S])
        top = sb("top", [P, TPB, GH])
        rest = sb("rest", [P, TPB, GH])
        top_all = sb("top_all", [P, TPB, P], BF16)
        top_pieces = top_all[:, :, 0:3 * GH].rearrange("p t (i h) -> p t i h", i=3)
        top_rows = sb("top_rows", [3 * GH, S], BF16)
        ctx_sb = sb("ctx_sb", [P, U, S])
        recip = sb("recip", [4 * U, S])
        gather_sel = sb("gather_sel", [P, 8 * U - 4])
        spread_sel = sb("spread_sel", [4 * U, U, P])
        exp_slot = [cx.enter_context(nc.psum_tensor(f"{tag}exp_slot{i}", [P, 2, S], F32)) for i in range(2)]
        dve_slot = [cx.enter_context(nc.psum_tensor(f"{tag}dve_slot{i}", [P, S], F32)) for i in range(2)]
        ctx = [cx.enter_context(nc.psum_tensor(f"{tag}ctx{i}", [P, S], F32)) for i in range(2)]
        cleared, q_cleared, selected = sem(tag + "cleared"), sem(tag + "q_cleared"), sem(tag + "selected")
        for_exp, probs_ready, probs_used = sem(tag + "for_exp"), sem(tag + "probs_ready"), sem(tag + "probs_used")
        for_dve, emptied = sem(tag + "for_dve"), sem(tag + "emptied")
        loaded = [sem(f"{tag}loaded{c}") for c in range(NC4)]
        vb_ready, top_ready, rows_in = sem(tag + "vb_ready"), sem(tag + "top_ready"), sem(tag + "rows_in")
        ctx_copied, normed, chain = sem(tag + "ctx_copied"), sem(tag + "normed"), sem(tag + "chain")
        with nc.Block() as block:
            @block.sync
            def _(sp):
                def load(b, c):
                    if not isinstance(b, int) or b > 0:
                        sp.wait_ge(for_exp, 3 * b * ES + (c + 1 - 3) * ES)
                    for i, (qp, kp) in enumerate(pairs):
                        for dst, src, p in ((qs, q_pieces, qp), (ks, k_pieces, kp)):
                            sp.dma_start(dst[i * hd:(i + 1) * hd, c * GH:(c + 1) * GH, :],
                                         src[p, c * 64:(c + 1) * 64, bass.ds(b * S, S)].rearrange("(h d) t -> d h t", d=hd))\
                                .then_inc(loaded[c], 16)

                def rows(b, c, events, following):
                    if c < NC4 - 1:
                        sp.wait_ge(emptied, base(b) + (number_of(events, "rows", 0, c) + 1))
                    else:
                        sp.wait_ge(emptied, base(b + 1) + (number_of(following, "rows", -1, c) + 1))
                    sp.dma_start(qs[ROWS:ROWS + 3, c * GH:(c + 1) * GH, :], top_rows[:]).then_inc(rows_in, 16)
                for c in range(NC4):
                    sp.wait_ge(cleared, c + 1)
                    sp.wait_ge(q_cleared, c + 1)
                    load(0, c)
                rows(0, 0, first, middle)
                rows(0, 1, first, middle)
                load(1, 0)
                rows(0, 2, first, middle)
                load(1, 1)
                with sp.Fori(1, B - 1) as b:
                    rows(b, 0, middle, middle)
                    load(b, 2)
                    rows(b, 1, middle, middle)
                    load(b + 1, 0)
                    rows(b, 2, middle, middle)
                    load(b + 1, 1)
                rows(B - 1, 0, middle, after)
                load(B - 1, 2)
                rows(B - 1, 1, middle, after)
                rows(B - 1, 2, middle, after)

            @block.gpsimd
            def _(pool):
                for c in range(NC4):
                    nc.gpsimd.memset(ks[:, c * GH:(c + 1) * GH, :], 1.0).then_inc(cleared, 1)
                nc.gpsimd.memset(top_all[:], 0.0)
                nc.gpsimd.memset(gather_sel[:], 0.0)
                nc.gpsimd.memset(spread_sel[:], 0.0).then_inc(selected, 1)
                pool.wait_ge(selected, 1)
                sums = gather_sel[:, 4 * U - 4:4 * U]
                nc.gpsimd.affine_select(out=sums, in_=sums, pattern=[[-VP, 4]], compare_op=ALU.not_equal, fill=sum_factor,
                                        base=-HD, channel_multiplier=1)
                back = spread_sel[:].rearrange("p u (j e) -> p u j e", j=4)
                nc.gpsimd.affine_select(out=back, in_=back, pattern=[[-4, U], [-1, 4], [0, VP]], compare_op=ALU.not_equal,
                                        fill=1.0, base=0, channel_multiplier=1).then_inc(selected, 1)

                def take(b, c, later=True):
                    if later:
                        pool.wait_ge(probs_used, 3 * b * ES + (c + 1 - 3) * ES)
                    cols = slice(c * P, (c + 1) * P)
                    nc.gpsimd.tensor_copy(vb[:, :, cols], vals[:, bass.ds(b * TPB, TPB), cols]).then_inc(vb_ready, 1)
                for c in range(NC4):
                    take(0, c, later=False)
                with pool.Fori(1, B) as b:
                    for c in range(NC4):
                        take(b, c)

            @block.tensor
            def _(pe):
                def run(b, events):
                    for what, args, n in events:
                        if what in ("max", "rows", "gather", "spread"):
                            out = dve_slot[n % 2]
                            ge(pe, emptied, base(b) + (n - 1 if n else 0))
                        if what == "max":
                            c, l, qt = args
                            if (l, qt) == (0, 0):
                                pe.wait_ge(loaded[c], b * LOADS + LOADS)
                            hh = c * GH + l
                            mm = nc.tensor.matmul(out[:, 0:k_to(qt)], qs[0:ROWS, hh, qt * P:(qt + 1) * P],
                                                  ks[0:ROWS, hh, 0:k_to(qt)], start=True, stop=not causal)
                            if causal:
                                mm = nc.tensor.matmul(out[:, qt * P:(qt + 1) * P], k["identb"][:], k["mask_qk"][:],
                                                      start=False, stop=True)
                            mm.then_inc(for_dve, 1)
                        elif what == "rows":
                            pe.wait_ge(top_ready, 3 * b + (3 * args[0] + args[1] + 1))
                            for qt in range(TPB):
                                mm = nc.tensor.transpose(out[:].bitcast(BF16)[:, qt * P:(qt + 1) * P], top_all[:, qt, :],
                                                         k["identb"][:])
                            mm.then_inc(for_dve, 1)
                        elif what == "gather":
                            pe.wait_ge(ctx_copied, b * U)
                            for u in range(U):
                                mm = nc.tensor.matmul(out[0:4 * U, :], gather_sel[:, 4 * (U - 1 - u):4 * (2 * U - 1 - u)],
                                                      ctx_sb[:, u, :], start=u == 0, stop=u == U - 1)
                            mm.then_inc(for_dve, 1)
                        elif what == "spread":
                            u, = args
                            if u == 0:
                                pe.wait_ge(emptied, base(b) + n)
                            nc.tensor.matmul(out[:], spread_sel[:, u, :], recip[:], start=True, stop=True)\
                                .then_inc(for_dve, 1)
                        elif what == "exp":
                            back, c, s, kt, half, e = args
                            if e == 0:
                                pe.wait_ge(rows_in, 16 * (3 * b + (3 * back + c + 1)))
                            ge(pe, probs_ready, exp_base(b, back, c) + (e - 1))
                            lo = q_from(kt)
                            for i in range(2):
                                hh = (4 * c + 2 * half + i) * subs + s
                                mm = nc.tensor.matmul(exp_slot[e % 2][:, i, lo:S], ks[:, hh, kt * P:(kt + 1) * P],
                                                      qs[:, hh, lo:S], start=True, stop=not causal)
                                if causal:
                                    mm = nc.tensor.matmul(exp_slot[e % 2][:, i, lo:lo + P], k["identb"][:],
                                                          k["mask_kq"][:], start=False, stop=True)
                            mm.then_inc(for_exp, 1)
                        elif what == "weigh":
                            back, c, s, kt, i = args
                            u = c * subs + s
                            if kt == 0:
                                ge(pe, ctx_copied, b * U + (back * U + (u - 1 if u else 0)))
                            if (s, kt) == (0, 0):
                                pe.wait_ge(vb_ready, 3 * b + (3 * back + c + 1))
                            lo = q_from(kt)
                            for half in range(2):
                                e = 2 * i + half
                                pe.wait_ge(probs_ready, exp_base(b, back, c) + (e + 1))
                                for j in (2 * half, 2 * half + 1):
                                    mm = nc.tensor.matmul(ctx[u % 2][VP * j:VP * j + VP, lo:S],
                                                          vb[:, kt, (4 * c + j) * VP:(4 * c + j + 1) * VP],
                                                          pt[:, e % 4, j % 2, lo:S], start=kt == 0, stop=kt == TPB - 1)
                                mm.then_inc(probs_used, 1)
                pe.wait_ge(selected, 2)
                each_sequence(pe, run)

            @block.scalar
            def _(act):
                def run(b, events):
                    for what, args, n in events:
                        if what == "exp":
                            back, c, s, kt, half, e = args
                            lo = q_from(kt)
                            act.wait_ge(for_exp, exp_base(b, back, c) + (e + 1))
                            ge(act, probs_used, exp_base(b, back, c) + (e - 3))
                            nc.scalar.activation(pt[:, e % 4, :, lo:S], exp_slot[e % 2][:, :, lo:S], ACT.Exp, scale=scale)\
                                .then_inc(probs_ready, 1)
                each_sequence(act, run)

            @block.vector
            def _(dve):
                def run(b, events):
                    links = 0

                    def linked(ins, step):
                        nonlocal links
                        links += 1
                        ins.then_inc(chain, 1)
                        dve.wait_ge(chain, (3 * b + step) * 4 + links % 4 if links % 4 else (3 * b + step + 1) * 4)
                    for what, args, n in events:
                        if what in ("max", "rows", "gather", "spread"):
                            dve.wait_ge(for_dve, base(b) + (n + 1))
                        if what == "max":
                            c, l, qt = args
                            nc.vector.tensor_reduce(top[:, qt, l:l + 1], dve_slot[n % 2][:, 0:k_to(qt)], axis=AX.X,
                                                    op=ALU.max).then_inc(emptied, 1)
                        elif what == "pieces":
                            dve.wait_ge(emptied, base(b) + n)
                            c, = args
                            linked(nc.vector.tensor_scalar(top[:], top[:], -1.0, None, ALU.mult), c)
                            linked(nc.vector.tensor_copy(top_pieces[:, :, 0, :], top[:]), c)
                            linked(nc.vector.tensor_tensor(rest[:], top[:], top_pieces[:, :, 0, :], ALU.subtract), c)
                            linked(nc.vector.tensor_copy(top_pieces[:, :, 1, :], rest[:]), c)
                            nc.vector.tensor_tensor(top_pieces[:, :, 2, :], rest[:], top_pieces[:, :, 1, :], ALU.subtract)\
                                .then_inc(top_ready, 1)
                        elif what == "rows":
                            ge(dve, rows_in, 16 * (3 * b + (3 * args[0] + args[1])))
                            nc.vector.tensor_copy(top_rows[:], dve_slot[n % 2][0:3 * GH, :].bitcast(BF16)[:, 0:S])\
                                .then_inc(emptied, 1)
                        elif what == "copy":
                            back, c, s = args
                            u = c * subs + s
                            dve.wait_ge(probs_used, exp_base(b, back, c) + (s + 1) * (ES // subs))
                            if events is middle and (back, c, s) == (0, 0, 0):
                                dve.wait_ge(emptied, base(b) + (number_of(events, "spread", U - 1) + 1))
                                if subs == 2:
                                    dve.wait_ge(normed, b * NC4)
                            nc.vector.tensor_copy(ctx_sb[:, u, :], ctx[u % 2][:]).then_inc(ctx_copied, 1)
                        elif what == "gather":
                            dve.wait_ge(ctx_copied, b * U)
                            nc.vector.reciprocal(recip[:], dve_slot[n % 2][0:4 * U, :]).then_inc(emptied, 1)
                        elif what == "spread":
                            u, = args
                            c, s = u // subs, u % subs
                            out = yT[:, c, bass.ds(b * S - S, S)]
                            if subs == 1:
                                nc.vector.tensor_tensor(out, ctx_sb[:, u, :], dve_slot[n % 2][:], ALU.mult).then_inc(emptied, 1)
                                continue
                            nc.vector.tensor_tensor(ctx_sb[:, u, :], ctx_sb[:, u, :], dve_slot[n % 2][:], ALU.mult)\
                                .then_inc(emptied, 1)
                            if s == 1:
                                dve.wait_ge(emptied, base(b) + (n + 1))
                                nc.vector.scalar_tensor_tensor(out=out, in0=ctx_sb[:, u, :], scalar=neg_lambda[:],
                                                               in1=ctx_sb[:, u - 1, :], op0=ALU.mult, op1=ALU.add)\
                                    .then_inc(normed, 1)
                for c in range(NC4):
                    nc.vector.memset(qs[:, c * GH:(c + 1) * GH, :], 0.0).then_inc(q_cleared, 1)
                each_sequence(dve, run)


def attention_lambda(nc, sem, d, neg_lambda, init):
    W = C // NH // 2
    with ExitStack() as cx:
        vecs = cx.enter_context(nc.sbuf_tensor("la_vecs", [P, 4, W], F32))
        prod = cx.enter_context(nc.sbuf_tensor("la_prod", [P, 2, W], F32))
        dots = cx.enter_context(nc.sbuf_tensor("la_dots", [P, 2], F32))
        exps = cx.enter_context(nc.sbuf_tensor("la_exps", [P, 2], F32))
        diff = cx.enter_context(nc.sbuf_tensor("la_diff", [P, 1], F32))
        vecs_in, chain, dots_ready, exps_ready = sem("la_vecs_in"), sem("la_chain"), sem("la_dots_ready"), sem("la_exps_ready")
        with nc.Block() as block:
            @block.sync
            def _(sp):
                for i in range(4):
                    sp.dma_start(vecs[:, i, :], d["lambdas"][i, :].partition_broadcast(P)).then_inc(vecs_in, 16)

            @block.scalar
            def _(act):
                act.wait_ge(dots_ready, 1)
                nc.scalar.activation(exps[:], dots[:], ACT.Exp).then_inc(exps_ready, 1)

            @block.vector
            def _(dve):
                n = [0]
                dve.wait_ge(vecs_in, 64)
                link(dve, chain, n, nc.vector.tensor_tensor(prod[:], vecs[:, 0:2, :], vecs[:, 2:4, :], ALU.mult))
                nc.vector.tensor_reduce(dots[:], prod[:], axis=AX.X, op=ALU.add).then_inc(dots_ready, 1)
                dve.wait_ge(exps_ready, 1)
                link(dve, chain, n, nc.vector.tensor_tensor(diff[:], exps[:, 1:2], exps[:, 0:1], ALU.subtract))
                nc.vector.tensor_scalar(neg_lambda[:], diff[:], -init, None, ALU.add)


def head_rms(nc, k, sem, d, yT, factor):
    items = [(c, b) for c in range(NC4) for b in range(B)]
    R = 4 * len(items)
    with ExitStack() as cx:
        def sb(name, shape, dt=F32):
            return cx.enter_context(nc.sbuf_tensor("hr_" + name, shape, dt))
        weight = sb("weight", [P, 1])
        eps = sb("eps", [P, 1])
        square = sb("square", [P, 2, S])
        root = sb("root", [R, S])
        recip = sb("recip", [R, S])
        gather_sel = sb("gather_sel", [P, 2 * R - 4])
        spread_sel = sb("spread_sel", [R, len(items), P])
        means = cx.enter_context(nc.psum_tensor("hr_means", [R, S], F32))
        slot = [cx.enter_context(nc.psum_tensor(f"hr_slot{i}", [P, S], F32)) for i in range(2)]
        weight_in, cleared, weight_ready, selected = (sem("hr_" + x) for x in (
            "weight_in", "cleared", "weight_ready", "selected"))
        square_ready, gathered, root_ready, recip_ready, spread, done = (sem("hr_" + x) for x in (
            "square_ready", "gathered", "root_ready", "recip_ready", "spread", "done"))
        with nc.Block() as block:
            @block.sync
            def _(sp):
                sp.wait_ge(cleared, 1)
                for j in range(4):
                    sp.dma_start(weight[VP * j:VP * j + HD, :], d["subln"]).then_inc(weight_in, 16)

            @block.gpsimd
            def _(pool):
                nc.gpsimd.memset(spread_sel[:], 0.0)
                nc.gpsimd.memset(gather_sel[:, 0:R - 4], 0.0)
                nc.gpsimd.memset(gather_sel[:, R:], 0.0)
                nc.gpsimd.tensor_copy(gather_sel[:, R - 4:R], k["sel_mean"][:].rearrange("p (j e) -> p j e", j=4)[:, :, 0])\
                    .then_inc(selected, 1)
                pool.wait_ge(selected, 1)
                back = spread_sel[:].rearrange("p n (j e) -> p n j e", j=4)
                nc.gpsimd.affine_select(out=back, in_=back, pattern=[[-4, len(items)], [-1, 4], [0, VP]],
                                        compare_op=ALU.not_equal, fill=1.0, base=0, channel_multiplier=1)\
                    .then_inc(selected, 1)

            @block.vector
            def _(dve):
                nc.vector.memset(eps[:], EPS)
                nc.vector.memset(weight[:], 0.0).then_inc(cleared, 1)
                for n, (c, b) in enumerate(items):
                    part = yT[:, c, b * S:(b + 1) * S]
                    if n >= 2:
                        dve.wait_ge(gathered, n - 1)
                    nc.vector.tensor_tensor(square[:, n % 2, :], part, part, ALU.mult).then_inc(square_ready, 1)
                dve.wait_ge(weight_in, 64)
                nc.vector.tensor_scalar(weight[:], weight[:], factor, None, ALU.mult).then_inc(weight_ready, 1)
                dve.wait_ge(root_ready, 1)
                nc.vector.reciprocal(recip[:], root[:]).then_inc(recip_ready, 1)
                dve.wait_ge(weight_ready, 1)
                for n, (c, b) in enumerate(items):
                    part = yT[:, c, b * S:(b + 1) * S]
                    dve.wait_ge(spread, n + 1)
                    nc.vector.scalar_tensor_tensor(out=part, in0=part, scalar=weight[:], in1=slot[n % 2][:],
                                                   op0=ALU.mult, op1=ALU.mult).then_inc(done, 1)

            @block.tensor
            def _(pe):
                pe.wait_ge(selected, 2)
                last = len(items) - 1
                for n in range(len(items)):
                    pe.wait_ge(square_ready, n + 1)
                    nc.tensor.matmul(means[:], gather_sel[:, R - 4 - 4 * n:2 * R - 4 - 4 * n], square[:, n % 2, :],
                                     start=n == 0, stop=n == last).then_inc(gathered, 1)
                pe.wait_ge(recip_ready, 1)
                for n in range(len(items)):
                    if n >= 2:
                        pe.wait_ge(done, n - 1)
                    nc.tensor.matmul(slot[n % 2][:], spread_sel[:, n, :], recip[:], start=True, stop=True).then_inc(spread, 1)

            @block.scalar
            def _(act):
                act.wait_ge(cleared, 1)
                act.wait_ge(gathered, len(items))
                nc.scalar.activation(root[:], means[:], ACT.Sqrt, bias=eps[0:R, :]).then_inc(root_ready, 1)


def project_out(nc, k, sem, tag, d, yT, resid, out):
    with ExitStack() as cx:
        def sb(name, shape, dt=F32):
            return cx.enter_context(nc.sbuf_tensor(tag + name, shape, dt))
        wo = sb("wo", [P, NC4, C])
        bo = sb("bo", [P, C])
        base = sb("base", [P, NT, C])
        slot = [cx.enter_context(nc.psum_tensor(f"{tag}slot{i}", [P, 512], F32)) for i in range(2)]
        cleared, bias_in, weights_in, based = sem(tag + "cleared"), sem(tag + "bias_in"), sem(tag + "weights_in"), sem(tag + "based")
        projected, added = sem(tag + "projected"), sem(tag + "added")
        with nc.Block() as block:
            @block.sync
            def _(sp):
                sp.dma_start(bo[:], d["bo"].partition_broadcast(P)).then_inc(bias_in, 16)
                sp.wait_ge(cleared, 1)
                for j in range(4):
                    sp.dma_start(wo[VP * j:VP * j + HD, :, :], d["Wo"].rearrange("(c j e) n -> j e c n", j=4, e=HD)[j])\
                        .then_inc(weights_in, 16)

            @block.gpsimd
            def _(pool):
                nc.gpsimd.memset(wo[:], 0.0).then_inc(cleared, 1)

            @block.vector
            def _(dve):
                dve.wait_ge(bias_in, 16)
                nc.vector.tensor_tensor(base[:], resid[:], bo[:].unsqueeze(1).to_broadcast([P, NT, C]), ALU.add)\
                    .then_inc(based, 1)
                dve.wait_ge(based, 1)
                for t in range(NT):
                    dve.wait_ge(projected, t + 1)
                    nc.vector.tensor_tensor(out[:, t, :], slot[t % 2][:, 0:C], base[:, t, :], ALU.add).then_inc(added, 1)

            @block.tensor
            def _(pe):
                pe.wait_ge(weights_in, 64)
                for t in range(NT):
                    if t >= 2:
                        pe.wait_ge(added, t - 1)
                    for c in range(NC4):
                        mm = nc.tensor.matmul(slot[t % 2][:, 0:C], yT[:, c, t * P:(t + 1) * P], wo[:, c, :],
                                              start=c == 0, stop=c == NC4 - 1)
                    mm.then_inc(projected, 1)


def route(nc, k, sem, tag, d, x, xT, E, K, capacity, tiles, slot_put, slot_get, weight, comb, tile_expert, rows_in, zero_tiles):
    G = K if capacity else 1
    NE = NT * E
    with ExitStack() as cx:
        def sb(name, shape, dt=F32):
            return cx.enter_context(nc.sbuf_tensor(tag + name, shape, dt))
        wg = sb("wg", [HC, 2, E])
        bg = sb("bg", [P, E])
        zeros = sb("zeros", [P, zero_tiles, C])
        io_e = sb("io_e", [P, E])
        io_128 = sb("io_128", [P, NT])
        io_tile = sb("io_tile", [P, tiles])
        logit = sb("logit", [P, NT, E])
        best = sb("best", [P, K, NT])
        same = sb("same", [P, NT, E])
        key = sb("key", [P, NT, E])
        least = sb("least", [P, NT])
        hot = sb("hot", [P, K, NT, E])
        counted = sb("counted", [P, G, NT, E])
        tot = sb("tot", [P, G, NT, E])
        run = [sb(f"run{i}", [P, G, NT, E]) for i in range(2)]
        rank = sb("rank", [P, G, NT, E])
        prod = sb("prod", [P, K, NT, E])
        prod2 = sb("prod2", [P, K, NT, E])
        over = sb("over", [P, E, NT])
        padded = sb("padded", [P, E])
        end = [sb(f"end{i}", [P, E]) for i in range(2)]
        start = sb("start", [P, E])
        past = sb("past", [P, tiles, E])
        tile_f = sb("tile_f", [P, tiles])
        rank_k = sb("rank_k", [P, K, NT])
        slot_k = sb("slot_k", [P, K, NT])
        valid = sb("valid", [P, K, NT])
        put_f = sb("put_f", [P, K, NT])
        gap = sb("gap", [P, K, NT])
        expo = sb("expo", [P, K, NT])
        sumexp = sb("sumexp", [P, NT])
        inv = sb("inv", [P, NT])
        acc_logit = cx.enter_context(nc.psum_tensor(tag + "acc_logit", [P, 512], F32))
        acc_before = cx.enter_context(nc.psum_tensor(tag + "acc_before", [P, 512], F32))
        acc_total = cx.enter_context(nc.psum_tensor(tag + "acc_total", [P, 512], F32))
        loads, iotas, zeroed, filled = sem(tag + "loads"), sem(tag + "iotas"), sem(tag + "zeroed"), sem(tag + "filled")
        logits_ready, chain, counted_ready, counts_ready, gap_ready, expo_ready = (sem(tag + x) for x in (
            "logits_ready", "chain", "counted_ready", "counts_ready", "gap_ready", "expo_ready"))
        with nc.Block() as block:
            @block.sync
            def _(sp):
                sp.dma_start(wg[:], d["wg"]).then_inc(loads, 16)
                if "bg" in d:
                    sp.dma_start(bg[:], d["bg"].partition_broadcast(P)).then_inc(loads, 16)
                sp.wait_ge(zeroed, 1)
                for i in range(tiles // zero_tiles):
                    part = rows_in[i * zero_tiles * P:(i + 1) * zero_tiles * P, :]
                    sp.dma_start(part.rearrange("(a p) c -> p a c", p=P), zeros[:]).then_inc(filled, 16)
                sp.wait_ge(filled, 16 * (tiles // zero_tiles))

            @block.gpsimd
            def _(pool):
                nc.gpsimd.memset(zeros[:], 0.0).then_inc(zeroed, 1)
                nc.gpsimd.iota(io_e[:], pattern=[[1, E]], base=0, channel_multiplier=0, allow_small_or_imprecise_dtypes=True)
                nc.gpsimd.iota(io_128[:], pattern=[[P, NT]], base=0, channel_multiplier=0,
                               allow_small_or_imprecise_dtypes=True)
                nc.gpsimd.iota(io_tile[:], pattern=[[P, tiles]], base=0, channel_multiplier=0,
                               allow_small_or_imprecise_dtypes=True).then_inc(iotas, 1)

            @block.tensor
            def _(pe):
                pe.wait_ge(loads, 32 if "bg" in d else 16)
                for t in range(NT):
                    for c in range(2):
                        mm = nc.tensor.matmul(acc_logit[:, t * E:(t + 1) * E], xT[0:HC, c, t * P:(t + 1) * P], wg[:, c, :],
                                              start=c == 0, stop=c == 1)
                mm.then_inc(logits_ready, 1)
                pe.wait_ge(counted_ready, 1)
                cols = counted[:].rearrange("p g t e -> p (g t e)")
                nc.tensor.matmul(acc_before[:, 0:G * NE], k["before"][:], cols, start=True, stop=True)
                nc.tensor.matmul(acc_total[:, 0:G * NE], k["ones"][:], cols, start=True, stop=True).then_inc(counts_ready, 1)

            @block.scalar
            def _(act):
                act.wait_ge(gap_ready, 1)
                nc.scalar.activation(expo[:], gap[:], ACT.Exp).then_inc(expo_ready, 1)

            @block.vector
            def _(dve):
                n = [0]
                V = nc.vector

                def do(ins):
                    link(dve, chain, n, ins)
                whole = [P, NT, E]

                def over_e(a):
                    return a.unsqueeze(2).to_broadcast(whole)
                dve.wait_ge(iotas, 1)
                dve.wait_ge(logits_ready, 1)
                psum = acc_logit[:, 0:NE].rearrange("p (t e) -> p t e", e=E)
                if "bg" in d:
                    do(V.tensor_tensor(logit[:], psum, bg[:].unsqueeze(1).to_broadcast(whole), ALU.add))
                else:
                    do(V.tensor_copy(logit[:], psum))
                for j in range(K):
                    do(V.tensor_reduce(best[:, j, :], logit[:], axis=AX.X, op=ALU.max))
                    do(V.tensor_tensor(same[:], logit[:], over_e(best[:, j, :]), ALU.is_equal))
                    do(V.scalar_tensor_tensor(out=key[:], in0=same[:], scalar=-64.0,
                                              in1=io_e[:].unsqueeze(1).to_broadcast(whole), op0=ALU.mult, op1=ALU.add))
                    do(V.tensor_reduce(least[:], key[:], axis=AX.X, op=ALU.min))
                    do(V.tensor_tensor(hot[:, j], key[:], over_e(least[:]), ALU.is_equal))
                    if j < K - 1:
                        do(V.scalar_tensor_tensor(out=logit[:], in0=hot[:, j], scalar=-3e38, in1=logit[:],
                                                  op0=ALU.mult, op1=ALU.add))
                if capacity:
                    V.tensor_copy(counted[:], hot[:]).then_inc(counted_ready, 1)
                else:
                    do(V.tensor_tensor(same[:], hot[:, 0], hot[:, 1], ALU.add))
                    do(V.tensor_tensor(key[:], hot[:, 2], hot[:, 3], ALU.add))
                    V.tensor_tensor(counted[:, 0], same[:], key[:], ALU.add).then_inc(counted_ready, 1)
                for j in range(K):
                    last = V.tensor_tensor(gap[:, j], best[:, j], best[:, 0], ALU.subtract)
                last.then_inc(gap_ready, 1)
                dve.wait_ge(expo_ready, 1)
                do(V.tensor_reduce(sumexp[:], expo[:].rearrange("p k t -> p t k"), axis=AX.X, op=ALU.add))
                do(V.reciprocal(inv[:], sumexp[:]))
                do(V.tensor_tensor(weight[:], expo[:], inv[:].unsqueeze(1).to_broadcast([P, K, NT]), ALU.mult))
                dve.wait_ge(counts_ready, 1)
                grid = "p (g t e) -> p g t e"
                do(V.tensor_copy(tot[:], acc_total[:, 0:G * NE].rearrange(grid, g=G, t=NT)))
                do(V.tensor_copy(run[0][:], tot[:]))
                a, b = run
                for s in (1, 2, 4, 8):
                    do(V.tensor_copy(b[:, :, 0:s, :], a[:, :, 0:s, :]))
                    do(V.tensor_tensor(b[:, :, s:NT, :], a[:, :, s:NT, :], a[:, :, 0:NT - s, :], ALU.add))
                    a, b = b, a
                do(V.tensor_tensor(rank[:], a[:], tot[:], ALU.subtract))
                do(V.tensor_tensor(rank[:], rank[:], acc_before[:, 0:G * NE].rearrange(grid, g=G, t=NT), ALU.add))
                if capacity:
                    do(V.tensor_tensor(rank[:, 1], rank[:, 1], a[:, 0, NT - 1, :].unsqueeze(1).to_broadcast(whole), ALU.add))
                    do(V.tensor_scalar(start[:], io_e[:], float(capacity), None, ALU.mult))
                    do(V.tensor_scalar(end[0][:], start[:], float(capacity), None, ALU.add))
                    last_end = end[0]
                else:
                    count = a[:, 0, NT - 1, :].unsqueeze(2).to_broadcast([P, E, NT])
                    do(V.tensor_tensor(over[:], count, io_128[:].unsqueeze(1).to_broadcast([P, E, NT]), ALU.is_gt))
                    do(V.tensor_reduce(padded[:], over[:], axis=AX.X, op=ALU.add))
                    do(V.tensor_scalar(padded[:], padded[:], float(P), None, ALU.mult))
                    do(V.tensor_copy(end[0][:], padded[:]))
                    u, v = end
                    for s in (1, 2, 4, 8):
                        do(V.tensor_copy(v[:, 0:s], u[:, 0:s]))
                        do(V.tensor_tensor(v[:, s:E], u[:, s:E], u[:, 0:E - s], ALU.add))
                        u, v = v, u
                    last_end = u
                    do(V.tensor_tensor(start[:], last_end[:], padded[:], ALU.subtract))
                do(V.tensor_tensor(past[:], last_end[:].unsqueeze(1).to_broadcast([P, tiles, E]),
                                   io_tile[:].unsqueeze(2).to_broadcast([P, tiles, E]), ALU.is_le))
                do(V.tensor_reduce(tile_f[:], past[:], axis=AX.X, op=ALU.add))
                do(V.tensor_scalar(tile_f[:], tile_f[:], float(E - 1), None, ALU.min))
                do(V.tensor_copy(tile_expert[:], tile_f[:]))
                for j in range(K):
                    g = j if capacity else 0
                    do(V.tensor_tensor(prod[:, j], hot[:, j], rank[:, g], ALU.mult))
                    do(V.tensor_tensor(prod2[:, j], hot[:, j], start[:].unsqueeze(1).to_broadcast(whole), ALU.mult))
                do(V.tensor_reduce(rank_k[:], prod[:], axis=AX.X, op=ALU.add))
                do(V.tensor_reduce(slot_k[:], prod2[:], axis=AX.X, op=ALU.add))
                do(V.tensor_tensor(slot_k[:], slot_k[:], rank_k[:], ALU.add))
                if capacity:
                    do(V.tensor_scalar(valid[:], rank_k[:], float(capacity), None, ALU.is_lt))
                    do(V.tensor_tensor(weight[:], weight[:], valid[:], ALU.mult))
                    do(V.tensor_scalar(put_f[:], valid[:], float(-tiles * P), float(tiles * P), ALU.mult, ALU.add))
                    do(V.tensor_tensor(put_f[:], put_f[:], slot_k[:], ALU.add))
                    do(V.tensor_tensor(slot_k[:], slot_k[:], valid[:], ALU.mult))
                    do(V.tensor_copy(slot_put[:], put_f[:]))
                else:
                    do(V.tensor_copy(slot_put[:], slot_k[:]))
                do(V.tensor_copy(slot_get[:], slot_k[:]))
                do(V.tensor_tensor(comb[:], hot[:, 0], over_e(weight[:, 0]), ALU.mult))
                for j in range(1, K):
                    do(V.tensor_tensor(prod[:, j], hot[:, j], over_e(weight[:, j]), ALU.mult))
                    do(V.tensor_tensor(comb[:], comb[:], prod[:, j], ALU.add))


def dispatch(nc, sem, tag, x, K, slot_put, rows_in, total):
    sent = sem(tag + "sent")
    with nc.Block() as block:
        @block.gpsimd
        def _(pool):
            for t in range(NT):
                for j in range(K):
                    pool.indirect_dma_start(out=rows_in, out_offset=bass.IndirectOffsetOnAxis(ap=slot_put[:, j, t:t + 1], axis=0),
                                            in_=x[:, t, :], in_offset=None, bounds_check=total - 1, oob_is_err=False)\
                        .then_inc(sent, 16)
            pool.wait_ge(sent, 16 * NT * K)


def experts(nc, k, sem, tag, d, E, F, A, swiglu, tiles, tile_expert, rows_in, rows_out, w1, w2, weights_in, load_w2):
    AC = A // P
    FH = F // 2
    LIMIT, ALPHA = 7.0, 1.702
    with ExitStack() as cx:
        def sb(name, shape, dt=F32):
            return cx.enter_context(nc.sbuf_tensor(tag + name, shape, dt))

        def ps(name, shape, dt=F32):
            return cx.enter_context(nc.psum_tensor(tag + name, shape, dt))
        w1_flat = w1[:].rearrange("p e c f -> p (e c f)")
        w2_flat = w2[:].rearrange("p e c f -> p (e c f)")
        xr = sb("xr", [P, 2, C])
        xrT = sb("xrT", [HC + 1, 2, 2, P])
        act_sb = sb("act_sb", [P, 2, A])
        glu = sb("glu", [P, 2, A]) if swiglu else None
        lin = sb("lin", [P, 2, A]) if swiglu else None
        gate = sb("gate", [P, 2, A]) if swiglu else None
        actT = sb("actT", [P, 2, AC, P])
        y = sb("y", [P, 2, C])
        xt_ps = ps("xt_ps", [P, 512])
        hid = [ps(f"hid{i}", [P, 2, 512]) for i in range(2)]
        at_ps = ps("at_ps", [P, AC * P if AC * P > 512 else 512])
        y_ps = ps("y_ps", [P, 512])
        ones_set, row_in = sem(tag + "ones_set"), [sem(f"{tag}row_in{i}") for i in range(2)]
        x_turned, x_moved, hid_ready, glu_ready, gate_ready, act_ready = (sem(tag + x) for x in (
            "x_turned", "x_moved", "hid_ready", "glu_ready", "gate_ready", "act_ready"))
        lin_ready, mix_ready, a_turned, a_moved, y_ready, y_moved = (sem(tag + x) for x in (
            "lin_ready", "mix_ready", "a_turned", "a_moved", "y_ready", "y_moved"))
        sent = [sem(f"{tag}sent{i}") for i in range(2)]

        def ge(eng, s, value):
            if not isinstance(value, int) or value > 0:
                eng.wait_ge(s, value)

        def steady(eng, body):
            body(1, 1)
            body(2, 0)
            with eng.Fori(1, (tiles - 2) // 2) as p:
                body(2 * p + 1, 1)
                body(2 * p + 2, 0)
        with nc.Block() as block:
            @block.sync
            def _(sp):
                def load(i, par):
                    ge(sp, x_turned, i - 1)
                    sp.dma_start(xr[:, par, :], rows_in[bass.ds(i * P, P), :]).then_inc(row_in[par], 16)

                def store(i, par):
                    sp.wait_ge(y_moved, i + 1)
                    sp.dma_start(rows_out[bass.ds(i * P, P), :], y[:, par, :]).then_inc(sent[par], 16)
                for i in range(2):
                    load(i, i % 2)
                for e in range(E if load_w2 else 0):
                    sp.dma_start(w2[:, e, :, :], d["w2"][e]).then_inc(weights_in, 16)
                for i in range(2, 4):
                    load(i, i % 2)
                with sp.Fori(2, tiles // 2) as p:
                    load(2 * p, 0)
                    store(2 * p - 4, 0)
                    load(2 * p + 1, 1)
                    store(2 * p - 3, 1)
                for i in range(tiles - 4, tiles):
                    store(i, i % 2)
                for par in range(2):
                    sp.wait_ge(sent[par], 16 * (tiles // 2))

            @block.gpsimd
            def _(pool):
                nc.gpsimd.memset(xrT[HC:HC + 1, :, :, :], 1.0).then_inc(ones_set, 1)

            @block.tensor
            def _(pe):
                def turn_x(i, par, half):
                    pe.wait_ge(row_in[par], 16 * (half + 1))
                    ge(pe, x_moved, i)
                    for c in range(2):
                        mm = nc.tensor.transpose(xt_ps[0:HC, c * P:(c + 1) * P], xr[:, par, c * HC:(c + 1) * HC],
                                                 k["ident"][:])
                    mm.then_inc(x_turned, 1)

                def turn_a(i, par):
                    pe.wait_ge(act_ready, i + 1)
                    ge(pe, a_moved, i)
                    for c in range(AC):
                        mm = nc.tensor.transpose(at_ps[:, c * P:(c + 1) * P], act_sb[:, par, c * P:(c + 1) * P],
                                                 k["ident"][:])
                    mm.then_inc(a_turned, 1)

                def layer1(i, par, e, o):
                    if o == 0:
                        pe.wait_ge(x_moved, i + 1)
                        ge(pe, act_ready, i - 1)
                    for c in range(2):
                        rows = HC + c
                        mm = nc.tensor.matmul(hid[par][:, o, 0:FH], xrT[0:rows, par, c, :],
                                              w1_flat[0:rows, bass.ds(e * (2 * F) + c * F + o * FH, FH)],
                                              start=c == 0, stop=c == 1)
                    if o == 1:
                        mm.then_inc(hid_ready, 1)

                def layer2(i, par, e):
                    pe.wait_ge(a_moved, i + 1)
                    ge(pe, y_moved, i)
                    for c in range(AC):
                        mm = nc.tensor.matmul(y_ps[:, 0:C], actT[:, par, c, :], w2_flat[:, bass.ds(e * (AC * C) + c * C, C)],
                                              start=c == 0, stop=c == AC - 1)
                    mm.then_inc(y_ready, 1)

                def expert(i):
                    return pe.value_load(tile_expert[0:1, bass.ds(i, 1)], min_val=0, max_val=E - 1)
                pe.wait_ge(ones_set, 1)
                pe.wait_ge(weights_in, 32 * E)
                turn_x(0, 0, 0)
                turn_x(1, 1, 0)
                e = expert(0)
                layer1(0, 0, e, 0)
                layer1(0, 0, e, 1)

                def body(i, par, half):
                    e = expert(i)
                    layer1(i, par, e, 0)
                    turn_a(i - 1, 1 - par)
                    layer1(i, par, e, 1)
                    turn_x(i + 1, 1 - par, half)
                    layer2(i - 1, 1 - par, expert(i - 1))
                body(1, 1, 1)
                body(2, 0, 1)
                with pe.Fori(1, (tiles - 2) // 2) as p:
                    body(2 * p + 1, 1, p + 1)
                    body(2 * p + 2, 0, p + 1)
                last = tiles - 1
                e = expert(last)
                layer1(last, 1, e, 0)
                turn_a(last - 1, 0)
                layer1(last, 1, e, 1)
                layer2(last - 1, 0, expert(last - 1))
                turn_a(last, 1)
                layer2(last, 1, expert(last))

            @block.vector
            def _(dve):
                def move_x(i, par):
                    dve.wait_ge(x_turned, i + 1)
                    ge(dve, hid_ready, i - 1)
                    nc.vector.tensor_copy(xrT[0:HC, par, :, :], xt_ps[0:HC, 0:2 * P].rearrange("p (c t) -> p c t", c=2))\
                        .then_inc(x_moved, 1)

                def move_a(i, par):
                    dve.wait_ge(a_turned, i + 1)
                    ge(dve, y_ready, i - 1)
                    nc.vector.tensor_copy(actT[:, par, :, :], at_ps[:, 0:AC * P].rearrange("p (c t) -> p c t", c=AC))\
                        .then_inc(a_moved, 1)

                def activate(i, par):
                    if not swiglu:
                        return
                    dve.wait_ge(hid_ready, i + 1)
                    ge(dve, act_ready, i - 1)
                    nc.vector.tensor_scalar(glu[:, par, :], hid[par][:, 0, 0:A], LIMIT, None, ALU.min).then_inc(glu_ready, 1)
                    nc.vector.tensor_scalar(lin[:, par, :], hid[par][:, 1, 0:A], LIMIT, -LIMIT, ALU.min, ALU.max)\
                        .then_inc(lin_ready, 1)
                    dve.wait_ge(lin_ready, i + 1)
                    dve.wait_ge(glu_ready, i + 1)
                    nc.vector.scalar_tensor_tensor(out=lin[:, par, :], in0=lin[:, par, :], scalar=1.0, in1=glu[:, par, :],
                                                   op0=ALU.add, op1=ALU.mult).then_inc(mix_ready, 1)
                    dve.wait_ge(mix_ready, i + 1)
                    dve.wait_ge(gate_ready, i + 1)
                    ge(dve, a_turned, i - 1)
                    nc.vector.tensor_tensor(act_sb[:, par, :], lin[:, par, :], gate[:, par, :], ALU.mult).then_inc(act_ready, 1)
                move_x(0, 0)
                move_x(1, 1)
                activate(0, 0)

                def body(i, par):
                    move_a(i - 1, 1 - par)
                    move_x(i + 1, 1 - par)
                    activate(i, par)
                steady(dve, body)
                last = tiles - 1
                move_a(last - 1, 0)
                activate(last, 1)
                move_a(last, 1)

            @block.scalar
            def _(act):
                def activate(i, par):
                    if swiglu:
                        act.wait_ge(glu_ready, i + 1)
                        ge(act, act_ready, i - 1)
                        nc.scalar.activation(gate[:, par, :], glu[:, par, :], ACT.Sigmoid, scale=ALPHA).then_inc(gate_ready, 1)
                    else:
                        act.wait_ge(hid_ready, i + 1)
                        ge(act, a_turned, i - 1)
                        nc.scalar.activation(act_sb[:, par, :].rearrange("p (o f) -> p o f", o=2), hid[par][:, :, 0:FH],
                                             ACT.Gelu).then_inc(act_ready, 1)

                def move_y(i, par, half):
                    act.wait_ge(y_ready, i + 1)
                    if not isinstance(half, int) or half > 0:
                        act.wait_ge(sent[par], 16 * half)
                    nc.scalar.activation(y[:, par, :], y_ps[:, 0:C], ACT.Copy).then_inc(y_moved, 1)
                activate(0, 0)
                activate(1, 1)
                move_y(0, 0, 0)
                activate(2, 0)
                move_y(1, 1, 0)
                with act.Fori(1, (tiles - 2) // 2) as p:
                    activate(2 * p + 1, 1)
                    move_y(2 * p, 0, p)
                    activate(2 * p + 2, 0)
                    move_y(2 * p + 1, 1, p)
                last = tiles - 1
                activate(last, 1)
                move_y(last - 1, 0, (last - 1) // 2)
                move_y(last, 1, last // 2)


def combine(nc, k, sem, tag, d, E, K, slot_get, weight, comb, rows_out, first, second, out):
    R = 8
    with ExitStack() as cx:
        def sb(name, shape, dt=F32):
            return cx.enter_context(nc.sbuf_tensor(tag + name, shape, dt))
        b2 = sb("b2", [E, C])
        combT = sb("combT", [E, NT, P])
        base = sb("base", [P, NT, C])
        acc = sb("acc", [P, 2, C])
        got = sb("got", [P, R, C])
        turned_ps = cx.enter_context(nc.psum_tensor(tag + "turned_ps", [P, 2, 512], F32))
        bias_ps = cx.enter_context(nc.psum_tensor(tag + "bias_ps", [P, 2, 512], F32))
        b2_in, turned, moved, biased, added, chain = (sem(tag + x) for x in (
            "b2_in", "turned", "moved", "biased", "added", "chain"))
        gathered = [sem(f"{tag}gathered{i}") for i in range(R)]
        used = sem(tag + "used")
        with nc.Block() as block:
            @block.sync
            def _(sp):
                sp.dma_start(b2[:], d["b2"]).then_inc(b2_in, 16)

            @block.gpsimd
            def _(pool):
                for t in range(NT):
                    for j in range(K):
                        n = t * K + j
                        if n >= R:
                            pool.wait_ge(used, n - R + 1)
                        pool.indirect_dma_start(out=got[:, n % R, :], out_offset=None, in_=rows_out,
                                                in_offset=bass.IndirectOffsetOnAxis(ap=slot_get[:, j, t:t + 1], axis=0))\
                            .then_inc(gathered[n % R], 16)

            @block.tensor
            def _(pe):
                pe.wait_ge(b2_in, 16)
                for t in range(NT):
                    if t >= 2:
                        pe.wait_ge(moved, t - 1)
                    nc.tensor.transpose(turned_ps[0:E, t % 2, 0:P], comb[:, t, :], k["ident"][:]).then_inc(turned, 1)
                for t in range(NT):
                    pe.wait_ge(moved, t + 1)
                    if t >= 2:
                        pe.wait_ge(added, t - 1)
                    nc.tensor.matmul(bias_ps[:, t % 2, 0:C], combT[:, t, :], b2[:], start=True, stop=True).then_inc(biased, 1)

            @block.scalar
            def _(act):
                for t in range(NT):
                    act.wait_ge(turned, t + 1)
                    nc.scalar.activation(combT[:, t, :], turned_ps[0:E, t % 2, 0:P], ACT.Copy).then_inc(moved, 1)

            @block.vector
            def _(dve):
                n_links = [0]
                link(dve, chain, n_links, nc.vector.tensor_tensor(base[:], first[:], second[:], ALU.add))
                for t in range(NT):
                    dve.wait_ge(biased, t + 1)
                    nc.vector.tensor_tensor(base[:, t, :], bias_ps[:, t % 2, 0:C], base[:, t, :], ALU.add).then_inc(added, 1)
                    dve.wait_ge(added, t + 1)
                    prev = base[:, t, :]
                    for j in range(K):
                        n = t * K + j
                        dst = out[:, t, :] if j == K - 1 else acc[:, j % 2, :]
                        dve.wait_ge(gathered[n % R], 16 * (n // R + 1))
                        nc.vector.scalar_tensor_tensor(out=dst, in0=got[:, n % R, :], scalar=weight[:, j, t:t + 1], in1=prev,
                                                       op0=ALU.mult, op1=ALU.add).then_inc(used, 1)
                        dve.wait_ge(used, n + 1)
                        prev = dst


def mixture_of_experts(nc, k, sem, tag, d, scope, prepare, E, K, F, A, swiglu, capacity, tiles, first, second, out):
    total = tiles * P
    rows_in = nc.dram_tensor(tag + "rows_in", (total, C), F32, kind="Internal").ap()
    rows_out = nc.dram_tensor(tag + "rows_out", (total, C), F32, kind="Internal").ap()
    with scope() as tables:
        slot_put = tables.sb(tag + "slot_put", [P, K, NT], U32)
        slot_get = tables.sb(tag + "slot_get", [P, K, NT], U32)
        weight = tables.sb(tag + "weight", [P, K, NT])
        comb = tables.sb(tag + "comb", [P, NT, E])
        tile_expert = tables.sb(tag + "tile_expert", [P, tiles], I32)
        w1 = tables.sb(tag + "w1", [HC + 1, E, 2, F])
        early = tables.sb(tag + "w2", [P, E, A // P, C]) if E * F <= 8 * 4 * C else None
        weights_in = sem(tag + "weights_in")
        with scope() as tokens:
            x = tokens.sb(tag + "x", [P, NT, C])
            with scope() as turned:
                xT = turned.sb(tag + "xT", [HC, 2, N])
                ahead = [(w1[:, e, :, :], d["w1"][e], weights_in) for e in range(E)]
                if early:
                    ahead += [(early[:, e, :, :], d["w2"][e], weights_in) for e in range(E)]
                prepare(x, xT, ahead)
                route(nc, k, sem, tag + "r_", d, x, xT, E, K, capacity, tiles, slot_put, slot_get, weight, comb,
                      tile_expert, rows_in, 10)
            dispatch(nc, sem, tag + "d_", x, K, slot_put, rows_in, total)
        with scope() as second_layers:
            w2 = early or second_layers.sb(tag + "w2", [P, E, A // P, C])
            experts(nc, k, sem, tag + "e_", d, E, F, A, swiglu, tiles, tile_expert, rows_in, rows_out, w1, w2, weights_in,
                    load_w2=not early)
        combine(nc, k, sem, tag + "c_", d, E, K, slot_get, weight, comb, rows_out, first, second, out)


def finish_program(nc, sem, h, out):
    sent = sem("result_sent")
    with nc.Block() as block:
        @block.sync
        def _(sp):
            sp.dma_start(out.rearrange("(t p) c -> p t c", p=P), h[:]).then_inc(sent, 16)
            sp.wait_ge(sent, 16)


def tower(nc, d, out):
    with ExitStack() as cx:
        def sb(name, shape, dt=F32):
            return cx.enter_context(nc.sbuf_tensor(name, shape, dt))

        held = []

        def sem(name):
            held.append(nc.alloc_semaphore(name=name))
            return held[-1]

        def clear_semaphores():
            nc.clear_and_free_semaphores(list(held))
            held.clear()
            nc.all_engine_barrier()
        k = build_constants(nc, cx, sb, sem)
        h = sb("h", [P, NT, C])
        q_pieces = nc.dram_tensor("q_pieces", (3, C, N), BF16, kind="Internal").ap()
        k_pieces = nc.dram_tensor("k_pieces", (3, C, N), BF16, kind="Internal").ap()

        def scope():
            stack = ExitStack()
            stack.sb = lambda name, shape, dt=F32: stack.enter_context(nc.sbuf_tensor(name, shape, dt))
            return stack

        def mixture_keyed_attention():
            with scope() as attn:
                vals = attn.sb("vals0", [P, NT, VW])
                with scope() as mix:
                    keys = mix.sb("keys", [P, 3, N // 2])
                    tab = mix.sb("tab", [P, 3, 2, C])
                    with scope() as norm:
                        x, xT = norm.sb("x0", [P, NT, C]), norm.sb("xT0", [HC, 2, N])
                        normalise(nc, k, sem, "n0_", h, x, xT)
                        project_qkv(nc, k, sem, "p0_", d["mix"], xT, q_pieces, k_pieces, vals, keys=keys)
                    mixture_tables(nc, sem, d, tab)
                    mixture_keys(nc, k, sem, tab, keys, k_pieces)
                yT = attn.sb("yT0", [P, NC4, N])
                attend(nc, k, sem, "a0_", q_pieces, k_pieces, vals, yT, NH, 1.0,
                       sum_factor=float(np.sqrt(np.float32(C))))
                project_out(nc, k, sem, "o0_", d["mix"], yT, h, h)

        def pre_norm_block():
            with scope() as ffn:
                x2 = ffn.sb("x2", [P, NT, C])
                with scope() as attn:
                    x1 = attn.sb("x1", [P, NT, C])
                    vals = attn.sb("vals1", [P, NT, VW])
                    normalise(nc, k, sem, "n1_", h, x1)
                    with scope() as norm:
                        x, xT = norm.sb("x1n", [P, NT, C]), norm.sb("x1nT", [HC, 2, N])
                        normalise(nc, k, sem, "n2_", x1, x, xT, d["ffn"]["ln1_w"], d["ffn"]["ln1_b"])
                        project_qkv(nc, k, sem, "p1_", d["ffn"], xT, q_pieces, k_pieces, vals)
                    yT = attn.sb("yT1", [P, NC4, N])
                    attend(nc, k, sem, "a1_", q_pieces, k_pieces, vals, yT, NH, 1.0 / float(np.sqrt(HD)), causal=True)
                    project_out(nc, k, sem, "o1_", d["ffn"], yT, x1, x2)
                mixture_of_experts(nc, k, sem, "m0_", d["moe0"], scope,
                                   lambda x, xT, ahead: normalise(nc, k, sem, "n3_", x2, x, xT, d["ffn"]["ln2_w"],
                                                                  d["ffn"]["ln2_b"], ahead=ahead),
                                   E=8, K=2, F=4 * C, A=4 * C, swiglu=False, capacity=CAPACITY, tiles=8 * CAPACITY // P,
                                   first=h, second=x2, out=h)

        def differential_attention():
            with scope() as attn:
                vals = attn.sb("vals2", [P, NT, VW])
                neg_lambda = attn.sb("neg_lambda", [P, 1])
                attention_lambda(nc, sem, d["diff"], neg_lambda, LAMBDA_INIT)
                with scope() as norm:
                    x, xT = norm.sb("x3", [P, NT, C]), norm.sb("x3T", [HC, 2, N])
                    normalise(nc, k, sem, "n4_", h, x, xT)
                    project_qkv(nc, k, sem, "p2_", d["diff"], xT, q_pieces, k_pieces, vals, guard=True)
                yT = attn.sb("yT2", [P, NC4, N])
                attend(nc, k, sem, "a2_", q_pieces, k_pieces, vals, yT, 2 * NH, float(HD // 2) ** -0.5,
                       neg_lambda=neg_lambda)
                head_rms(nc, k, sem, d["diff"], yT, 1.0 - LAMBDA_INIT)
                project_out(nc, k, sem, "o2_", d["diff"], yT, h, h)

        def gated_experts():
            with scope() as moe:
                x = moe.sb("x4", [P, NT, C])
                normalise(nc, k, sem, "n5_", h, x)
                mixture_of_experts(nc, k, sem, "m1_", d["moe1"], scope,
                                   lambda t, tT, ahead: normalise(nc, k, sem, "n6_", x, t, tT, d["moe1"]["scale"],
                                                                  rms=True, ahead=ahead),
                                   E=16, K=4, F=4 * C, A=2 * C, swiglu=True, capacity=None, tiles=4 * NT + 16,
                                   first=h, second=x, out=h)

        embed(nc, k, sem, d, h)
        mixture_keyed_attention()
        clear_semaphores()
        pre_norm_block()
        clear_semaphores()
        differential_attention()
        clear_semaphores()
        gated_experts()
        finish_program(nc, sem, h, out)


def kernel(**inputs):
    import concourse.bacc as _bacc
    from concourse.bass_utils import run_bass_kernel_spmd as _run
    a = {n: np.asarray(v) for n, v in inputs.items()}

    def halves(w):
        return w.reshape(2, HC, -1).transpose(1, 0, 2)

    arrays = {}
    arrays["ids"] = a["x"].reshape(NT, P).T
    arrays["tok_embed"] = a["L0_tok_tok_embed"]
    arrays["tok_W1"] = a["L0_tok_W1"].T.reshape(FRONT // P, P, C).transpose(1, 0, 2)
    arrays["tok_W2"] = halves(a["L0_tok_W2"].T)
    arrays["tok_b1"] = a["L0_tok_b1"].reshape(2, HC).T
    arrays["tok_b2"] = a["L0_tok_b2"]
    w = a["L0_attn_Wqkv"].reshape(C, C, 3)
    bias = a["L0_attn_bqkv"].reshape(C, 3)
    for i, n in enumerate("qkv"):
        arrays[f"mix.W{n}"] = halves(w[:, :, i])
    arrays["mix.bq"] = bias[:, 0].reshape(2, HC).T
    arrays["mix.bk"] = bias[:, 1].reshape(2, HC).T
    arrays["mix.bk_packed"] = np.stack([bias[0:P, 1], np.concatenate([bias[P:C, 1], bias[P:C, 1]])], axis=1)
    arrays["mix.bv"] = bias[:, 2]
    arrays["mix.Wo"] = a["L0_attn_Wproj"]
    arrays["mix.bo"] = a["L0_attn_bproj"]
    arrays["mix_mean"] = a["L0_attn_mean"]
    arrays["mix_logvar"] = a["L0_attn_logvar"]
    arrays["mix_coef"] = a["L0_attn_mix_coef"]
    for g, p in (("ffn", "L0_ffn_"), ("diff", "L1_attn_")):
        for i, n in enumerate("qkv"):
            if g == "ffn":
                wn, bn = a[p + "attn_qkv_w"][:, i * C:(i + 1) * C], a[p + "attn_qkv_b"][i * C:(i + 1) * C]
            else:
                wn, bn = a[p + "W" + n], a[p + "b" + n]
            arrays[f"{g}.W{n}"] = halves(wn)
            arrays[f"{g}.b{n}"] = bn if n == "v" else bn.reshape(2, HC).T
    arrays["ffn.Wo"], arrays["ffn.bo"] = a["L0_ffn_attn_proj_w"], a["L0_ffn_attn_proj_b"]
    arrays["diff.Wo"], arrays["diff.bo"] = a["L1_attn_Wo"], a["L1_attn_bo"]
    for n in ("ln1_w", "ln1_b", "ln2_w", "ln2_b"):
        arrays["ffn." + n] = a["L0_ffn_" + n]
    arrays["diff.lambdas"] = np.stack([a["L1_attn_lambda_" + n] for n in ("q1", "q2", "k1", "k2")])
    arrays["diff.subln"] = a["L1_attn_subln_w"].reshape(HD, 1)

    def first_layer(w, bias):
        e, _, f = w.shape
        w = w.reshape(e, 2, HC, f)
        rows = np.stack([np.zeros_like(bias), bias], axis=1)
        return np.concatenate([w, rows[:, :, None, :]], axis=2).transpose(0, 2, 1, 3)

    def second_layer(w):
        e, f, _ = w.shape
        return w.reshape(e, f // P, P, C).transpose(0, 2, 1, 3)
    arrays["moe0.wg"] = halves(a["L0_ffn_w_g"])
    arrays["moe0.w1"] = first_layer(a["L0_ffn_exp_fc_w"], a["L0_ffn_exp_fc_b"][:, 0, :])
    arrays["moe0.w2"] = second_layer(a["L0_ffn_exp_proj_w"])
    arrays["moe0.b2"] = a["L0_ffn_exp_proj_b"][:, 0, :]
    arrays["moe1.scale"] = a["L1_ffn_norm_scale"]
    arrays["moe1.wg"] = halves(a["L1_ffn_gate_w"].T)
    arrays["moe1.bg"] = a["L1_ffn_gate_b"]
    m1, mb1 = a["L1_ffn_mlp1_w"].transpose(0, 2, 1), a["L1_ffn_mlp1_b"]
    arrays["moe1.w1"] = first_layer(np.concatenate([m1[:, :, 0::2], m1[:, :, 1::2]], axis=2),
                                    np.concatenate([mb1[:, 0::2], mb1[:, 1::2]], axis=1))
    arrays["moe1.w2"] = second_layer(a["L1_ffn_mlp2_w"].transpose(0, 2, 1))
    arrays["moe1.b2"] = a["L1_ffn_mlp2_b"]
    arrays = {n: np.ascontiguousarray(v) for n, v in arrays.items()}

    nc = _bacc.Bacc("TRN2", target_bir_lowering=False, num_devices=1)
    d, feeds = {}, {}
    for n, v in arrays.items():
        name = "in_" + n.replace(".", "_")
        ap = nc.dram_tensor(name, v.shape, mybir.dt.from_np(v.dtype), kind="ExternalInput").ap()
        feeds[name] = v
        if "." in n:
            group, member = n.split(".")
            d.setdefault(group, {})[member] = ap
        else:
            d[n] = ap
    out = nc.dram_tensor("out_0", (N, C), F32, kind="ExternalOutput").ap()
    tower(nc, d, out)
    r = _run(nc, [feeds], core_ids=[0])
    return r.results[0]["out_0"].reshape(B, S, C)
```
